# Optimizing a Trainium2 kernel written in Bass

```python
import numpy as np
import jax
import jax.numpy as jnp

def _softmax(x, axis=-1):
    return jax.nn.softmax(x, axis=axis)

def _gelu(x):
    return jax.nn.gelu(x, approximate=True)

def _silu(x):
    return jax.nn.silu(x)

def _sigmoid(x):
    return jax.nn.sigmoid(x)

def _layernorm(x, axis=-1, eps=1e-05):
    m = jnp.mean(x, axis=axis, keepdims=True)
    v = jnp.var(x, axis=axis, keepdims=True)
    return (x - m) / jnp.sqrt(v + eps)

def _scatter_add(tgt, idx, src, axis=0):
    return tgt.at[idx].add(src)

def _segment_sum(src, seg, n):
    return jax.ops.segment_sum(src, seg, n)
kernel_name = 'mk_gnn_resnorm_d2_gnn_r8_77a32c'

def setup_inputs(seed: int=0):
    np.random.seed(seed)
    _w = jnp.asarray

    def _rec_inputs():
        import jax
        import jax.numpy as jnp
        _gk = jax.random.key(seed)
        x = -0.000202 + 1 * jax.random.normal(jax.random.fold_in(_gk, 1), (6250, 128), jnp.float32)
        src = jax.random.randint(jax.random.fold_in(_gk, 2), (200000,), 0, 6250, jnp.int32)
        dst = jax.random.randint(jax.random.fold_in(_gk, 3), (200000,), 0, 6250, jnp.int32)
        _o = jnp.argsort(dst, stable=True)
        src = src[_o]
        dst = dst[_o]
        edge_attr_128 = -4.21973e-05 + 0.999841 * jax.random.normal(jax.random.fold_in(_gk, 11), (200000, 128), jnp.float32)
        return (x, src, dst, edge_attr_128)
    x, src, dst, edge_attr_128 = _rec_inputs()

    def _L0_gnn_setup():
        import jax, jax.numpy as jnp
        import numpy as np
        HIDDEN = 128
        N_NODES = 6250
        N_EDGES = 75000
        EPS = 1e-05

        def _linear_params(key, fan_in, fan_out):
            kw, kb = jax.random.split(key)
            bound = 1.0 / np.sqrt(fan_in)
            W = jax.random.uniform(kw, (fan_in, fan_out), jnp.float32, -bound, bound)
            b = jax.random.uniform(kb, (fan_out,), jnp.float32, -bound, bound)
            return (W, b)

        def _mlp2(x, W1, b1, W2, b2):
            h = jax.nn.silu(x @ W1 + b1)
            return h @ W2 + b2

        def _layernorm(x, gamma, beta):
            mu = jnp.mean(x, axis=-1, keepdims=True)
            var = jnp.mean(jnp.square(x - mu), axis=-1, keepdims=True)
            return (x - mu) * jax.lax.rsqrt(var + EPS) * gamma + beta
        key = jax.random.key(seed)
        ks = jax.random.split(key, 8)
        h_node = jax.random.normal(ks[0], (N_NODES, HIDDEN), jnp.float32)
        h_edge = jax.random.normal(ks[1], (N_EDGES, HIDDEN), jnp.float32)
        edge_index = jax.random.randint(ks[2], (2, N_EDGES), 0, N_NODES, jnp.int64 if jax.config.jax_enable_x64 else jnp.int32)
        msg_W1, msg_b1 = _linear_params(ks[3], 3 * HIDDEN, HIDDEN)
        msg_W2, msg_b2 = _linear_params(ks[4], HIDDEN, HIDDEN)
        upd_W1, upd_b1 = _linear_params(ks[5], 2 * HIDDEN, HIDDEN)
        upd_W2, upd_b2 = _linear_params(ks[6], HIDDEN, HIDDEN)
        ln_gamma = jnp.ones((HIDDEN,), jnp.float32)
        ln_beta = jnp.zeros((HIDDEN,), jnp.float32)
        return {'h_node': h_node, 'h_edge': h_edge, 'edge_index': edge_index, 'msg_W1': msg_W1, 'msg_b1': msg_b1, 'msg_W2': msg_W2, 'msg_b2': msg_b2, 'upd_W1': upd_W1, 'upd_b1': upd_b1, 'upd_W2': upd_W2, 'upd_b2': upd_b2, 'ln_gamma': ln_gamma, 'ln_beta': ln_beta}
    _L0_gnn_all = _L0_gnn_setup()
    _L0_gnn_in = {k: v for k, v in _L0_gnn_all.items() if k in ('msg_W1', 'msg_b1', 'msg_W2', 'msg_b2', 'upd_W1', 'upd_b1', 'upd_W2', 'upd_b2', 'ln_gamma', 'ln_beta')}
    del _L0_gnn_all

    def _L1_gnn_setup():
        import jax, jax.numpy as jnp
        import numpy as np
        N_NODES = 6250
        N_EDGES = 100000
        D = 128
        key = jax.random.key(seed)
        k1, k2, k3, k4 = jax.random.split(key, 4)
        node_feat = jax.random.normal(k1, (N_NODES, D), dtype=jnp.float32)
        edge_index = jax.random.randint(k2, (2, N_EDGES), 0, N_NODES, dtype=jnp.int32)
        W1 = jax.random.normal(k3, (2 * D, D), dtype=jnp.float32) * (1.0 / np.sqrt(2 * D))
        b1 = jnp.zeros((D,), dtype=jnp.float32)
        W2 = jax.random.normal(k4, (D, D), dtype=jnp.float32) * (1.0 / np.sqrt(D))
        b2 = jnp.zeros((D,), dtype=jnp.float32)
        return {'node_feat': node_feat, 'edge_index': edge_index, 'W1': W1, 'b1': b1, 'W2': W2, 'b2': b2}
    _L1_gnn_all = _L1_gnn_setup()
    _L1_gnn_in = {k: v for k, v in _L1_gnn_all.items() if k in ('W1', 'b1', 'W2', 'b2')}
    del _L1_gnn_all
    return {'x': x, 'src': src, 'dst': dst, 'edge_attr_128': edge_attr_128, 'L0_gnn_msg_W1': _L0_gnn_in['msg_W1'], 'L0_gnn_msg_b1': _L0_gnn_in['msg_b1'], 'L0_gnn_msg_W2': _L0_gnn_in['msg_W2'], 'L0_gnn_msg_b2': _L0_gnn_in['msg_b2'], 'L0_gnn_upd_W1': _L0_gnn_in['upd_W1'], 'L0_gnn_upd_b1': _L0_gnn_in['upd_b1'], 'L0_gnn_upd_W2': _L0_gnn_in['upd_W2'], 'L0_gnn_upd_b2': _L0_gnn_in['upd_b2'], 'L0_gnn_ln_gamma': _L0_gnn_in['ln_gamma'], 'L0_gnn_ln_beta': _L0_gnn_in['ln_beta'], 'L1_gnn_W1': _L1_gnn_in['W1'], 'L1_gnn_b1': _L1_gnn_in['b1'], 'L1_gnn_W2': _L1_gnn_in['W2'], 'L1_gnn_b2': _L1_gnn_in['b2']}

def reference(x, src, dst, edge_attr_128, L0_gnn_msg_W1, L0_gnn_msg_b1, L0_gnn_msg_W2, L0_gnn_msg_b2, L0_gnn_upd_W1, L0_gnn_upd_b1, L0_gnn_upd_W2, L0_gnn_upd_b2, L0_gnn_ln_gamma, L0_gnn_ln_beta, L1_gnn_W1, L1_gnn_b1, L1_gnn_W2, L1_gnn_b2):
    import jax
    import jax.numpy as jnp

    def _L0_gnn_ref(h_node, h_edge, edge_index, msg_W1, msg_b1, msg_W2, msg_b2, upd_W1, upd_b1, upd_W2, upd_b2, ln_gamma, ln_beta):
        import jax, jax.numpy as jnp
        import numpy as np
        HIDDEN = 128
        N_NODES = 6250
        N_EDGES = 75000
        EPS = 1e-05

        def _linear_params(key, fan_in, fan_out):
            kw, kb = jax.random.split(key)
            bound = 1.0 / np.sqrt(fan_in)
            W = jax.random.uniform(kw, (fan_in, fan_out), jnp.float32, -bound, bound)
            b = jax.random.uniform(kb, (fan_out,), jnp.float32, -bound, bound)
            return (W, b)

        def _mlp2(x, W1, b1, W2, b2):
            h = jax.nn.silu(x @ W1 + b1)
            return h @ W2 + b2

        def _layernorm(x, gamma, beta):
            mu = jnp.mean(x, axis=-1, keepdims=True)
            var = jnp.mean(jnp.square(x - mu), axis=-1, keepdims=True)
            return (x - mu) * jax.lax.rsqrt(var + EPS) * gamma + beta
        src, dst = (edge_index[0], edge_index[1])
        m_in = jnp.concatenate([h_node[src], h_node[dst], h_edge], axis=-1)
        m = _mlp2(m_in, msg_W1, msg_b1, msg_W2, msg_b2)
        agg = jax.ops.segment_sum(m, dst, num_segments=h_node.shape[0])
        h_new = _mlp2(jnp.concatenate([h_node, agg], axis=-1), upd_W1, upd_b1, upd_W2, upd_b2)
        return _layernorm(h_node + h_new, ln_gamma, ln_beta)

    def _L1_gnn_ref(node_feat, edge_index, W1, b1, W2, b2):
        import jax, jax.numpy as jnp
        import numpy as np
        N_NODES = 6250
        N_EDGES = 100000
        D = 128
        src, dst = (edge_index[0], edge_index[1])
        n = node_feat.shape[0]
        msgs = node_feat[src]
        agg = jax.ops.segment_sum(msgs, dst, num_segments=n)
        deg = jax.ops.segment_sum(jnp.ones_like(dst, dtype=node_feat.dtype), dst, num_segments=n)
        agg = agg / jnp.maximum(deg, 1.0)[:, None]
        h = jnp.concatenate([node_feat, agg], axis=-1)
        h = jax.nn.relu(h @ W1 + b1)
        h = jax.nn.relu(h @ W2 + b2)
        return h
    edge_index = jnp.stack([src, dst])
    x = _layernorm(x + _L0_gnn_ref(x, edge_attr_128, edge_index, L0_gnn_msg_W1, L0_gnn_msg_b1, L0_gnn_msg_W2, L0_gnn_msg_b2, L0_gnn_upd_W1, L0_gnn_upd_b1, L0_gnn_upd_W2, L0_gnn_upd_b2, L0_gnn_ln_gamma, L0_gnn_ln_beta), axis=-1)
    x = _layernorm(x + _L1_gnn_ref(x, edge_index, L1_gnn_W1, L1_gnn_b1, L1_gnn_W2, L1_gnn_b2), axis=-1)
    return x

_drawn_inputs = setup_inputs


def setup_inputs(seed=0):
    import zlib

    import numpy as np

    out = dict(_drawn_inputs(seed))
    spreads = {'L0_gnn_ln_gamma': (1.0, 0.2),
     'L0_gnn_ln_beta': (0.0, 0.1),
     'L1_gnn_b1': (0.0, 0.1),
     'L1_gnn_b2': (0.0, 0.1)}
    factors = {'L0_gnn_upd_b1': 8.0}
    for name, (base, spread) in spreads.items():
        noise = np.random.default_rng([zlib.crc32(name.encode()), seed]).standard_normal(out[name].shape)
        drawn = base * np.exp(spread * noise) if base else spread * noise
        out[name] = jnp.asarray(drawn.astype(out[name].dtype))
    for name, factor in factors.items():
        out[name] = (out[name] * factor).astype(out[name].dtype)
    return out
```

```python
import numpy as np
import concourse.bass as bass
from concourse import mybir
from contextlib import ExitStack

F32, BF16, F16, I32 = mybir.dt.float32, mybir.dt.bfloat16, mybir.dt.float16, mybir.dt.int32
ALU = mybir.AluOpType
ACT = mybir.ActivationFunctionType
AX = mybir.AxisListType

N_NODES, N_EDGES, D = 6250, 200000, 128
P = 128
QT, GQ = 4, 7
GT = QT * GQ
GE = GT * P
GROUPS = -(-N_EDGES // GE)
TILES = GROUPS * GT
QUADS = GROUPS * GQ
EP = TILES * P
NB = -(-N_NODES // P)
NP_ = NB * P
NW = NP_ + P
SPREAD = -(-(EP - N_EDGES) // (NP_ - N_NODES))
W0 = 20
WIN = [(0, W0), (2, 10), (5, 12), (8, 12)]
AB = 25
A2 = 2 * AB
ROFF = [A2 * sum(w for _, w in WIN[:j]) for j in range(QT)]
RCOLS = ROFF[-1] + A2 * WIN[-1][1]
LASTQ = P - W0
CLEARED = 96
CH = 7
CHUNKS = NB // CH
CN = CH * P
HN = CN // 2
SW = D + 1
SWP = 132
EPS = 1e-5
SKIP = 8192


def bass_gnn_two_layers(nc, x_nm, xT, eT, src_pt, dst_pt, dst_next_pt, src_row, dst_row, dst_first,
                        mW1, mb1, mW2, mb2, uW1, ub1, uW2, ub2, gamma, beta, W1, b1, W2, b2, out,
                        force_general=False):
    def dram(name, shape, dt):
        return nc.dram_tensor(name, shape, dt).ap()

    P_d = dram("P_d", (NP_, D), F32)
    Q_d = dram("Q_d", (NW, 3 * D), BF16)
    rel_d = dram("rel_d", (EP,), BF16)
    A_d = dram("A_d", (GROUPS, P, NB * P), BF16)
    acc_d = dram("acc_d", (NW, SWP), F32)
    x1_d = dram("x1_d", (NP_, D), F32)

    with ExitStack() as top:
        def sem(name, ctx=top):
            return ctx.enter_context(nc.semaphore(name))

        def sb(name, shape, dt=F32, ctx=top):
            return ctx.enter_context(nc.sbuf_tensor(name, shape, dt))

        sumT = sb("sumT", [P, NW])
        deg = sb("deg", [1, NW])
        flag = sb("flag", [1, 1], I32)
        offs = sb("offs", [1, QUADS], I32)
        gbase = sb("gbase", [1, GROUPS], I32)
        ident = sb("ident", [P, P])
        identb = sb("identb", [P, P], BF16)
        pid = sb("pid", [P, 1])
        iota = sb("iota", [P, 1000], F16)
        ones_row = sb("ones_row", [1, P])
        wc = sb("wc", [P, D])
        eps_col = sb("eps_col", [P, 1])

        with ExitStack() as ctx:
            build_prepare(nc, ctx, lambda n: sem(n, ctx), lambda n, s, d=F32: sb(n, s, d, ctx), locals())
        with ExitStack() as ctx:
            build_edges(nc, ctx, lambda n: sem(n, ctx), lambda n, s, d=F32: sb(n, s, d, ctx), locals(), force_general)
        with ExitStack() as ctx:
            build_nodes(nc, ctx, lambda n: sem(n, ctx), lambda n, s, d=F32: sb(n, s, d, ctx), locals())


def build_prepare(nc, ctx, sem, sb, v):
    P_d, Q_d, rel_d = v["P_d"], v["Q_d"], v["rel_d"]
    pid, ident, identb, iota, ones_row = v["pid"], v["ident"], v["identb"], v["iota"], v["ones_row"]
    flag, offs, gbase = v["flag"], v["offs"], v["gbase"]
    wab = sb("wab", [P, 2, D])
    xT_sb = sb("xT_sb", [P, NP_])
    b1bc = sb("b1bc", [P, D])
    D_i, N_i, F_i = sb("D_i", [P, TILES], I32), sb("N_i", [P, TILES], I32), sb("F_i", [P, TILES + 1], I32)
    rel = sb("rel", [P, TILES])
    bad = sb("bad", [P, TILES])
    bad1 = sb("bad1", [P, 1])
    ones_col = sb("ones_col", [P, 1])
    RP = 2 * GROUPS
    RC = EP // RP
    R_i, RB_i, relR = sb("R_i", [RP, RC], I32), sb("RB_i", [RP, 1], I32), sb("relR", [RP, RC], BF16)
    orow = sb("orow", [1, QUADS])
    Pst = [sb(f"Pst{i}", [P, CH, D]) for i in range(2)]
    qf = sb("qf", [P, CH, D])
    qr = sb("qr", [P, CH, D])
    Qst = [sb(f"Qst{i}", [P, CH, 3, D], BF16) for i in range(2)]
    zeros = sb("zeros", [P, 3 * D], BF16)
    pq = [ctx.enter_context(nc.psum_tensor(f"pq{i}", [P, 8, 2 * D], F32)) for i in range(2)]

    w_in, x_in, e_in, r_in = sem("w_in"), sem("x_in"), sem("e_in"), sem("r_in")
    made, dv, pq_ready, p_out, q1_out, q2_out, r_out, q3_out, qf_out = (
        sem(n) for n in ("made", "dv", "pq_ready", "p_out", "q1_out", "q2_out", "r_out", "q3_out", "qf_out"))
    rel_ready, bad_ready, bad_sum, st_z, st_r = (
        sem(n) for n in ("rel_ready", "bad_ready", "bad_sum", "st_z", "st_r"))
    st_p, st_q = ([sem(f"{n}{i}") for i in range(2)] for n in ("st_p", "st_q"))

    with nc.Block() as block:
        @block.sync
        def _(sp):
            sp.dma_start(wab[:], v["mW1"][0:2 * D, :].rearrange("(c k) n -> k c n", c=2)).then_inc(w_in, 16)
            sp.dma_start(xT_sb[:], v["xT"]).then_inc(x_in, 16)
            sp.dma_start(b1bc[:], v["mb1"].partition_broadcast(P)).then_inc(w_in, 16)
            sp.dma_start(v["wc"][:], v["mW1"][2 * D:3 * D, :]).then_inc(w_in, 16)
            sp.dma_start(D_i[:], v["dst_pt"]).then_inc(e_in, 16)
            sp.dma_start(N_i[:], v["dst_next_pt"]).then_inc(e_in, 16)
            sp.dma_start(F_i[:], v["dst_first"].partition_broadcast(P)).then_inc(e_in, 16)
            half = v["dst_row"].rearrange("(g h c) -> h g c", h=2, c=RC)
            with nc.allow_non_contiguous_dma(reason="one word for each half of a group"):
                fg = v["dst_first"][0:TILES].rearrange("(g t) -> g t", t=GT)[:, 0:1]
                for h in range(2):
                    sp.dma_start(RB_i[h * GROUPS:(h + 1) * GROUPS, :], fg).then_inc(r_in, 16)
                    sp.dma_start(R_i[h * GROUPS:(h + 1) * GROUPS, :], half[h]).then_inc(r_in, 16)
            for c in range(CHUNKS):
                rows = slice(c * CN, (c + 1) * CN)
                sp.wait_ge(p_out, c + 1)
                sp.dma_start(P_d[rows, :].rearrange("(j p) n -> p j n", p=P), Pst[c % 2][:]).then_inc(st_p[c % 2], 16)
                sp.wait_ge(q3_out, c + 1)
                sp.dma_start(Q_d[rows, :].rearrange("(j p) n -> p j n", p=P),
                             Qst[c % 2][:].rearrange("p j t n -> p j (t n)")).then_inc(st_q[c % 2], 16)
            sp.wait_ge(made, 5)
            sp.dma_start(Q_d[NP_:NW, :], zeros[:]).then_inc(st_z, 16)
            sp.wait_ge(rel_ready, 1)
            sp.dma_start(rel_d.rearrange("(g h c) -> h g c", h=2, c=RC)[0], relR[0:GROUPS, :]).then_inc(st_r, 16)
            sp.dma_start(rel_d.rearrange("(g h c) -> h g c", h=2, c=RC)[1], relR[GROUPS:RP, :]).then_inc(st_r, 16)
            for i in range(2):
                sp.wait_ge(st_p[i], 16 * ((CHUNKS + 1 - i) // 2))
                sp.wait_ge(st_q[i], 16 * ((CHUNKS + 1 - i) // 2))
            sp.wait_ge(st_z, 16)
            sp.wait_ge(st_r, 32)

        @block.gpsimd
        def _(pool):
            pool.iota(pid[:], [[0, 1]], base=0, channel_multiplier=1, allow_small_or_imprecise_dtypes=True).then_inc(made, 1)
            pool.iota(iota[:], [[1, 1000]], base=0, channel_multiplier=0, allow_small_or_imprecise_dtypes=True).then_inc(made, 1)
            pool.memset(ident[:], 0.0).then_inc(made, 1)
            pool.memset(identb[:], 0.0).then_inc(made, 1)
            pool.memset(zeros[:], 0.0).then_inc(made, 1)
            pool.memset(ones_row[:], 1.0)
            pool.memset(v["eps_col"][:], EPS)
            pool.memset(ones_col[:], 1.0)
            pool.memset(v["sumT"][:], 0.0)
            pool.memset(v["deg"][:], 0.0).then_inc(made, 1)
            pool.wait_ge(made, 6)
            for m in (ident, identb):
                pool.affine_select(out=m[:], in_=m[:], compare_op=ALU.not_equal, fill=1.0, base=0,
                                   pattern=[[-1, P]], channel_multiplier=1).then_inc(made, 1)

        @block.tensor
        def _(pe):
            pe.wait_ge(w_in, 48)
            pe.wait_ge(x_in, 16)
            for c in range(CHUNKS):
                if c >= 2:
                    pe.wait_ge(p_out, c - 1)
                    pe.wait_ge(qf_out, c - 1)
                for j in range(CH):
                    n0 = (c * CH + j) * P
                    last = nc.tensor.matmul(pq[c % 2][:, j, :], xT_sb[:, n0:n0 + P],
                                            wab[:].rearrange("k c n -> k (c n)"), start=True, stop=True)
                last.then_inc(pq_ready, 1)
            pe.wait_ge(bad_ready, 1)
            pe.wait_ge(made, 8)
            nc.tensor.matmul(pq[0][0:1, 0, 0:1], bad1[:], ones_col[:], start=True, stop=True).then_inc(bad_sum, 1)

        @block.scalar
        def _(act):
            for c in range(CHUNKS):
                act.wait_ge(qf_out, c + 1)
                if c >= 2:
                    act.wait_ge(st_p[c % 2], 16 * (c // 2))
                nc.scalar.activation(Pst[c % 2][:], pq[c % 2][:, 0:CH, 0:D], ACT.Copy).then_inc(p_out, 1)
                if c >= 2:
                    act.wait_ge(st_q[c % 2], 16 * (c // 2))
                nc.scalar.activation(Qst[c % 2][:, :, 0, :], qf[:], ACT.Copy).then_inc(q1_out, 1)
                act.wait_ge(r_out, c + 1)
                nc.scalar.activation(Qst[c % 2][:, :, 1, :], qr[:], ACT.Copy).then_inc(q2_out, 1)

        @block.vector
        def _(dve):
            n = [0]

            def link(ins):
                n[0] += 1
                ins.then_inc(dv, 1)
                dve.wait_ge(dv, n[0])

            V = nc.vector
            dve.wait_ge(w_in, 48)
            for c in range(CHUNKS):
                dve.wait_ge(pq_ready, c + 1)
                bb = b1bc[:].unsqueeze(1).broadcast_to([P, CH, D])
                V.tensor_tensor(qf[:], pq[c % 2][:, 0:CH, D:2 * D], bb, ALU.add).then_inc(qf_out, 1)
                dve.wait_ge(q1_out, c + 1)
                V.tensor_tensor(qr[:], qf[:], Qst[c % 2][:, :, 0, :], ALU.subtract).then_inc(r_out, 1)
                dve.wait_ge(q2_out, c + 1)
                V.tensor_tensor(Qst[c % 2][:, :, 2, :], qr[:], Qst[c % 2][:, :, 1, :], ALU.subtract).then_inc(q3_out, 1)
                dve.wait_ge(q3_out, c + 1)
            dve.wait_ge(r_in, 64)
            V.tensor_scalar(relR[:], R_i[:], RB_i[:, 0:1], None, ALU.subtract).then_inc(rel_ready, 1)
            dve.wait_ge(e_in, 48)
            F = F_i[:, 0:TILES]
            Fg = F.rearrange("p (g t) -> p g t", t=GT)[:, :, 0:1]
            Fq = F.rearrange("p (q t) -> p q t", t=QT)[:, :, 0:1]
            link(V.tensor_tensor(bad[:], D_i[:], N_i[:], ALU.is_gt))
            link(V.tensor_tensor(rel[:].rearrange("p (g t) -> p g t", t=GT), D_i[:].rearrange("p (g t) -> p g t", t=GT),
                                 Fg.broadcast_to([P, GROUPS, GT]), ALU.subtract))
            link(V.scalar_tensor_tensor(bad[:], rel[:], float(P - 1), bad[:], ALU.is_gt, ALU.add))
            link(V.tensor_tensor(rel[:].rearrange("p (q t) -> p q t", t=QT), D_i[:].rearrange("p (q t) -> p q t", t=QT),
                                 Fq.broadcast_to([P, QUADS, QT]), ALU.subtract))
            relq, badq = (t[:].rearrange("p (q t) -> p q t", t=QT) for t in (rel, bad))
            for j, (w0, w) in enumerate(WIN):
                link(V.scalar_tensor_tensor(badq[:, :, j], relq[:, :, j], float(w0 + w - 1), badq[:, :, j], ALU.is_gt, ALU.add))
                link(V.scalar_tensor_tensor(badq[:, :, j], relq[:, :, j], float(w0), badq[:, :, j], ALU.is_lt, ALU.add))
            link(V.tensor_tensor(rel[:], F_i[:, 1:TILES + 1], F, ALU.is_le))
            link(V.tensor_tensor(bad[:], bad[:], rel[:], ALU.add))
            F1 = F_i[0:1, 0:TILES].rearrange("p (g q t) -> p g q t", q=GQ, t=QT)[:, :, :, 0]
            o3 = orow[:].rearrange("p (g q) -> p g q", q=GQ)
            link(V.tensor_tensor(o3, F1, F1[:, :, 0:1].broadcast_to([1, GROUPS, GQ]), ALU.subtract))
            b1v = bad[0:1, 0:QUADS].rearrange("p (g q) -> p g q", q=GQ)
            step = rel[0:1, 0:QUADS].rearrange("p (g q) -> p g q", q=GQ)
            link(V.tensor_tensor(step[:, :, 1:GQ], o3[:, :, 1:GQ], o3[:, :, 0:GQ - 1], ALU.subtract))
            link(V.scalar_tensor_tensor(b1v[:, :, 1:GQ], step[:, :, 1:GQ], float(W0 - 1), b1v[:, :, 1:GQ], ALU.is_gt, ALU.add))
            lo, lb = o3[:, :, GQ - 1:GQ], b1v[:, :, GQ - 1:GQ]
            link(V.scalar_tensor_tensor(lb, lo, float(LASTQ), lb, ALU.is_gt, ALU.add))
            link(V.scalar_tensor_tensor(lb, lo, float(CLEARED - W0), lb, ALU.is_lt, ALU.add))
            link(V.tensor_scalar(offs[:], orow[:], 0.0, float(LASTQ), ALU.max, ALU.min))
            Fg1 = F_i[0:1, 0:TILES].rearrange("p (g t) -> p g t", t=GT)[:, :, 0]
            link(V.tensor_scalar(gbase[:], Fg1, 0.0, float(NP_ - 1), ALU.max, ALU.min))
            V.reduce_sum(bad1[:], bad[:], AX.X).then_inc(bad_ready, 1)
            dve.wait_ge(bad_sum, 1)
            V.tensor_scalar(flag[:], pq[0][0:1, 0, 0:1], 1.0, None, ALU.min)




def build_edges(nc, ctx, sem, sb, v, force_general):
    flag, offs, gbase = v["flag"], v["offs"], v["gbase"]
    pid, ident, identb, iota, wc = v["pid"], v["ident"], v["identb"], v["iota"], v["wc"]
    sumT, deg = v["sumT"], v["deg"]

    eT = [sb(f"eT{k}", [P, GE]) for k in range(2)]
    src_i = [sb(f"src_i{k}", [P, GT], I32) for k in range(2)]
    dst_i = [sb(f"dst_i{k}", [P, GT], I32) for k in range(2)]
    first_i = [sb(f"first_i{k}", [P, GT], I32) for k in range(2)]
    rel_b = sb("rel_b", [P, GE], BF16)
    nodeE = [sb(f"nodeE{k}", [P, GE], BF16) for k in range(2)]
    Qw = [sb(f"Qw{k}", [P, 3 * D], BF16) for k in range(2)]
    gath = sb("gath", [P, GQ, QT * D])
    rel_g = [sb(f"rel_g{k}", [P, GT]) for k in range(2)]
    rel_q = sb("rel_q", [P, GT])
    blk_i, low_i = sb("blk_i", [P, GT], I32), sb("low_i", [P, GT], I32)
    key = [sb(f"key{k}", [P, GT]) for k in range(2)]
    low = [sb(f"low{k}", [P, GT]) for k in range(2)]
    edgeN = [sb(f"edgeN{k}", [P, QT, P]) for k in range(2)]
    edgeL = [sb(f"edgeL{k}", [P, QT, P], BF16) for k in range(2)]
    edgeK = [sb(f"edgeK{k}", [P, RCOLS], BF16) for k in range(2)]
    pre = [sb(f"pre{k}", [P, QT * D]) for k in range(2)]
    h = [sb(f"h{k}", [P, QT, D + 2]) for k in range(2)]
    counts = [sb(f"counts{k}", [P, A2, P], BF16) for k in range(2)]
    sumS = sb("sumS", [P, SWP])

    ps_pre = [ctx.enter_context(nc.psum_tensor(f"ps_pre{k}", [P, QT * D], F32)) for k in range(2)]
    ps_cnt = [ctx.enter_context(nc.psum_tensor(f"ps_cnt{k}", [P, 2, 512], F32)) for k in range(2)]
    ps_sum = [ctx.enter_context(nc.psum_tensor(f"ps_sum{k}", [P, 512], F32)) for k in range(2)]
    TR = 2 * P

    e_in = [sem(f"e_in{k}") for k in range(2)]
    i_in = [sem(f"i_in{k}") for k in range(2)]
    r_in = sem("r_in")
    q_in = [sem(f"q_in{k}") for k in range(2)]
    g_in = [sem(f"g_in{q}") for q in range(GQ)]
    c_out = [sem(f"c_out{k}") for k in range(2)]
    prepared = sem("prepared")
    onehots = sem("onehots")
    pre_mm, cnt_mm, sum_mm = sem("pre_mm"), sem("cnt_mm"), sem("sum_mm")
    pre_add, silu, cnt_copy = sem("pre_add"), sem("silu"), sem("cnt_copy")
    sum_copy, sum_tr, sum_add = sem("sum_copy"), sem("sum_tr"), sem("sum_add")
    dv = sem("dv")
    h_ones = sem("h_ones")
    gen = general_path(nc, ctx, sem, sb, v, 0, eT[0], ps_pre[0], ps_sum[0])

    def loop(eng, first, group, last):
        first()
        with eng.Fori(0, (GROUPS - 2) // 2) as i:
            group(i, 1)
            group(i + 1, 0)
        last()

    with nc.Block() as block:
        @block.sync
        def _(sp):
            def load(g, k):
                sp.dma_start(src_i[k][:], v["src_pt"][:, bass.ds(g * GT, GT)]).then_inc(i_in[k], 16)
                sp.dma_start(dst_i[k][:], v["dst_pt"][:, bass.ds(g * GT, GT)]).then_inc(i_in[k], 16)
                sp.dma_start(first_i[k][:], v["dst_first"][bass.ds(g * GT, GT)].partition_broadcast(P)).then_inc(i_in[k], 16)
                base = sp.value_load(gbase[0:1, bass.ds(g, 1)], min_val=0, max_val=NP_ - 1)
                sp.dma_start(Qw[k][:], v["Q_d"][bass.ds(base, P), :]).then_inc(q_in[k], 16)
                sp.dma_start(eT[k][:], v["eT"][:, bass.ds(g * GE, GE)]).then_inc(e_in[k], 16)

            def load_rel(g):
                sp.dma_start(rel_b[:], v["rel_d"][bass.ds(g * GE, GE)].partition_broadcast(P)).then_inc(r_in, 16)

            def store(g, k):
                sp.wait_ge(cnt_copy, g * GQ + GQ)
                sp.dma_start(v["A_d"][bass.ds(g, 1), :, :].rearrange("a p c -> (a p) c"),
                             counts[k][:, 0:NB, :].rearrange("p a d -> p (a d)")).then_inc(c_out[k], 16)

            def fast():
                load(0, 0)
                load_rel(0)
                load(1, 1)
                sp.wait_ge(prepared, 1)
                load_rel(1)
                with sp.Fori(0, (GROUPS - 2) // 2) as i:
                    for k in range(2):
                        g = 2 * i + k
                        sp.wait_ge(prepared, g + 2)
                        load_rel(g + 2)
                        sp.wait_ge(sum_mm, g * GQ + GQ)
                        load(g + 2, k)
                        store(g, k)
                for g in (GROUPS - 2, GROUPS - 1):
                    store(g, g % 2)
                for k in range(2):
                    sp.wait_ge(c_out[k], 16 * (GROUPS // 2))

            fork(sp, flag, fast, gen["sync"], force_general)

        @block.gpsimd
        def _(pool):
            turn = sem("turn")

            def group(half, k, first=False):
                g = 2 * half + k
                pool.wait_ge(i_in[k], 48 * (half + 1))
                pool.sem_inc(turn, 1)
                for q in range(GQ):
                    if not first:
                        pool.wait_ge(pre_add, (g - 1) * GQ + q + 1)
                        pool.sem_inc(turn, 1)
                    for t in range(QT):
                        c = q * QT + t
                        pool.indirect_dma_start(
                            gath[:, q, t * D:(t + 1) * D], None, v["P_d"],
                            bass.IndirectOffsetOnAxis(ap=src_i[k][:, c:c + 1], axis=0)).then_inc(g_in[q], 16)

            def fast():
                loop(pool, lambda: group(0, 0, True), group, lambda: group(GROUPS // 2 - 1, 1))

            fork(pool, flag, fast, gen["gpsimd"], force_general)

        @block.vector
        def _(dve):
            V = nc.vector
            def make_keys(half, k, early=False):
                g = 2 * half + k
                dve.wait_ge(i_in[k], 48 * (half + 1))
                D3 = dst_i[k][:]
                Fg = first_i[k][:, 0:1].broadcast_to([P, GT])
                Fq = first_i[k][:].rearrange("p (q t) -> p q t", t=QT)[:, :, 0:1].broadcast_to([P, GQ, QT])
                V.tensor_tensor(rel_g[k][:], D3, Fg, ALU.subtract)
                V.tensor_tensor(rel_q[:].rearrange("p (q t) -> p q t", t=QT), D3.rearrange("p (q t) -> p q t", t=QT),
                                Fq, ALU.subtract)
                V.tensor_scalar(blk_i[:], src_i[k][:], 7, None, ALU.arith_shift_right)
                V.tensor_scalar(low_i[:], src_i[k][:], P - 1, None, ALU.bitwise_and).then_inc(dv, 1)
                dve.wait_ge(dv, g + 1)
                V.tensor_copy(low[k][:], low_i[:])
                kq, bq, rq = (t[:].rearrange("p (q t) -> p q t", t=QT) for t in (key[k], blk_i, rel_q))
                for j, (w0, w) in enumerate(WIN):
                    V.scalar_tensor_tensor(kq[:, :, j], bq[:, :, j], float(w), rq[:, :, j], ALU.mult, ALU.add)

            def expand(k, cols):
                return V.tensor_scalar(nodeE[k][:, cols], rel_b[:, cols], pid[:, 0:1], None, ALU.is_equal)

            def expand_first(half, k, early=False):
                g = 2 * half + k
                if not early:
                    dve.wait_ge(pre_mm, (g - 1) * GQ)
                dve.wait_ge(r_in, 16 * (g + 1))
                expand(k, slice(0, GE // 2))

            def expand_rest(half, k, early=False):
                expand(k, slice(GE // 2, GE))
                if not early:
                    dve.wait_ge(c_out[k], 16 * half)
                V.memset(counts[k][:, :, CLEARED:P], 0.0).then_inc(prepared, 1)

            def hots(s, q, k, first=False):
                x = (k + q) % 2
                if not first:
                    dve.wait_ge(sum_mm, s - 1)
                    dve.wait_ge(cnt_mm, s - 1)
                c = slice(q * QT, (q + 1) * QT)
                io = iota[:, 0:P].unsqueeze(1).broadcast_to([P, QT, P])
                V.tensor_tensor(edgeN[x][:], io, rel_g[k][:, c].unsqueeze(2).broadcast_to([P, QT, P]), ALU.is_equal)
                V.tensor_tensor(edgeL[x][:], io, low[k][:, c].unsqueeze(2).broadcast_to([P, QT, P]), ALU.is_equal)
                for j, (w0, w) in enumerate(WIN):
                    last = V.tensor_scalar(edgeK[x][:, ROFF[j]:ROFF[j] + A2 * w], iota[:, w0:w0 + A2 * w],
                                           key[k][:, q * QT + j:q * QT + j + 1], None, ALU.is_equal)
                last.then_inc(onehots, 1)

            def add(s, q, k, g, first=False):
                x = (k + q) % 2
                dve.wait_ge(pre_mm, s + 1)
                dve.wait_ge(g_in[q], 16 * QT * (g + 1))
                if not first:
                    dve.wait_ge(silu, s - 1)
                V.tensor_tensor(pre[x][:], ps_pre[x][:], gath[:, q, :], ALU.add).then_inc(pre_add, 1)

            def add_sums(g, k):
                dve.wait_ge(sum_tr, g + 2)
                dve.wait_ge(sum_add, g + 1)
                base = dve.value_load(gbase[0:1, bass.ds(g, 1)], min_val=0, max_val=NP_ - 1)
                V.tensor_tensor(sumT[:, bass.ds(base, P)], ps_sum[k][:, TR:TR + P], sumT[:, bass.ds(base, P)], ALU.add)
                V.tensor_tensor(deg[0:1, bass.ds(base, P)], ps_sum[k][0:1, TR + P:TR + 2 * P], deg[0:1, bass.ds(base, P)],
                                ALU.add).then_inc(sum_add, 1)

            def group(half, k, first=False, last=False):
                g = 2 * half + k
                nxt = (half, 1) if k == 0 else (half + 1, 0)
                for q in range(GQ):
                    s = g * GQ + q
                    add(s, q, k, g, first and q < 2)
                    if q < GQ - 1:
                        hots(s + 1, q + 1, k, first and q == 0)
                    elif not last:
                        dve.wait_ge(prepared, g + 2)
                        hots(s + 1, 0, 1 - k)
                    if not last and q in (2, 3, 4):
                        (make_keys, expand_first, expand_rest)[q - 2](*nxt, early=first)
                    if q == 5 and not first:
                        add_sums(g - 1, 1 - k)

            def fast():
                for k in range(2):
                    V.memset(h[k][:, :, D:D + 2], 1.0).then_inc(h_ones, 1)
                dve.sem_inc(sum_add, 1)
                for part in (make_keys, expand_first, expand_rest):
                    part(0, 0, early=True)
                dve.wait_ge(prepared, 1)
                hots(0, 0, 0, True)
                loop(dve, lambda: group(0, 0, first=True), group, lambda: group(GROUPS // 2 - 1, 1, last=True))
                add_sums(GROUPS - 1, 1)

            fork(dve, flag, fast, gen["vector"], force_general)

        @block.tensor
        def _(pe):
            T = nc.tensor

            def products(s, q, k, half, first=False):
                x = (k + q) % 2
                if q == 0:
                    pe.wait_ge(e_in[k], 16 * (half + 1))
                    pe.wait_ge(q_in[k], 16 * (half + 1))
                    pe.wait_ge(prepared, 2 * half + k + 1)
                if not first:
                    pe.wait_ge(pre_add, s - 1)
                for t in range(QT):
                    e0 = (q * QT + t) * P
                    o = ps_pre[x][:, t * D:(t + 1) * D]
                    T.matmul(o, eT[k][:, e0:e0 + P], wc[:], start=True, stop=False)
                    for part in range(3):
                        last = T.matmul(o, nodeE[k][:, e0:e0 + P], Qw[k][:, part * D:(part + 1) * D],
                                        start=False, stop=(part == 2))
                last.then_inc(pre_mm, 1)

            def count(s, q, k, off, first=False):
                x = (k + q) % 2
                pe.wait_ge(onehots, s + 1)
                if not first:
                    pe.wait_ge(cnt_copy, s - 1)
                for b in range(2):
                    o = ps_cnt[x][:, b, 0:AB * W0].rearrange("p (a d) -> p a d", d=W0)
                    for j, (w0, w) in enumerate(WIN):
                        r = edgeK[x][:, ROFF[j] + b * AB * w:ROFF[j] + (b + 1) * AB * w].rearrange("p (a d) -> p a d", d=w)
                        last = T.matmul(o[:, :, w0:w0 + w], edgeL[x][:, j, :], r, start=(j == 0),
                                        stop=(j == QT - 1 and q == 0))
                if q > 0:
                    pe.wait_ge(cnt_copy, s)
                    for b in range(2):
                        o = ps_cnt[x][:, b, 0:AB * W0].rearrange("p (a d) -> p a d", d=W0)
                        last = T.matmul(o[:, :, 0:1], identb[:], counts[k][:, b * AB:(b + 1) * AB, bass.ds(off, 1)],
                                        start=False, stop=True)
                last.then_inc(cnt_mm, 1)

            def sums(s, q, k, g, first=False):
                x = (k + q) % 2
                pe.wait_ge(silu, s + 1)
                if q == 0 and not first:
                    pe.wait_ge(sum_add, g)
                for t in range(QT):
                    last = T.matmul(ps_sum[k][:, 0:SW], edgeN[x][:, t, :], h[x][:, t, 0:SW],
                                    start=(q == 0 and t == 0), stop=(q == GQ - 1 and t == QT - 1))
                last.then_inc(sum_mm, 1)

            def transpose_sums(g, k):
                pe.wait_ge(sum_copy, g + 1)
                T.matmul(ps_sum[k][:, TR:TR + P], sumS[:, 0:D], ident[:], is_transpose=True, start=True, stop=True)
                T.matmul(ps_sum[k][0:1, TR + P:TR + 2 * P], sumS[:, D:SW], ident[:], start=True, stop=True).then_inc(sum_tr, 1)

            def group(half, k, first=False, last=False, second=False):
                g = 2 * half + k
                off = [0] + [pe.value_load(offs[0:1, bass.ds(g * GQ + q, 1)], min_val=0, max_val=LASTQ)
                             for q in range(1, GQ)]
                for q in range(GQ):
                    s = g * GQ + q
                    if q < GQ - 1:
                        products(s + 1, q + 1, k, half, first and q == 0)
                    elif not last:
                        half1, k1 = (half, 1) if k == 0 else (half + 1, 0)
                        products(s + 1, 0, k1, half1)
                    sums(s, q, k, g, first)
                    if q < GQ - 1:
                        count(s + 1, q + 1, k, off[q + 1], first and q == 0)
                    elif not last:
                        count(s + 1, 0, k1, 0)
                    if q == 1 and not first:
                        transpose_sums(g - 1, 1 - k)

            def fast():
                pe.sem_inc(sum_tr, 1)
                pe.wait_ge(h_ones, 2)
                products(0, 0, 0, 0, True)
                count(0, 0, 0, 0, True)
                loop(pe, lambda: group(0, 0, first=True), group, lambda: group(GROUPS // 2 - 1, 1, last=True))
                transpose_sums(GROUPS - 1, 1)

            fork(pe, flag, fast, gen["tensor"], force_general)

        @block.scalar
        def _(act):
            A = nc.scalar

            def copy_counts(s, q, k, g, off, first=False):
                x = (k + q) % 2
                if q == 0:
                    act.wait_ge(prepared, g + 1)
                act.wait_ge(cnt_mm, s + 1)
                A.activation(counts[k][:].rearrange("p (b a) d -> p b a d", b=2)[:, :, :, bass.ds(off, W0)],
                             ps_cnt[x][:, :, 0:AB * W0].rearrange("p b (a d) -> p b a d", d=W0),
                             ACT.Copy).then_inc(cnt_copy, 1)

            def activate(s, q, k, first):
                x = (k + q) % 2
                act.wait_ge(pre_add, s + 1)
                if not first:
                    act.wait_ge(sum_mm, s - 1)
                A.activation(h[x][:, :, 0:D], pre[x][:].rearrange("p (t n) -> p t n", n=D), ACT.Silu).then_inc(silu, 1)

            def copy_sums(g, k, first):
                act.wait_ge(sum_mm, (g + 1) * GQ)
                if not first:
                    act.wait_ge(sum_tr, g + 1)
                A.activation(sumS[:, 0:SW], ps_sum[k][:, 0:SW], ACT.Copy).then_inc(sum_copy, 1)

            def group(half, k, first=False, last=False):
                g = 2 * half + k
                off = [0] + [act.value_load(offs[0:1, bass.ds(g * GQ + q, 1)], min_val=0, max_val=LASTQ)
                             for q in range(1, GQ)]
                for q in range(GQ):
                    s = g * GQ + q
                    activate(s, q, k, first and q < 2)
                    copy_counts(s, q, k, g, off[q], first)
                    if q == 1 and not first:
                        copy_sums(g - 1, 1 - k, False)

            def fast():
                act.wait_ge(h_ones, 2)
                loop(act, lambda: group(0, 0, first=True), group, lambda: group(GROUPS // 2 - 1, 1, last=True))
                copy_sums(GROUPS - 1, 1, False)

            fork(act, flag, fast, gen["scalar"], force_general)


def fork(eng, flag, fast, general, force_general):
    bad = eng.value_load(flag[0:1, 0:1], min_val=0, max_val=1)
    if force_general is None:
        fast()
        return
    with eng.If(bad == (2 if force_general else 0)):
        fast()
    with eng.Else():
        general(eng)


def general_path(nc, ctx, sem, sb, v, layer, e_buf, ps_a, ps_b):
    ident, wc, acc_d = v["ident"], v["wc"], v["acc_d"]
    L = f"{layer}"
    src_c, dst_c = sb("g_src" + L, [P, 1], I32), sb("g_dst" + L, [P, 1], I32)
    dst_r = sb("g_dst_r" + L, [P, P], I32)
    same = sb("g_same" + L, [P, P])
    before = sb("g_before" + L, [P, P])
    tmp = sb("g_tmp" + L, [P, P])
    dup = sb("g_dup" + L, [P, 1])
    row_to = sb("g_row_to" + L, [P, 1], I32)
    dst_f = sb("g_dst_f" + L, [P, 1])
    rows = sb("g_rows" + L, [P, D])
    q_rows = sb("g_q_rows" + L, [P, 3 * D], BF16)
    old = sb("g_old" + L, [P, SWP])
    new = sb("g_new" + L, [P, SWP])
    hm = sb("g_h" + L, [P, SWP])
    back = sb("g_back" + L, [P, SWP])
    ld = {n: sem(f"g_ld_{n}" + L) for n in ("e", "src", "dst", "dsts")}
    ga = {n: sem(f"g_ga_{n}" + L) for n in ("rows", "q", "old")}
    zr, pm, vm, sm, sc, mk, bk, bt, bc = (sem(f"g_{n}" + L) for n in (
        "zr", "pm", "vm", "sm", "sc", "mk", "bk", "bt", "bc"))
    turn, done = sem("g_turn" + L), sem("g_done" + L)
    DVE_STEPS = 7

    def sync(sp):
        sp.wait_ge(mk, 1)
        for b in range(NW // P):
            sp.dma_start(acc_d[b * P:(b + 1) * P, :], new[:]).then_inc(zr, 16)
        if layer == 1:
            sp.dma_start(v["x1_d"].rearrange("(j p) n -> p j n", p=P), v["x1"][:]).then_inc(zr, 16)
        sp.wait_ge(zr, 16 * (NW // P + layer))
        with sp.Fori(0, TILES) as t:
            sp.wait_ge(done, t + 1)
            if layer == 0:
                sp.dma_start(e_buf[:, 0:P], v["eT"][:, bass.ds(t * P, P)]).then_inc(ld["e"], 16)
            with nc.allow_non_contiguous_dma(reason="one index for each partition"):
                sp.dma_start(src_c[:], v["src_row"][bass.ds(t * P, P)].rearrange("(p a) -> p a", a=1)).then_inc(ld["src"], 16)
                sp.dma_start(dst_c[:], v["dst_row"][bass.ds(t * P, P)].rearrange("(p a) -> p a", a=1)).then_inc(ld["dst"], 16)
            sp.dma_start(dst_r[:], v["dst_row"][bass.ds(t * P, P)].partition_broadcast(P)).then_inc(ld["dsts"], 16)
        sp.wait_ge(done, TILES + 1)
        with sp.Fori(0, NB) as b:
            sp.wait_ge(bc, b + 1)
            sp.dma_start(back[:], acc_d[bass.ds(b * P, P), :]).then_inc(bk, 16)

    def gpsimd(pool):
        pool.memset(new[:], 0.0)
        pool.memset(hm[:], 1.0)
        pool.memset(before[:], 0.0).then_inc(mk, 1)
        pool.wait_ge(mk, 1)
        pool.affine_select(out=before[:], in_=before[:], compare_op=ALU.is_ge, fill=1.0, base=0,
                           pattern=[[1, P]], channel_multiplier=-1).then_inc(mk, 1)
        table = v["P_d"] if layer == 0 else v["x1_d"]
        at = lambda c: bass.IndirectOffsetOnAxis(ap=c, axis=0)
        pool.wait_ge(zr, 16 * (NW // P + layer))
        pool.sem_inc(done, 1)
        with pool.Fori(0, TILES) as t:
            pool.wait_ge(ld["src"], 16 * (t + 1))
            pool.wait_ge(ld["dst"], 16 * (t + 1))
            pool.sem_inc(turn, 1)
            if layer == 0:
                pool.indirect_dma_start(rows[:], None, table, at(src_c[:, 0:1])).then_inc(ga["rows"], 16)
                pool.indirect_dma_start(q_rows[:], None, v["Q_d"], at(dst_c[:, 0:1])).then_inc(ga["q"], 16)
            else:
                pool.indirect_dma_start(hm[:, 0:D], None, table, at(src_c[:, 0:1])).then_inc(ga["rows"], 16)
            pool.indirect_dma_start(old[:], None, acc_d, at(dst_c[:, 0:1])).then_inc(ga["old"], 16)
            pool.wait_ge(vm, DVE_STEPS * (t + 1))
            pool.sem_inc(turn, 1)
            pool.indirect_dma_start(acc_d, at(row_to[:, 0:1]), new[:], None,
                                    bounds_check=NW - 1, oob_is_err=False).then_inc(sc, 16)
            pool.wait_ge(sc, 16 * (t + 1))
            pool.sem_inc(done, 1)

    def vector(dve):
        V = nc.vector

        dve.wait_ge(mk, 2)
        with dve.Fori(0, TILES) as t:
            k = [0]

            def link(ins):
                k[0] += 1
                ins.then_inc(vm, 1)
                dve.wait_ge(vm, DVE_STEPS * t + k[0])
            dve.wait_ge(ld["dst"], 16 * (t + 1))
            dve.wait_ge(ld["dsts"], 16 * (t + 1))
            dve.wait_ge(done, t + 1)
            link(V.tensor_copy(dst_f[:], dst_c[:]))
            link(V.tensor_scalar(same[:], dst_r[:], dst_f[:, 0:1], None, ALU.is_equal))
            link(V.tensor_tensor(tmp[:], same[:], before[:], ALU.mult))
            link(V.reduce_sum(dup[:], tmp[:], AX.X))
            link(V.tensor_scalar(dup[:], dup[:], 1.0, float(SKIP), ALU.min, ALU.mult))
            link(V.tensor_tensor(row_to[:], dup[:], dst_f[:], ALU.add))
            dve.wait_ge(ga["old"], 16 * (t + 1))
            if layer == 0:
                dve.wait_ge(ga["rows"], 16 * (t + 1))
                dve.wait_ge(ga["q"], 16 * (t + 1))
                dve.wait_ge(pm, 2 * t + 1)
                V.tensor_tensor(tmp[:], ps_a[:, 0:D], rows[:], ALU.add).then_inc(sm, 1)
                for part in range(3):
                    dve.wait_ge(sm, 4 * t + part + 1)
                    V.tensor_tensor(tmp[:], tmp[:], q_rows[:, part * D:(part + 1) * D], ALU.add).then_inc(sm, 1)
                dve.wait_ge(pm, 2 * t + 2)
            else:
                dve.wait_ge(pm, t + 1)
            V.tensor_tensor(new[:, 0:SW], ps_b[:, 0:SW], old[:, 0:SW], ALU.add).then_inc(vm, 1)

    def scalar(act):
        act.sem_inc(bc, 1)
        if layer == 0:
            with act.Fori(0, TILES) as t:
                act.wait_ge(sm, 4 * t + 4)
                nc.scalar.activation(hm[:, 0:D], tmp[:], ACT.Silu).then_inc(bt, 1)
        with act.Fori(0, NB) as b:
            act.wait_ge(pm, (2 - layer) * TILES + b + 1)
            last = nc.scalar.activation(v["sumT"][:, bass.ds(b * P, P)], ps_a[:, 0:P], ACT.Copy)
            if layer == 0:
                last = nc.scalar.activation(v["deg"][0:1, bass.ds(b * P, P)], ps_a[0:1, P:2 * P], ACT.Copy)
            last.then_inc(bc, 1)

    def tensor(pe):
        T = nc.tensor
        with pe.Fori(0, TILES) as t:
            if layer == 0:
                pe.wait_ge(ld["e"], 16 * (t + 1))
                T.matmul(ps_a[:, 0:D], e_buf[:, 0:P], wc[:], start=True, stop=True).then_inc(pm, 1)
                pe.wait_ge(bt, t + 1)
            else:
                pe.wait_ge(ga["rows"], 16 * (t + 1))
            pe.wait_ge(vm, DVE_STEPS * t + DVE_STEPS - 1)
            T.matmul(ps_b[:, 0:SW], same[:], hm[:, 0:SW], start=True, stop=True).then_inc(pm, 1)
        with pe.Fori(0, NB) as b:
            pe.wait_ge(bk, 16 * (b + 1))
            T.matmul(ps_a[:, 0:P], back[:, 0:D], ident[:], is_transpose=True, start=True, stop=True)
            T.matmul(ps_a[0:1, P:2 * P], back[:, D:SW], ident[:], start=True, stop=True).then_inc(pm, 1)
            pe.wait_ge(bc, b + 2)

    return dict(sync=sync, gpsimd=gpsimd, vector=vector, scalar=scalar, tensor=tensor)


def build_nodes(nc, ctx, sem, sb, v):
    x1 = sb("x1", [P, NB, D])
    x1T = sb("x1T", [P, NP_])
    x1h = sb("x1h", [P, NB, 2, D], F16)
    v = dict(v, x1=x1, x1T=x1T, x1h=x1h)
    with ExitStack() as c:
        update_0(nc, c, lambda n: c.enter_context(nc.semaphore(n)),
                 lambda n, s, d=F32: c.enter_context(nc.sbuf_tensor("u0_" + n, s, d)), v)
    with ExitStack() as c:
        sums_1(nc, c, lambda n: c.enter_context(nc.semaphore(n)),
               lambda n, s, d=F32: c.enter_context(nc.sbuf_tensor(n, s, d)), v)
    with ExitStack() as c:
        update_1(nc, c, lambda n: c.enter_context(nc.semaphore(n)),
                 lambda n, s, d=F32: c.enter_context(nc.sbuf_tensor(n, s, d)), v)


def update_0(nc, ctx, sem, sb, v):
    sumT, deg, ident, ones_row, eps_col = v["sumT"], v["deg"], v["ident"], v["ones_row"], v["eps_col"]
    x1, x1T, x1h = v["x1"], v["x1T"], v["x1h"]
    w2, u2 = sb("w2", [P, D]), sb("u2", [P, D])
    u1 = sb("u1", [P, 2, D])
    mb2 = sb("mb2", [1, D])
    ub1 = sb("ub1", [P, 1])
    ub2bc, gbc, bbc = sb("ub2bc", [P, D]), sb("gbc", [P, D]), sb("bbc", [P, D])
    xT_c = [sb(f"xT_c{i}", [P, CN]) for i in range(2)]
    x_c = [sb(f"x_c{i}", [P, CH, D]) for i in range(2)]
    aggT_c = [sb(f"aggT_c{i}", [P, 2, HN]) for i in range(2)]
    hT_c = [sb(f"hT_c{i}", [P, 2, HN]) for i in range(2)]
    xbeta = sb("xbeta", [P, NB, D])
    z = x1
    st = sb("st", [P, NB, 6])
    mv = [sb(f"mv{i}", [P, NB, 2]) for i in range(2)]
    sd = [sb(f"sd{i}", [P, NB]) for i in range(2)]
    rs = [sb(f"rs{i}", [P, NB]) for i in range(2)]
    ps_a, ps_h, ps_y = (ctx.enter_context(nc.psum_tensor(f"u0_{n}", [P, 2, 512], F32)) for n in "ahy")
    ps_t = ctx.enter_context(nc.psum_tensor("u0_t", [P, 2, 512], F32))
    w_in, x_in, xT_in = sem("u0_w_in"), [sem(f"u0_x_in{i}") for i in range(2)], [sem(f"u0_xT_in{i}") for i in range(2)]
    agg_mm, agg_cp, h_mm, h_act, y_mm, z_add, xb = (sem(f"u0_{n}") for n in ("agg_mm", "agg_cp", "h_mm", "h_act", "y_mm", "z_add", "xb"))
    mv_ok, sd_ok, rs_ok, x_norm, x_hi, x_lo, t_mm, t_cp, dv = (
        sem(f"u0_{n}") for n in ("mv_ok", "sd_ok", "rs_ok", "x_norm", "x_hi", "x_lo", "t_mm", "t_cp", "dv"))

    with nc.Block() as block:
        @block.sync
        def _(sp):
            sp.dma_start(w2[:], v["mW2"]).then_inc(w_in, 16)
            sp.dma_start(mb2[:], v["mb2"].rearrange("(a n) -> a n", a=1)).then_inc(w_in, 16)
            sp.dma_start(u1[:], v["uW1"].rearrange("(c k) n -> k c n", c=2)).then_inc(w_in, 16)
            sp.dma_start(u2[:], v["uW2"]).then_inc(w_in, 16)
            with nc.allow_non_contiguous_dma(reason="one word for each partition"):
                sp.dma_start(ub1[:], v["ub1"].rearrange("(n a) -> n a", a=1)).then_inc(w_in, 16)
            sp.dma_start(ub2bc[:], v["ub2"].partition_broadcast(P)).then_inc(w_in, 16)
            sp.dma_start(gbc[:], v["gamma"].partition_broadcast(P)).then_inc(w_in, 16)
            sp.dma_start(bbc[:], v["beta"].partition_broadcast(P)).then_inc(w_in, 16)
            for c in range(CHUNKS):
                if c >= 2:
                    sp.wait_ge(h_mm, c - 1)
                sp.dma_start(xT_c[c % 2][:], v["xT"][:, c * CN:(c + 1) * CN]).then_inc(xT_in[c % 2], 16)
                if c >= 2:
                    sp.wait_ge(z_add, c - 1)
                sp.dma_start(x_c[c % 2][:], v["x_nm"][c * CN:(c + 1) * CN, :].rearrange("(j p) n -> p j n", p=P)).then_inc(x_in[c % 2], 16)

        @block.tensor
        def _(pe):
            T = nc.tensor

            def aggregate(c):
                if c >= 1:
                    pe.wait_ge(agg_cp, c)
                for i in range(2):
                    cols = slice(c * CN + i * HN, c * CN + (i + 1) * HN)
                    T.matmul(ps_a[:, i, 0:HN], w2[:], sumT[:, cols], start=True, stop=False)
                    last = T.matmul(ps_a[:, i, 0:HN], mb2[:], deg[0:1, cols], start=False, stop=True)
                last.then_inc(agg_mm, 1)

            def hidden(c):
                pe.wait_ge(xT_in[c % 2], 16 * (c // 2 + 1))
                if c >= 1:
                    pe.wait_ge(h_act, c)
                for i in range(2):
                    T.matmul(ps_h[:, i, 0:HN], u1[:, 0, :], xT_c[c % 2][:, i * HN:(i + 1) * HN], start=True, stop=False)
                pe.wait_ge(agg_cp, c + 1)
                for i in range(2):
                    last = T.matmul(ps_h[:, i, 0:HN], u1[:, 1, :], aggT_c[c % 2][:, i, :], start=False, stop=True)
                last.then_inc(h_mm, 1)

            def output(c):
                pe.wait_ge(h_act, c + 1)
                if c >= 1:
                    pe.wait_ge(z_add, c)
                for j in range(CH):
                    last = T.matmul(ps_y[:, j // 4, (j % 4) * D:(j % 4 + 1) * D],
                                    hT_c[c % 2][:].rearrange("p i n -> p (i n)")[:, j * P:(j + 1) * P], u2[:],
                                    start=True, stop=True)
                last.then_inc(y_mm, 1)

            pe.wait_ge(w_in, 128)
            aggregate(0)
            for c in range(CHUNKS):
                hidden(c)
                if c + 1 < CHUNKS:
                    aggregate(c + 1)
                output(c)
            for c in range(CHUNKS):
                pe.wait_ge(x_norm, c + 1)
                if c >= 1:
                    pe.wait_ge(t_cp, c)
                for j in range(CH):
                    last = T.matmul(ps_t[:, j // 4, (j % 4) * D:(j % 4 + 1) * D], x1[:, c * CH + j, :], ident[:],
                                    is_transpose=True, start=True, stop=True)
                last.then_inc(t_mm, 1)

        @block.scalar
        def _(act):
            A = nc.scalar
            act.wait_ge(w_in, 128)
            for c in range(CHUNKS):
                act.wait_ge(agg_mm, c + 1)
                if c >= 2:
                    act.wait_ge(h_mm, c - 1)
                A.activation(aggT_c[c % 2][:], ps_a[:, :, 0:HN], ACT.Copy).then_inc(agg_cp, 1)
                act.wait_ge(h_mm, c + 1)
                if c >= 2:
                    act.wait_ge(y_mm, c - 1)
                A.activation(hT_c[c % 2][:], ps_h[:, :, 0:HN], ACT.Silu, bias=ub1[:, 0:1]).then_inc(h_act, 1)
            for i in range(2):
                act.wait_ge(mv_ok, (i + 1) * CHUNKS)
                A.activation(sd[i][:], mv[i][:, :, 1], ACT.Sqrt, bias=eps_col[:, 0:1]).then_inc(sd_ok, 1)
            for c in range(CHUNKS):
                b = slice(c * CH, (c + 1) * CH)
                act.wait_ge(x_norm, c + 1)
                A.activation(x1h[:, b, 0, :], x1[:, b, :], ACT.Copy).then_inc(x_hi, 1)
                act.wait_ge(t_mm, c + 1)
                A.activation(x1T[:, c * CN:c * CN + 4 * P], ps_t[:, 0, :], ACT.Copy)
                A.activation(x1T[:, c * CN + 4 * P:(c + 1) * CN], ps_t[:, 1, 0:3 * P], ACT.Copy).then_inc(t_cp, 1)

        @block.vector
        def _(dve):
            V = nc.vector
            n = [0]

            def link(ins):
                n[0] += 1
                ins.then_inc(dv, 1)
                dve.wait_ge(dv, n[0])

            def bc(t):
                return t[:].unsqueeze(1).broadcast_to([P, CH, D])

            dve.wait_ge(w_in, 128)
            for c in range(CHUNKS):
                b = slice(c * CH, (c + 1) * CH)
                dve.wait_ge(x_in[c % 2], 16 * (c // 2 + 1))
                V.tensor_tensor(xbeta[:, b, :], x_c[c % 2][:], bc(bbc), ALU.add)
                link(V.tensor_tensor(x_c[c % 2][:], x_c[c % 2][:], bc(ub2bc), ALU.add))
                dve.wait_ge(y_mm, c + 1)
                V.tensor_tensor(z[:, c * CH:c * CH + 4, :], ps_y[:, 0, :].rearrange("p (j n) -> p j n", n=D),
                                x_c[c % 2][:, 0:4, :], ALU.add)
                V.tensor_tensor(z[:, c * CH + 4:(c + 1) * CH, :], ps_y[:, 1, 0:3 * D].rearrange("p (j n) -> p j n", n=D),
                                x_c[c % 2][:, 4:CH, :], ALU.add).then_inc(z_add, 1)
                dve.wait_ge(z_add, c + 1)
                stats(V, link, z, st, mv[0], b, mv_ok)
            dve.wait_ge(sd_ok, 1)
            link(V.reciprocal(rs[0][:], sd[0][:]))
            dve.wait_ge(mv_ok, CHUNKS)
            for c in range(CHUNKS):
                b = slice(c * CH, (c + 1) * CH)
                for j in range(c * CH, (c + 1) * CH):
                    last = V.tensor_scalar(z[:, j, :], z[:, j, :], mv[0][:, j, 0:1], rs[0][:, j:j + 1], ALU.subtract, ALU.mult)
                link(last)
                link(V.tensor_tensor(z[:, b, :], z[:, b, :], bc(gbc), ALU.mult))
                link(V.tensor_tensor(z[:, b, :], z[:, b, :], xbeta[:, b, :], ALU.add))
                stats(V, link, z, st, mv[1], b, mv_ok)
            dve.wait_ge(sd_ok, 2)
            link(V.reciprocal(rs[1][:], sd[1][:]))
            dve.wait_ge(mv_ok, 2 * CHUNKS)

            def low_part(c):
                b = slice(c * CH, (c + 1) * CH)
                dve.wait_ge(x_hi, c + 1)
                V.tensor_tensor(x1h[:, b, 1, :], x1[:, b, :], x1h[:, b, 0, :], ALU.subtract).then_inc(x_lo, 1)

            for c in range(CHUNKS):
                for j in range(c * CH, (c + 1) * CH):
                    last = V.tensor_scalar(x1[:, j, :], z[:, j, :], mv[1][:, j, 0:1], rs[1][:, j:j + 1], ALU.subtract, ALU.mult)
                last.then_inc(x_norm, 1)
                dve.wait_ge(x_norm, c + 1)
                if c >= 1:
                    low_part(c - 1)
            low_part(CHUNKS - 1)
            link(V.tensor_scalar(deg[0:1, 0:NP_], deg[0:1, 0:NP_], 1.0, None, ALU.max))
            link(V.reciprocal(deg[0:1, 0:NP_], deg[0:1, 0:NP_]))
            V.memset(sumT[:], 0.0)


def stats(V, link, z, st, mv, b, done):
    for j in range(b.start, b.stop):
        last = V.bn_stats(st[:, j, :], z[:, j, :])
    link(last)
    for j in range(b.start, b.stop):
        last = V.bn_aggr(mv[:, j, :], st[:, j, :])
    last.then_inc(done, 1)


def sums_1(nc, ctx, sem, sb, v):
    RING = 4
    A_c = [sb(f"A_c{r}", [P, NB * P], BF16) for r in range(RING)]
    sumT, gbase, x1h = v["sumT"], v["gbase"], v["x1h"]
    ps = [ctx.enter_context(nc.psum_tensor(f"ps_n{i}", [P, 512], F32)) for i in range(RING)]
    a_in = [sem(f"a_in{r}") for r in range(RING)]
    agg_mm, agg_add = sem("s1_mm"), sem("s1_add")
    gen = general_path(nc, ctx, sem, sb, v, 1, None, ps[0], ps[1])
    with nc.Block() as block:
        @block.sync
        def _(sp):
            def fast():
                for r in range(RING):
                    sp.dma_start(A_c[r][:], v["A_d"][r]).then_inc(a_in[r], 16)
                with sp.Fori(0, GROUPS // RING - 1) as i:
                    for r in range(RING):
                        g = RING * i + r
                        sp.wait_ge(agg_mm, g + 1)
                        sp.dma_start(A_c[r][:], v["A_d"][bass.ds(g + RING, 1), :, :].rearrange("a p c -> (a p) c")).then_inc(a_in[r], 16)
            fork(sp, v["flag"], fast, gen["sync"], v["force_general"])

        @block.tensor
        def _(pe):
            def fast():
                with pe.Fori(0, GROUPS // RING) as i:
                    for r in range(RING):
                        pe.wait_ge(a_in[r], 16 * (i + 1))
                        pe.wait_ge(agg_add, RING * i + 1)
                        for a in range(NB):
                            for part in range(2):
                                last = nc.tensor.matmul(ps[r][:, 0:P], x1h[:, a, part, :], A_c[r][:, a * P:(a + 1) * P],
                                                        start=(a == 0 and part == 0), stop=(a == NB - 1 and part == 1))
                        last.then_inc(agg_mm, 1)
            fork(pe, v["flag"], fast, gen["tensor"], v["force_general"])

        @block.vector
        def _(dve):
            def fast():
                dve.sem_inc(agg_add, 1)
                with dve.Fori(0, GROUPS // RING) as i:
                    for r in range(RING):
                        g = RING * i + r
                        base = dve.value_load(gbase[0:1, bass.ds(g, 1)], min_val=0, max_val=NP_ - 1)
                        dve.wait_ge(agg_mm, g + 1)
                        dve.wait_ge(agg_add, g + 1)
                        nc.vector.tensor_tensor(sumT[:, bass.ds(base, P)], ps[r][:, 0:P], sumT[:, bass.ds(base, P)],
                                                ALU.add).then_inc(agg_add, 1)
            fork(dve, v["flag"], fast, gen["vector"], v["force_general"])

        @block.scalar
        def _(act):
            fork(act, v["flag"], lambda: act.nop(), gen["scalar"], v["force_general"])

        @block.gpsimd
        def _(pool):
            fork(pool, v["flag"], lambda: pool.nop(), gen["gpsimd"], v["force_general"])


def update_1(nc, ctx, sem, sb, v):
    sumT, rdeg, ident, ones_row, eps_col = v["sumT"], v["deg"], v["ident"], v["ones_row"], v["eps_col"]
    x1, x1T = v["x1"], v["x1T"]
    w1, w2 = sb("l1_w1", [P, 2, D]), sb("l1_w2", [P, D])
    b1, b2bc = sb("l1_b1", [P, 1]), sb("l1_b2", [P, D])
    hT_c = [sb(f"l1_hT{i}", [P, 2, HN]) for i in range(2)]
    z = sb("l1_z", [P, NB, D])
    st = sb("l1_st", [P, NB, 6])
    mv = sb("l1_mv", [P, NB, 2])
    sd, rs = sb("l1_sd", [P, NB]), sb("l1_rs", [P, NB])
    ps_r, ps_h, ps_y = (ctx.enter_context(nc.psum_tensor(f"u1_{n}", [P, 2, 512], F32)) for n in "rhy")
    w_in, dv, r_mm, scaled, h_mm, h_act, y_mm, z_add, mv_ok, sd_ok, normed, stored = (
        sem(f"u1_{n}") for n in ("w_in", "dv", "r_mm", "scaled", "h_mm", "h_act", "y_mm", "z_add", "mv_ok", "sd_ok",
                                 "normed", "stored"))

    with nc.Block() as block:
        @block.sync
        def _(sp):
            sp.dma_start(w1[:], v["W1"].rearrange("(c k) n -> k c n", c=2)).then_inc(w_in, 16)
            sp.dma_start(w2[:], v["W2"]).then_inc(w_in, 16)
            with nc.allow_non_contiguous_dma(reason="one word for each partition"):
                sp.dma_start(b1[:], v["b1"].rearrange("(n a) -> n a", a=1)).then_inc(w_in, 16)
            sp.dma_start(b2bc[:], v["b2"].partition_broadcast(P)).then_inc(w_in, 16)
            for c in range(CHUNKS):
                sp.wait_ge(normed, c + 1)
                sp.dma_start(v["out"][c * CN:(c + 1) * CN, :].rearrange("(j p) n -> p j n", p=P),
                             z[:, c * CH:(c + 1) * CH, :]).then_inc(stored, 16)
            sp.wait_ge(stored, 16 * CHUNKS)

        @block.tensor
        def _(pe):
            T = nc.tensor

            def spread(c):
                if c >= 1:
                    pe.wait_ge(scaled, c)
                for i in range(2):
                    last = T.matmul(ps_r[:, i, 0:HN], ones_row[:], rdeg[0:1, c * CN + i * HN:c * CN + (i + 1) * HN],
                                    start=True, stop=True)
                last.then_inc(r_mm, 1)

            pe.wait_ge(w_in, 64)
            spread(0)
            for c in range(CHUNKS):
                if c >= 1:
                    pe.wait_ge(h_act, c)
                for i in range(2):
                    cols = slice(c * CN + i * HN, c * CN + (i + 1) * HN)
                    T.matmul(ps_h[:, i, 0:HN], w1[:, 0, :], x1T[:, cols], start=True, stop=False)
                pe.wait_ge(scaled, c + 1)
                for i in range(2):
                    cols = slice(c * CN + i * HN, c * CN + (i + 1) * HN)
                    last = T.matmul(ps_h[:, i, 0:HN], w1[:, 1, :], sumT[:, cols], start=False, stop=True)
                last.then_inc(h_mm, 1)
                if c + 1 < CHUNKS:
                    spread(c + 1)
                pe.wait_ge(h_act, c + 1)
                if c >= 1:
                    pe.wait_ge(z_add, c)
                for j in range(CH):
                    last = T.matmul(ps_y[:, j // 4, (j % 4) * D:(j % 4 + 1) * D],
                                    hT_c[c % 2][:].rearrange("p i n -> p (i n)")[:, j * P:(j + 1) * P], w2[:],
                                    start=True, stop=True)
                last.then_inc(y_mm, 1)

        @block.scalar
        def _(act):
            act.wait_ge(w_in, 64)
            for c in range(CHUNKS):
                act.wait_ge(h_mm, c + 1)
                if c >= 2:
                    act.wait_ge(y_mm, c - 1)
                nc.scalar.activation(hT_c[c % 2][:], ps_h[:, :, 0:HN], ACT.Relu, bias=b1[:, 0:1]).then_inc(h_act, 1)
            act.wait_ge(mv_ok, CHUNKS)
            nc.scalar.activation(sd[:], mv[:, :, 1], ACT.Sqrt, bias=eps_col[:, 0:1]).then_inc(sd_ok, 1)

        @block.vector
        def _(dve):
            V = nc.vector
            n = [0]

            def link(ins):
                n[0] += 1
                ins.then_inc(dv, 1)
                dve.wait_ge(dv, n[0])

            def scale(c):
                dve.wait_ge(r_mm, c + 1)
                cols = slice(c * CN, (c + 1) * CN)
                s3 = sumT[:, cols].rearrange("p (i n) -> p i n", i=2)
                V.tensor_tensor(s3, ps_r[:, :, 0:HN], s3, ALU.mult).then_inc(scaled, 1)

            dve.wait_ge(w_in, 64)
            scale(0)
            for c in range(CHUNKS):
                if c + 1 < CHUNKS:
                    scale(c + 1)
                b0 = c * CH
                dve.wait_ge(y_mm, c + 1)
                for i, m in ((0, 4), (1, 3)):
                    zz = z[:, b0 + 4 * i:b0 + 4 * i + m, :]
                    last = V.tensor_tensor(zz, ps_y[:, i, 0:m * D].rearrange("p (j n) -> p j n", n=D),
                                           b2bc[:].unsqueeze(1).broadcast_to([P, m, D]), ALU.add)
                last.then_inc(z_add, 1)
                dve.wait_ge(z_add, c + 1)
                b = slice(b0, b0 + CH)
                link(V.scalar_tensor_tensor(z[:, b, :], z[:, b, :], 0.0, x1[:, b, :], ALU.max, ALU.add))
                stats(V, link, z, st, mv, b, mv_ok)
            dve.wait_ge(sd_ok, 1)
            link(V.reciprocal(rs[:], sd[:]))
            for c in range(CHUNKS):
                for j in range(c * CH, (c + 1) * CH):
                    last = V.tensor_scalar(z[:, j, :], z[:, j, :], mv[:, j, 0:1], rs[:, j:j + 1], ALU.subtract, ALU.mult)
                last.then_inc(normed, 1)


def kernel(x, src, dst, edge_attr_128, L0_gnn_msg_W1, L0_gnn_msg_b1, L0_gnn_msg_W2, L0_gnn_msg_b2, L0_gnn_upd_W1,
           L0_gnn_upd_b1, L0_gnn_upd_W2, L0_gnn_upd_b2, L0_gnn_ln_gamma, L0_gnn_ln_beta, L1_gnn_W1, L1_gnn_b1,
           L1_gnn_W2, L1_gnn_b2):
    import concourse.bacc as _bacc
    from concourse.bass_utils import run_bass_kernel_spmd as _run

    x, src, dst, e = (np.asarray(a) for a in (x, src, dst, edge_attr_128))
    pad = EP - N_EDGES
    x_nm = np.zeros((NP_, D), x.dtype)
    x_nm[:N_NODES] = x
    eT = np.zeros((D, EP), e.dtype)
    eT[:, :N_EDGES] = e.T
    src_row = np.zeros(EP, src.dtype)
    src_row[:N_EDGES] = src
    dst_row = np.full(EP + 1, NP_, dst.dtype)
    dst_row[:N_EDGES] = dst
    dst_row[N_EDGES:EP] = N_NODES + np.arange(pad) // SPREAD
    arrays = {
        "x_nm": x_nm, "xT": x_nm.T, "eT": eT,
        "src_pt": src_row.reshape(TILES, P).T, "dst_pt": dst_row[:EP].reshape(TILES, P).T,
        "dst_next_pt": dst_row[1:].reshape(TILES, P).T, "src_row": src_row, "dst_row": dst_row[:EP],
        "dst_first": dst_row[::P],
        "mW1": L0_gnn_msg_W1, "mb1": L0_gnn_msg_b1, "mW2": L0_gnn_msg_W2, "mb2": L0_gnn_msg_b2,
        "uW1": L0_gnn_upd_W1, "ub1": L0_gnn_upd_b1, "uW2": L0_gnn_upd_W2, "ub2": L0_gnn_upd_b2,
        "gamma": L0_gnn_ln_gamma, "beta": L0_gnn_ln_beta,
        "W1": L1_gnn_W1, "b1": L1_gnn_b1, "W2": L1_gnn_W2, "b2": L1_gnn_b2,
    }
    arrays = {k: np.ascontiguousarray(np.asarray(a)) for k, a in arrays.items()}
    nc = _bacc.Bacc("TRN2", target_bir_lowering=False, num_devices=1)
    aps = {k: nc.dram_tensor(k, a.shape, mybir.dt.from_np(a.dtype), kind="ExternalInput").ap() for k, a in arrays.items()}
    out = nc.dram_tensor("out", (NP_, D), F32, kind="ExternalOutput").ap()
    bass_gnn_two_layers(nc, out=out, **aps)
    r = _run(nc, [arrays], core_ids=[0])
    return r.results[0]["out"][:N_NODES]
```

```python
import numpy as np
import concourse.bass as bass
from concourse import mybir
from contextlib import ExitStack

F32, BF16, F16, I32 = mybir.dt.float32, mybir.dt.bfloat16, mybir.dt.float16, mybir.dt.int32
ALU = mybir.AluOpType
ACT = mybir.ActivationFunctionType
AX = mybir.AxisListType

N_NODES, N_EDGES, D = 6250, 200000, 128
P = 128
QT, GQ = 4, 7
GT = QT * GQ
GE = GT * P
GROUPS = -(-N_EDGES // GE)
TILES = GROUPS * GT
QUADS = GROUPS * GQ
EP = TILES * P
NB = -(-N_NODES // P)
NP_ = NB * P
NW = NP_ + P
SPREAD = -(-(EP - N_EDGES) // (NP_ - N_NODES))
W0 = 20
WIN = [(0, W0), (2, 10), (5, 12), (8, 12)]
AB = 25
A2 = 2 * AB
ROFF = [A2 * sum(w for _, w in WIN[:j]) for j in range(QT)]
RCOLS = ROFF[-1] + A2 * WIN[-1][1]
LASTQ = P - W0
CLEARED = 96
CH = 7
CHUNKS = NB // CH
CN = CH * P
HN = CN // 2
SW = D + 1
SWP = 132
EPS = 1e-5
SKIP = 8192


def bass_gnn_two_layers(nc, x_nm, xT, eT, src_pt, dst_pt, dst_next_pt, src_row, dst_row, dst_first,
                        mW1, mb1, mW2, mb2, uW1, ub1, uW2, ub2, gamma, beta, W1, b1, W2, b2, out,
                        force_general=False):
    def dram(name, shape, dt):
        return nc.dram_tensor(name, shape, dt).ap()

    P_d = dram("P_d", (NP_, D), F32)
    Q_d = dram("Q_d", (NW, 3 * D), BF16)
    rel_d = dram("rel_d", (EP,), BF16)
    A_d = dram("A_d", (GROUPS, P, NB * P), BF16)
    acc_d = dram("acc_d", (NW, SWP), F32)
    x1_d = dram("x1_d", (NP_, D), F32)
    deg_d = dram("deg_d", (NP_,), F32)
    rdeg_d = dram("rdeg_d", (NP_,), F32)

    with ExitStack() as top:
        def sem(name, ctx=top):
            return ctx.enter_context(nc.semaphore(name))

        def sb(name, shape, dt=F32, ctx=top):
            return ctx.enter_context(nc.sbuf_tensor(name, shape, dt))

        sumT = sb("sumT", [P, NW])
        deg = sb("deg", [P, NW])
        flag = sb("flag", [1, 1], I32)
        offs = sb("offs", [1, QUADS], I32)
        gbase = sb("gbase", [1, GROUPS], I32)
        ident = sb("ident", [P, P])
        identb = sb("identb", [P, P], BF16)
        pid = sb("pid", [P, 1])
        iota = sb("iota", [P, 1000], F16)
        wc = sb("wc", [P, D])
        eps_col = sb("eps_col", [P, 1])
        u1a, wagg, bagg, u2 = sb("u1a", [P, D]), sb("wagg", [P, D]), sb("bagg", [1, D]), sb("u2", [P, D])
        ub1_sb, ub2bc, gbc, bbc = sb("ub1_sb", [P, 1]), sb("ub2bc", [P, D]), sb("gbc", [P, D]), sb("bbc", [P, D])

        with ExitStack() as both:
            gath = sb("gath", [P, GQ, QT * D], F32, both)
            src_i = [sb(f"src_i{k}", [P, GT], I32, both) for k in range(2)]
            g_in = [sem(f"g_in{q}") for q in range(GQ)]
            with ExitStack() as ctx:
                build_prepare(nc, ctx, lambda n: sem(n, ctx), lambda n, s, d=F32: sb(n, s, d, ctx), locals())
            with ExitStack() as ctx:
                build_edges(nc, ctx, lambda n: sem(n, ctx), lambda n, s, d=F32: sb(n, s, d, ctx), locals(), force_general)
        with ExitStack() as ctx:
            build_nodes(nc, ctx, lambda n: sem(n, ctx), lambda n, s, d=F32: sb(n, s, d, ctx), locals())


def build_prepare(nc, ctx, sem, sb, v):
    P_d, Q_d, rel_d = v["P_d"], v["Q_d"], v["rel_d"]
    pid, ident, identb, iota = v["pid"], v["ident"], v["identb"], v["iota"]
    flag, offs, gbase = v["flag"], v["offs"], v["gbase"]
    wab = sb("wab", [P, 2, D])
    mw2, mw2T, u1b, mb2c = sb("mw2", [P, D]), sb("mw2T", [P, D]), sb("u1b", [P, D]), sb("mb2c", [P, 1])
    xT_sb = sb("xT_sb", [P, NP_])
    b1bc = sb("b1bc", [P, D])
    D_i, N_i, F_i = sb("D_i", [P, TILES], I32), sb("N_i", [P, TILES], I32), sb("F_i", [P, TILES + 1], I32)
    rel = sb("rel", [P, TILES])
    bad = sb("bad", [P, TILES])
    bad1 = sb("bad1", [P, 1])
    ones_col = sb("ones_col", [P, 1])
    RP = 2 * GROUPS
    RC = EP // RP
    R_i, RB_i, relR = sb("R_i", [RP, RC], I32), sb("RB_i", [RP, 1], I32), sb("relR", [RP, RC], BF16)
    orow = sb("orow", [1, QUADS])
    Pst = [sb(f"Pst{i}", [P, CH, D]) for i in range(2)]
    qf = [sb(f"qf{i}", [P, CH, D]) for i in range(2)]
    qr = [sb(f"qr{i}", [P, CH, D]) for i in range(2)]
    QR = 4
    Qst = [sb(f"Qst{i}", [P, CH, 3, D], BF16) for i in range(QR)]
    zeros = sb("zeros", [P, 3 * D], BF16)
    ps_p, ps_q = ([ctx.enter_context(nc.psum_tensor(f"ps_{n}{i}", [P, 8, D], F32)) for i in range(2)] for n in "pq")

    w_in, b_in, e_in, r_in, s_in = sem("w_in"), sem("b_in"), sem("e_in"), sem("r_in"), sem("s_in")
    u_in, wt = sem("u_in"), sem("wt")
    x_in = [sem(f"x_in{i}") for i in range(CHUNKS)]
    made, dv, p_mm, q_mm, p_out, q1_out, q2_out, r_out, q3_out, qf_out = (
        sem(n) for n in ("made", "dv", "p_mm", "q_mm", "p_out", "q1_out", "q2_out", "r_out", "q3_out", "qf_out"))
    rel_ready, bad_ready, bad_sum, st_z, st_r = (
        sem(n) for n in ("rel_ready", "bad_ready", "bad_sum", "st_z", "st_r"))
    st_p = [sem(f"st_p{i}") for i in range(2)]
    st_q = [sem(f"st_q{i}") for i in range(QR)]

    with nc.Block() as block:
        @block.sync
        def _(sp):
            sp.dma_start(wab[:], v["mW1"][0:2 * D, :].rearrange("(c k) n -> k c n", c=2)).then_inc(w_in, 16)
            for c in range(CHUNKS):
                sp.dma_start(xT_sb[:, c * CN:(c + 1) * CN], v["xT"][:, c * CN:(c + 1) * CN]).then_inc(x_in[c], 16)
            sp.dma_start(b1bc[:], v["mb1"].partition_broadcast(P)).then_inc(b_in, 16)
            sp.dma_start(v["wc"][:], v["mW1"][2 * D:3 * D, :]).then_inc(b_in, 16)
            for to, a in ((mw2, v["mW2"]), (v["u1a"], v["uW1"][0:D, :]), (u1b, v["uW1"][D:2 * D, :]), (v["u2"], v["uW2"])):
                sp.dma_start(to[:], a).then_inc(u_in, 16)
            with nc.allow_non_contiguous_dma(reason="one word for each partition"):
                sp.dma_start(mb2c[:], v["mb2"].rearrange("(n a) -> n a", a=1)).then_inc(u_in, 16)
                sp.dma_start(v["ub1_sb"][:], v["ub1"].rearrange("(n a) -> n a", a=1)).then_inc(u_in, 16)
            for to, a in ((v["ub2bc"], v["ub2"]), (v["gbc"], v["gamma"]), (v["bbc"], v["beta"])):
                sp.dma_start(to[:], a.partition_broadcast(P)).then_inc(u_in, 16)
            sp.wait_ge(made, 5)
            sp.dma_start(Q_d[NP_:NW, :], zeros[:]).then_inc(st_z, 16)
            for c in range(CHUNKS):
                sp.wait_ge(p_out, c + 1)
                sp.dma_start(P_d[c * CN:(c + 1) * CN, :].rearrange("(j p) n -> p j n", p=P),
                             Pst[c % 2][:]).then_inc(st_p[c % 2], 16)
            sp.wait_ge(rel_ready, 1)
            sp.dma_start(rel_d.rearrange("(g h c) -> h g c", h=2, c=RC)[0], relR[0:GROUPS, :]).then_inc(st_r, 16)
            sp.dma_start(rel_d.rearrange("(g h c) -> h g c", h=2, c=RC)[1], relR[GROUPS:RP, :]).then_inc(st_r, 16)
            for c in range(CHUNKS):
                sp.wait_ge(q3_out, c + 1)
                sp.dma_start(Q_d[c * CN:(c + 1) * CN, :].rearrange("(j p) n -> p j n", p=P),
                             Qst[c % QR][:].rearrange("p j t n -> p j (t n)")).then_inc(st_q[c % QR], 16)
            for i in range(QR):
                sp.wait_ge(st_q[i], 16 * len(range(i, CHUNKS, QR)))
            sp.wait_ge(st_z, 16)
            sp.wait_ge(st_r, 32)

        @block.gpsimd
        def _(pool):
            pool.iota(pid[:], [[0, 1]], base=0, channel_multiplier=1, allow_small_or_imprecise_dtypes=True).then_inc(made, 1)
            pool.iota(iota[:], [[1, 1000]], base=0, channel_multiplier=0, allow_small_or_imprecise_dtypes=True).then_inc(made, 1)
            pool.memset(ident[:], 0.0).then_inc(made, 1)
            pool.memset(identb[:], 0.0).then_inc(made, 1)
            pool.memset(zeros[:], 0.0).then_inc(made, 1)
            pool.memset(v["eps_col"][:], EPS)
            pool.memset(ones_col[:], 1.0)
            pool.memset(v["sumT"][:], 0.0)
            pool.memset(v["deg"][0:1, :], 0.0).then_inc(made, 1)
            pool.wait_ge(made, 6)
            for m in (ident, identb):
                pool.affine_select(out=m[:], in_=m[:], compare_op=ALU.not_equal, fill=1.0, base=0,
                                   pattern=[[-1, P]], channel_multiplier=1).then_inc(made, 1)
            pool.wait_ge(s_in, 16)
            for i in range(2):
                pool.wait_ge(st_p[i], 16 * len(range(i, CHUNKS, 2)))
            for c in range(GT):
                q, t = divmod(c, QT)
                pool.indirect_dma_start(v["gath"][:, q, t * D:(t + 1) * D], None, P_d,
                                        bass.IndirectOffsetOnAxis(ap=v["src_i"][0][:, c:c + 1], axis=0)).then_inc(v["g_in"][q], 16)

        @block.tensor
        def _(pe):
            pe.wait_ge(w_in, 16)
            for ps, half, done, free in ((ps_p, 0, p_mm, p_out), (ps_q, 1, q_mm, qf_out)):
                for c in range(CHUNKS):
                    if half == 0:
                        pe.wait_ge(x_in[c], 16)
                    if c >= 2:
                        pe.wait_ge(free, c - 1)
                    for j in range(CH):
                        n0 = (c * CH + j) * P
                        last = nc.tensor.matmul(ps[c % 2][:, j, :], xT_sb[:, n0:n0 + P], wab[:, half, :], start=True, stop=True)
                    last.then_inc(done, 1)
            pe.wait_ge(u_in, 144)
            pe.wait_ge(made, 8)
            nc.tensor.matmul(ps_p[1][:, 0, :], mw2[:], ident[:], is_transpose=True, start=True, stop=True).then_inc(wt, 1)
            pe.wait_ge(wt, 2)
            nc.tensor.matmul(ps_p[1][:, 1, :], mw2T[:], u1b[:], start=True, stop=True)
            nc.tensor.matmul(ps_p[1][0:1, 2, :], mb2c[:], u1b[:], start=True, stop=True).then_inc(wt, 1)
            pe.wait_ge(bad_ready, 1)
            nc.tensor.matmul(ps_p[0][0:1, 0, 0:1], bad1[:], ones_col[:], start=True, stop=True).then_inc(bad_sum, 1)

        @block.scalar
        def _(act):
            act.dma_start(D_i[:], v["dst_pt"]).then_inc(e_in, 16)
            act.dma_start(N_i[:], v["dst_next_pt"]).then_inc(e_in, 16)
            act.dma_start(F_i[:], v["dst_first"].partition_broadcast(P)).then_inc(e_in, 16)
            half = v["dst_row"].rearrange("(g h c) -> h g c", h=2, c=RC)
            with nc.allow_non_contiguous_dma(reason="one word for each half of a group"):
                fg = v["dst_first"][0:TILES].rearrange("(g t) -> g t", t=GT)[:, 0:1]
                for h in range(2):
                    act.dma_start(RB_i[h * GROUPS:(h + 1) * GROUPS, :], fg).then_inc(r_in, 16)
                    act.dma_start(R_i[h * GROUPS:(h + 1) * GROUPS, :], half[h]).then_inc(r_in, 16)
            act.dma_start(v["src_i"][0][:], v["src_pt"][:, 0:GT]).then_inc(s_in, 16)
            for c in range(CHUNKS):
                act.wait_ge(p_mm, c + 1)
                if c >= 2:
                    act.wait_ge(st_p[c % 2], 16 * (c // 2))
                nc.scalar.activation(Pst[c % 2][:], ps_p[c % 2][:, 0:CH, :], ACT.Copy).then_inc(p_out, 1)
            for c in range(CHUNKS + 1):
                if c < CHUNKS:
                    act.wait_ge(qf_out, c + 1)
                    if c >= QR:
                        act.wait_ge(st_q[c % QR], 16 * (c // QR))
                    nc.scalar.activation(Qst[c % QR][:, :, 0, :], qf[c % 2][:], ACT.Copy).then_inc(q1_out, 1)
                if c >= 1:
                    act.wait_ge(r_out, c)
                    nc.scalar.activation(Qst[(c - 1) % QR][:, :, 1, :], qr[(c - 1) % 2][:], ACT.Copy).then_inc(q2_out, 1)
            act.wait_ge(wt, 1)
            nc.scalar.activation(mw2T[:], ps_p[1][:, 0, :], ACT.Copy).then_inc(wt, 1)
            act.wait_ge(wt, 3)
            nc.scalar.activation(v["wagg"][:], ps_p[1][:, 1, :], ACT.Copy)
            nc.scalar.activation(v["bagg"][:], ps_p[1][0:1, 2, :], ACT.Copy)

        @block.vector
        def _(dve):
            n = [0]

            def link(ins):
                n[0] += 1
                ins.then_inc(dv, 1)
                dve.wait_ge(dv, n[0])

            V = nc.vector
            dve.wait_ge(r_in, 64)
            V.tensor_scalar(relR[:], R_i[:], RB_i[:, 0:1], None, ALU.subtract).then_inc(rel_ready, 1)
            dve.wait_ge(e_in, 48)
            F = F_i[:, 0:TILES]
            Fg = F.rearrange("p (g t) -> p g t", t=GT)[:, :, 0:1]
            Fq = F.rearrange("p (q t) -> p q t", t=QT)[:, :, 0:1]
            link(V.tensor_tensor(bad[:], D_i[:], N_i[:], ALU.is_gt))
            link(V.tensor_tensor(rel[:].rearrange("p (g t) -> p g t", t=GT), D_i[:].rearrange("p (g t) -> p g t", t=GT),
                                 Fg.broadcast_to([P, GROUPS, GT]), ALU.subtract))
            link(V.scalar_tensor_tensor(bad[:], rel[:], float(P - 1), bad[:], ALU.is_gt, ALU.add))
            link(V.tensor_tensor(rel[:].rearrange("p (q t) -> p q t", t=QT), D_i[:].rearrange("p (q t) -> p q t", t=QT),
                                 Fq.broadcast_to([P, QUADS, QT]), ALU.subtract))
            relq, badq = (t[:].rearrange("p (q t) -> p q t", t=QT) for t in (rel, bad))
            for j, (w0, w) in enumerate(WIN):
                link(V.scalar_tensor_tensor(badq[:, :, j], relq[:, :, j], float(w0 + w - 1), badq[:, :, j], ALU.is_gt, ALU.add))
                link(V.scalar_tensor_tensor(badq[:, :, j], relq[:, :, j], float(w0), badq[:, :, j], ALU.is_lt, ALU.add))
            link(V.tensor_tensor(rel[:], F_i[:, 1:TILES + 1], F, ALU.is_le))
            link(V.tensor_tensor(bad[:], bad[:], rel[:], ALU.add))
            F1 = F_i[0:1, 0:TILES].rearrange("p (g q t) -> p g q t", q=GQ, t=QT)[:, :, :, 0]
            o3 = orow[:].rearrange("p (g q) -> p g q", q=GQ)
            link(V.tensor_tensor(o3, F1, F1[:, :, 0:1].broadcast_to([1, GROUPS, GQ]), ALU.subtract))
            b1v = bad[0:1, 0:QUADS].rearrange("p (g q) -> p g q", q=GQ)
            step = rel[0:1, 0:QUADS].rearrange("p (g q) -> p g q", q=GQ)
            link(V.tensor_tensor(step[:, :, 1:GQ], o3[:, :, 1:GQ], o3[:, :, 0:GQ - 1], ALU.subtract))
            link(V.scalar_tensor_tensor(b1v[:, :, 1:GQ], step[:, :, 1:GQ], float(W0 - 1), b1v[:, :, 1:GQ], ALU.is_gt, ALU.add))
            lo, lb = o3[:, :, GQ - 1:GQ], b1v[:, :, GQ - 1:GQ]
            link(V.scalar_tensor_tensor(lb, lo, float(LASTQ), lb, ALU.is_gt, ALU.add))
            link(V.scalar_tensor_tensor(lb, lo, float(CLEARED - W0), lb, ALU.is_lt, ALU.add))
            link(V.tensor_scalar(offs[:], orow[:], 0.0, float(LASTQ), ALU.max, ALU.min))
            Fg1 = F_i[0:1, 0:TILES].rearrange("p (g t) -> p g t", t=GT)[:, :, 0]
            link(V.tensor_scalar(gbase[:], Fg1, 0.0, float(NP_ - 1), ALU.max, ALU.min))
            V.reduce_sum(bad1[:], bad[:], AX.X).then_inc(bad_ready, 1)
            dve.wait_ge(b_in, 32)
            for i in range(CHUNKS + 2):
                if i < CHUNKS:
                    dve.wait_ge(q_mm, i + 1)
                    if i >= 2:
                        dve.wait_ge(r_out, i - 1)
                    V.tensor_tensor(qf[i % 2][:], ps_q[i % 2][:, 0:CH, :],
                                    b1bc[:].unsqueeze(1).broadcast_to([P, CH, D]), ALU.add).then_inc(qf_out, 1)
                if 1 <= i <= CHUNKS:
                    c = i - 1
                    dve.wait_ge(q1_out, c + 1)
                    if c >= 2:
                        dve.wait_ge(q3_out, c - 1)
                    V.tensor_tensor(qr[c % 2][:], qf[c % 2][:], Qst[c % QR][:, :, 0, :], ALU.subtract).then_inc(r_out, 1)
                if i >= 2:
                    c = i - 2
                    dve.wait_ge(q2_out, c + 1)
                    V.tensor_tensor(Qst[c % QR][:, :, 2, :], qr[c % 2][:], Qst[c % QR][:, :, 1, :], ALU.subtract).then_inc(q3_out, 1)
            dve.wait_ge(bad_sum, 1)
            V.tensor_scalar(flag[:], ps_p[0][0:1, 0, 0:1], 1.0, None, ALU.min)




def build_edges(nc, ctx, sem, sb, v, force_general):
    flag, offs, gbase = v["flag"], v["offs"], v["gbase"]
    pid, ident, identb, iota, wc = v["pid"], v["ident"], v["identb"], v["iota"], v["wc"]
    sumT, deg = v["sumT"], v["deg"]
    gath, src_i, g_in = v["gath"], v["src_i"], v["g_in"]

    eT = [sb(f"eT{k}", [P, GE]) for k in range(2)]
    dst_i = [sb(f"dst_i{k}", [P, GT], I32) for k in range(2)]
    first_i = [sb(f"first_i{k}", [P, GT], I32) for k in range(2)]
    rel_b = sb("rel_b", [P, GE], BF16)
    nodeE = [sb(f"nodeE{k}", [P, GE], BF16) for k in range(2)]
    Qw = [sb(f"Qw{k}", [P, 3 * D], BF16) for k in range(2)]
    rel_g = [sb(f"rel_g{k}", [P, GT]) for k in range(2)]
    rel_q = sb("rel_q", [P, GT])
    blk_i, low_i = sb("blk_i", [P, GT], I32), sb("low_i", [P, GT], I32)
    key = [sb(f"key{k}", [P, GT]) for k in range(2)]
    low = [sb(f"low{k}", [P, GT]) for k in range(2)]
    edgeN = [sb(f"edgeN{k}", [P, QT, P]) for k in range(2)]
    edgeL = [sb(f"edgeL{k}", [P, QT, P], BF16) for k in range(2)]
    edgeK = [sb(f"edgeK{k}", [P, RCOLS], BF16) for k in range(2)]
    pre = [sb(f"pre{k}", [P, QT * D]) for k in range(2)]
    h = [sb(f"h{k}", [P, QT, D + 2]) for k in range(2)]
    counts = [sb(f"counts{k}", [P, A2, P], BF16) for k in range(2)]
    carry = [sb(f"carry{k}", [P, A2], BF16) for k in range(2)]
    sumS = sb("sumS", [P, SWP])

    ps_pre = [ctx.enter_context(nc.psum_tensor(f"ps_pre{k}", [P, QT * D], F32)) for k in range(2)]
    ps_cnt = [ctx.enter_context(nc.psum_tensor(f"ps_cnt{k}", [P, 2, 512], F32)) for k in range(2)]
    ps_sum = [ctx.enter_context(nc.psum_tensor(f"ps_sum{k}", [P, 512], F32)) for k in range(2)]
    TR = 2 * P

    e_in = [sem(f"e_in{k}") for k in range(2)]
    i_in = [sem(f"i_in{k}") for k in range(2)]
    s_in = [sem(f"s_in{k}") for k in range(2)]
    r_in = sem("r_in")
    q_in = [sem(f"q_in{k}") for k in range(2)]
    c_out = [sem(f"c_out{k}") for k in range(2)]
    prepared = sem("prepared")
    onehots = sem("onehots")
    pre_mm, cnt_mm, sum_mm = sem("pre_mm"), sem("cnt_mm"), sem("sum_mm")
    pre_add, silu, cnt_copy = sem("pre_add"), sem("silu"), sem("cnt_copy")
    carried = sem("carried")
    sum_copy, sum_tr, sum_add = sem("sum_copy"), sem("sum_tr"), sem("sum_add")
    dv = sem("dv")
    h_ones = sem("h_ones")
    gen = general_path(nc, ctx, sem, sb, v, 0, eT[0], ps_pre[0], ps_sum[0])

    def loop(eng, first, group, last):
        first()
        with eng.Fori(0, (GROUPS - 2) // 2) as i:
            group(i, 1)
            group(i + 1, 0)
        last()

    with nc.Block() as block:
        @block.sync
        def _(sp):
            def load(g, k):
                if type(g) is not int or g > 0:
                    sp.dma_start(src_i[k][:], v["src_pt"][:, bass.ds(g * GT, GT)]).then_inc(s_in[k], 16)
                sp.dma_start(dst_i[k][:], v["dst_pt"][:, bass.ds(g * GT, GT)]).then_inc(i_in[k], 16)
                sp.dma_start(first_i[k][:], v["dst_first"][bass.ds(g * GT, GT)].partition_broadcast(P)).then_inc(i_in[k], 16)
                base = sp.value_load(gbase[0:1, bass.ds(g, 1)], min_val=0, max_val=NP_ - 1)
                sp.dma_start(Qw[k][:], v["Q_d"][bass.ds(base, P), :]).then_inc(q_in[k], 16)
                sp.dma_start(eT[k][:], v["eT"][:, bass.ds(g * GE, GE)]).then_inc(e_in[k], 16)

            def load_rel(g):
                sp.dma_start(rel_b[:], v["rel_d"][bass.ds(g * GE, GE)].partition_broadcast(P)).then_inc(r_in, 16)

            def store(g, k):
                sp.wait_ge(cnt_copy, g * GQ + GQ)
                sp.dma_start(v["A_d"][bass.ds(g, 1), :, :].rearrange("a p c -> (a p) c"),
                             counts[k][:, 0:NB, :].rearrange("p a d -> p (a d)")).then_inc(c_out[k], 16)

            def fast():
                load(0, 0)
                load_rel(0)
                load(1, 1)
                sp.wait_ge(prepared, 1)
                load_rel(1)
                with sp.Fori(0, (GROUPS - 2) // 2) as i:
                    for k in range(2):
                        g = 2 * i + k
                        sp.wait_ge(prepared, g + 2)
                        load_rel(g + 2)
                        sp.wait_ge(sum_mm, g * GQ + GQ)
                        load(g + 2, k)
                        store(g, k)
                for g in (GROUPS - 2, GROUPS - 1):
                    store(g, g % 2)
                for k in range(2):
                    sp.wait_ge(c_out[k], 16 * (GROUPS // 2))

            fork(sp, flag, fast, gen["sync"], force_general)

        @block.gpsimd
        def _(pool):
            turn = sem("turn")

            def group(half, k):
                g = 2 * half + k
                pool.wait_ge(s_in[k], 16 * (half + k))
                pool.sem_inc(turn, 1)
                for q in range(GQ):
                    pool.wait_ge(pre_add, (g - 1) * GQ + q + 1)
                    pool.sem_inc(turn, 1)
                    for t in range(QT):
                        c = q * QT + t
                        pool.indirect_dma_start(
                            gath[:, q, t * D:(t + 1) * D], None, v["P_d"],
                            bass.IndirectOffsetOnAxis(ap=src_i[k][:, c:c + 1], axis=0)).then_inc(g_in[q], 16)

            def fast():
                loop(pool, lambda: None, group, lambda: group(GROUPS // 2 - 1, 1))

            fork(pool, flag, fast, gen["gpsimd"], force_general)

        @block.vector
        def _(dve):
            V = nc.vector
            def make_keys(half, k, first=False):
                g = 2 * half + k
                if not (first and k == 0):
                    dve.wait_ge(s_in[k], 16 * (half + k))
                dve.wait_ge(i_in[k], 32 * (half + 1))
                D3 = dst_i[k][:]
                Fg = first_i[k][:, 0:1].broadcast_to([P, GT])
                Fq = first_i[k][:].rearrange("p (q t) -> p q t", t=QT)[:, :, 0:1].broadcast_to([P, GQ, QT])
                V.tensor_tensor(rel_g[k][:], D3, Fg, ALU.subtract)
                V.tensor_tensor(rel_q[:].rearrange("p (q t) -> p q t", t=QT), D3.rearrange("p (q t) -> p q t", t=QT),
                                Fq, ALU.subtract)
                V.tensor_scalar(blk_i[:], src_i[k][:], 7, None, ALU.arith_shift_right)
                V.tensor_scalar(low_i[:], src_i[k][:], P - 1, None, ALU.bitwise_and).then_inc(dv, 1)
                dve.wait_ge(dv, g + 1)
                V.tensor_copy(low[k][:], low_i[:])
                kq, bq, rq = (t[:].rearrange("p (q t) -> p q t", t=QT) for t in (key[k], blk_i, rel_q))
                for j, (w0, w) in enumerate(WIN):
                    V.scalar_tensor_tensor(kq[:, :, j], bq[:, :, j], float(w), rq[:, :, j], ALU.mult, ALU.add)

            def expand(k, cols):
                return V.tensor_scalar(nodeE[k][:, cols], rel_b[:, cols], pid[:, 0:1], None, ALU.is_equal)

            def expand_first(half, k, early=False):
                g = 2 * half + k
                if not early:
                    dve.wait_ge(pre_mm, (g - 1) * GQ)
                dve.wait_ge(r_in, 16 * (g + 1))
                expand(k, slice(0, GE // 2))

            def expand_rest(half, k, early=False):
                expand(k, slice(GE // 2, GE))
                if not early:
                    dve.wait_ge(c_out[k], 16 * half)
                V.memset(counts[k][:, :, CLEARED:P], 0.0).then_inc(prepared, 1)

            def hots(s, q, k, first=False):
                x = (k + q) % 2
                if not first:
                    dve.wait_ge(sum_mm, s - 1)
                    dve.wait_ge(cnt_mm, s - 1)
                c = slice(q * QT, (q + 1) * QT)
                io = iota[:, 0:P].unsqueeze(1).broadcast_to([P, QT, P])
                V.tensor_tensor(edgeN[x][:], io, rel_g[k][:, c].unsqueeze(2).broadcast_to([P, QT, P]), ALU.is_equal)
                V.tensor_tensor(edgeL[x][:], io, low[k][:, c].unsqueeze(2).broadcast_to([P, QT, P]), ALU.is_equal)
                for j, (w0, w) in enumerate(WIN):
                    last = V.tensor_scalar(edgeK[x][:, ROFF[j]:ROFF[j] + A2 * w], iota[:, w0:w0 + A2 * w],
                                           key[k][:, q * QT + j:q * QT + j + 1], None, ALU.is_equal)
                last.then_inc(onehots, 1)

            def add(s, q, k, g, first=False):
                x = (k + q) % 2
                dve.wait_ge(pre_mm, s + 1)
                dve.wait_ge(g_in[q], 16 * QT * (g + 1))
                if not first:
                    dve.wait_ge(silu, s - 1)
                V.tensor_tensor(pre[x][:], ps_pre[x][:], gath[:, q, :], ALU.add).then_inc(pre_add, 1)

            def add_sums(g, k):
                dve.wait_ge(sum_tr, g + 2)
                dve.wait_ge(sum_add, g + 1)
                base = dve.value_load(gbase[0:1, bass.ds(g, 1)], min_val=0, max_val=NP_ - 1)
                V.tensor_tensor(sumT[:, bass.ds(base, P)], ps_sum[k][:, TR:TR + P], sumT[:, bass.ds(base, P)], ALU.add)
                V.tensor_tensor(deg[0:1, bass.ds(base, P)], ps_sum[k][0:1, TR + P:TR + 2 * P], deg[0:1, bass.ds(base, P)],
                                ALU.add).then_inc(sum_add, 1)

            def group(half, k, first=False, last=False):
                g = 2 * half + k
                nxt = (half, 1) if k == 0 else (half + 1, 0)
                for q in range(GQ):
                    s = g * GQ + q
                    add(s, q, k, g, first and q < 2)
                    if q < GQ - 1:
                        hots(s + 1, q + 1, k, first and q == 0)
                    elif not last:
                        dve.wait_ge(prepared, g + 2)
                        hots(s + 1, 0, 1 - k)
                    if not last and q in (2, 3, 4):
                        if q == 2:
                            make_keys(*nxt)
                        else:
                            (expand_first, expand_rest)[q - 3](*nxt, early=first)
                    if q == 5 and not first:
                        add_sums(g - 1, 1 - k)

            def fast():
                for k in range(2):
                    V.memset(h[k][:, :, D:D + 2], 1.0).then_inc(h_ones, 1)
                dve.sem_inc(sum_add, 1)
                make_keys(0, 0, first=True)
                expand_first(0, 0, early=True)
                expand_rest(0, 0, early=True)
                dve.wait_ge(prepared, 1)
                hots(0, 0, 0, True)
                loop(dve, lambda: group(0, 0, first=True), group, lambda: group(GROUPS // 2 - 1, 1, last=True))
                add_sums(GROUPS - 1, 1)

            fork(dve, flag, fast, gen["vector"], force_general)

        @block.tensor
        def _(pe):
            T = nc.tensor

            def products(s, q, k, half, first=False):
                x = (k + q) % 2
                if q == 0:
                    pe.wait_ge(e_in[k], 16 * (half + 1))
                    pe.wait_ge(q_in[k], 16 * (half + 1))
                    pe.wait_ge(prepared, 2 * half + k + 1)
                if not first:
                    pe.wait_ge(pre_add, s - 1)
                for t in range(QT):
                    e0 = (q * QT + t) * P
                    o = ps_pre[x][:, t * D:(t + 1) * D]
                    T.matmul(o, eT[k][:, e0:e0 + P], wc[:], start=True, stop=False)
                    for part in range(3):
                        last = T.matmul(o, nodeE[k][:, e0:e0 + P], Qw[k][:, part * D:(part + 1) * D],
                                        start=False, stop=(part == 2))
                last.then_inc(pre_mm, 1)

            def count(s, q, k, g, first=False):
                x = (k + q) % 2
                pe.wait_ge(onehots, s + 1)
                if not first:
                    pe.wait_ge(cnt_copy, s - 1)
                for b in range(2):
                    o = ps_cnt[x][:, b, 0:AB * W0].rearrange("p (a d) -> p a d", d=W0)
                    for j, (w0, w) in enumerate(WIN):
                        r = edgeK[x][:, ROFF[j] + b * AB * w:ROFF[j] + (b + 1) * AB * w].rearrange("p (a d) -> p a d", d=w)
                        last = T.matmul(o[:, :, w0:w0 + w], edgeL[x][:, j, :], r, start=(j == 0),
                                        stop=(j == QT - 1 and q == 0))
                if q > 0:
                    pe.wait_ge(carried, g * (GQ - 1) + q)
                    for b in range(2):
                        o = ps_cnt[x][:, b, 0:AB * W0].rearrange("p (a d) -> p a d", d=W0)
                        last = T.matmul(o[:, :, 0:1], identb[:], carry[x][:, b * AB:(b + 1) * AB].unsqueeze(2),
                                        start=False, stop=True)
                last.then_inc(cnt_mm, 1)

            def sums(s, q, k, g, first=False):
                x = (k + q) % 2
                pe.wait_ge(silu, s + 1)
                if q == 0 and not first:
                    pe.wait_ge(sum_add, g)
                for t in range(QT):
                    last = T.matmul(ps_sum[k][:, 0:SW], edgeN[x][:, t, :], h[x][:, t, 0:SW],
                                    start=(q == 0 and t == 0), stop=(q == GQ - 1 and t == QT - 1))
                last.then_inc(sum_mm, 1)

            def transpose_sums(g, k):
                pe.wait_ge(sum_copy, g + 1)
                T.matmul(ps_sum[k][:, TR:TR + P], sumS[:, 0:D], ident[:], is_transpose=True, start=True, stop=True)
                T.matmul(ps_sum[k][0:1, TR + P:TR + 2 * P], sumS[:, D:SW], ident[:], start=True, stop=True).then_inc(sum_tr, 1)

            def group(half, k, first=False, last=False, second=False):
                g = 2 * half + k
                for q in range(GQ):
                    s = g * GQ + q
                    if q < GQ - 1:
                        products(s + 1, q + 1, k, half, first and q == 0)
                    elif not last:
                        half1, k1 = (half, 1) if k == 0 else (half + 1, 0)
                        products(s + 1, 0, k1, half1)
                    sums(s, q, k, g, first)
                    if q < GQ - 1:
                        count(s + 1, q + 1, k, g, first and q == 0)
                    elif not last:
                        count(s + 1, 0, k1, g + 1)
                    if q == 1 and not first:
                        transpose_sums(g - 1, 1 - k)

            def fast():
                pe.sem_inc(sum_tr, 1)
                pe.wait_ge(h_ones, 2)
                products(0, 0, 0, 0, True)
                count(0, 0, 0, 0, True)
                loop(pe, lambda: group(0, 0, first=True), group, lambda: group(GROUPS // 2 - 1, 1, last=True))
                transpose_sums(GROUPS - 1, 1)

            fork(pe, flag, fast, gen["tensor"], force_general)

        @block.scalar
        def _(act):
            A = nc.scalar

            act_turn = sem("act_turn")

            def copy_counts(s, q, k, g, off, off_next):
                x = (k + q) % 2
                if q == 0:
                    act.wait_ge(prepared, g + 1)
                act.wait_ge(cnt_mm, s + 1)
                act.sem_inc(act_turn, 1)
                A.activation(counts[k][:].rearrange("p (b a) d -> p b a d", b=2)[:, :, :, bass.ds(off, W0)],
                             ps_cnt[x][:, :, 0:AB * W0].rearrange("p b (a d) -> p b a d", d=W0),
                             ACT.Copy).then_inc(cnt_copy, 1)
                if q < GQ - 1:
                    act.wait_ge(cnt_copy, s + 1)
                    act.sem_inc(act_turn, 1)
                    A.activation(carry[1 - x][:].unsqueeze(2), counts[k][:, :, bass.ds(off_next, 1)],
                                 ACT.Copy).then_inc(carried, 1)

            def activate(s, q, k, first):
                x = (k + q) % 2
                act.wait_ge(pre_add, s + 1)
                if not first:
                    act.wait_ge(sum_mm, s - 1)
                A.activation(h[x][:, :, 0:D], pre[x][:].rearrange("p (t n) -> p t n", n=D), ACT.Silu).then_inc(silu, 1)

            def copy_sums(g, k, first):
                act.wait_ge(sum_mm, (g + 1) * GQ)
                if not first:
                    act.wait_ge(sum_tr, g + 1)
                A.activation(sumS[:, 0:SW], ps_sum[k][:, 0:SW], ACT.Copy).then_inc(sum_copy, 1)

            def group(half, k, first=False, last=False):
                g = 2 * half + k
                off = [0] + [act.value_load(offs[0:1, bass.ds(g * GQ + q, 1)], min_val=0, max_val=LASTQ)
                             for q in range(1, GQ)]
                for q in range(GQ):
                    s = g * GQ + q
                    activate(s, q, k, first and q < 2)
                    copy_counts(s, q, k, g, off[q], off[q + 1] if q < GQ - 1 else None)
                    if q == 1 and not first:
                        copy_sums(g - 1, 1 - k, False)

            def fast():
                act.wait_ge(h_ones, 2)
                loop(act, lambda: group(0, 0, first=True), group, lambda: group(GROUPS // 2 - 1, 1, last=True))
                copy_sums(GROUPS - 1, 1, False)

            fork(act, flag, fast, gen["scalar"], force_general)


def fork(eng, flag, fast, general, force_general):
    bad = eng.value_load(flag[0:1, 0:1], min_val=0, max_val=1)
    if force_general is None:
        fast()
        return
    with eng.If(bad == (2 if force_general else 0)):
        fast()
    with eng.Else():
        general(eng)


def general_path(nc, ctx, sem, sb, v, layer, e_buf, ps_a, ps_b):
    ident, wc, acc_d = v["ident"], v["wc"], v["acc_d"]
    L = f"{layer}"
    src_c, dst_c = sb("g_src" + L, [P, 1], I32), sb("g_dst" + L, [P, 1], I32)
    dst_r = sb("g_dst_r" + L, [P, P], I32)
    same = sb("g_same" + L, [P, P])
    before = sb("g_before" + L, [P, P])
    tmp = sb("g_tmp" + L, [P, P])
    dup = sb("g_dup" + L, [P, 1])
    row_to = sb("g_row_to" + L, [P, 1], I32)
    dst_f = sb("g_dst_f" + L, [P, 1])
    rows = sb("g_rows" + L, [P, D])
    q_rows = sb("g_q_rows" + L, [P, 3 * D], BF16)
    old = sb("g_old" + L, [P, SWP])
    new = sb("g_new" + L, [P, SWP])
    hm = sb("g_h" + L, [P, SWP])
    back = sb("g_back" + L, [P, SWP])
    ld = {n: sem(f"g_ld_{n}" + L) for n in ("e", "src", "dst", "dsts")}
    ga = {n: sem(f"g_ga_{n}" + L) for n in ("rows", "q", "old")}
    zr, pm, vm, sm, sc, mk, bk, bt, bc = (sem(f"g_{n}" + L) for n in (
        "zr", "pm", "vm", "sm", "sc", "mk", "bk", "bt", "bc"))
    turn, done = sem("g_turn" + L), sem("g_done" + L)
    DVE_STEPS = 7

    def sync(sp):
        sp.wait_ge(mk, 1)
        for b in range(NW // P):
            sp.dma_start(acc_d[b * P:(b + 1) * P, :], new[:]).then_inc(zr, 16)
        if layer == 1:
            sp.dma_start(v["x1_d"].rearrange("(j p) n -> p j n", p=P), v["x1"][:]).then_inc(zr, 16)
        sp.wait_ge(zr, 16 * (NW // P + layer))
        with sp.Fori(0, TILES) as t:
            sp.wait_ge(done, t + 1)
            if layer == 0:
                sp.dma_start(e_buf[:, 0:P], v["eT"][:, bass.ds(t * P, P)]).then_inc(ld["e"], 16)
            with nc.allow_non_contiguous_dma(reason="one index for each partition"):
                sp.dma_start(src_c[:], v["src_row"][bass.ds(t * P, P)].rearrange("(p a) -> p a", a=1)).then_inc(ld["src"], 16)
                sp.dma_start(dst_c[:], v["dst_row"][bass.ds(t * P, P)].rearrange("(p a) -> p a", a=1)).then_inc(ld["dst"], 16)
            sp.dma_start(dst_r[:], v["dst_row"][bass.ds(t * P, P)].partition_broadcast(P)).then_inc(ld["dsts"], 16)
        sp.wait_ge(done, TILES + 1)
        with sp.Fori(0, NB) as b:
            sp.wait_ge(bc, b + 1)
            sp.dma_start(back[:], acc_d[bass.ds(b * P, P), :]).then_inc(bk, 16)

    def gpsimd(pool):
        pool.memset(new[:], 0.0)
        pool.memset(hm[:], 1.0)
        pool.memset(before[:], 0.0).then_inc(mk, 1)
        pool.wait_ge(mk, 1)
        pool.affine_select(out=before[:], in_=before[:], compare_op=ALU.is_ge, fill=1.0, base=0,
                           pattern=[[1, P]], channel_multiplier=-1).then_inc(mk, 1)
        table = v["P_d"] if layer == 0 else v["x1_d"]
        at = lambda c: bass.IndirectOffsetOnAxis(ap=c, axis=0)
        pool.wait_ge(zr, 16 * (NW // P + layer))
        pool.sem_inc(done, 1)
        with pool.Fori(0, TILES) as t:
            pool.wait_ge(ld["src"], 16 * (t + 1))
            pool.wait_ge(ld["dst"], 16 * (t + 1))
            pool.sem_inc(turn, 1)
            if layer == 0:
                pool.indirect_dma_start(rows[:], None, table, at(src_c[:, 0:1])).then_inc(ga["rows"], 16)
                pool.indirect_dma_start(q_rows[:], None, v["Q_d"], at(dst_c[:, 0:1])).then_inc(ga["q"], 16)
            else:
                pool.indirect_dma_start(hm[:, 0:D], None, table, at(src_c[:, 0:1])).then_inc(ga["rows"], 16)
            pool.indirect_dma_start(old[:], None, acc_d, at(dst_c[:, 0:1])).then_inc(ga["old"], 16)
            pool.wait_ge(vm, DVE_STEPS * (t + 1))
            pool.sem_inc(turn, 1)
            pool.indirect_dma_start(acc_d, at(row_to[:, 0:1]), new[:], None,
                                    bounds_check=NW - 1, oob_is_err=False).then_inc(sc, 16)
            pool.wait_ge(sc, 16 * (t + 1))
            pool.sem_inc(done, 1)

    def vector(dve):
        V = nc.vector

        dve.wait_ge(mk, 2)
        with dve.Fori(0, TILES) as t:
            k = [0]

            def link(ins):
                k[0] += 1
                ins.then_inc(vm, 1)
                dve.wait_ge(vm, DVE_STEPS * t + k[0])
            dve.wait_ge(ld["dst"], 16 * (t + 1))
            dve.wait_ge(ld["dsts"], 16 * (t + 1))
            dve.wait_ge(done, t + 1)
            link(V.tensor_copy(dst_f[:], dst_c[:]))
            link(V.tensor_scalar(same[:], dst_r[:], dst_f[:, 0:1], None, ALU.is_equal))
            link(V.tensor_tensor(tmp[:], same[:], before[:], ALU.mult))
            link(V.reduce_sum(dup[:], tmp[:], AX.X))
            link(V.tensor_scalar(dup[:], dup[:], 1.0, float(SKIP), ALU.min, ALU.mult))
            link(V.tensor_tensor(row_to[:], dup[:], dst_f[:], ALU.add))
            dve.wait_ge(ga["old"], 16 * (t + 1))
            if layer == 0:
                dve.wait_ge(ga["rows"], 16 * (t + 1))
                dve.wait_ge(ga["q"], 16 * (t + 1))
                dve.wait_ge(pm, 2 * t + 1)
                V.tensor_tensor(tmp[:], ps_a[:, 0:D], rows[:], ALU.add).then_inc(sm, 1)
                for part in range(3):
                    dve.wait_ge(sm, 4 * t + part + 1)
                    V.tensor_tensor(tmp[:], tmp[:], q_rows[:, part * D:(part + 1) * D], ALU.add).then_inc(sm, 1)
                dve.wait_ge(pm, 2 * t + 2)
            else:
                dve.wait_ge(pm, t + 1)
            V.tensor_tensor(new[:, 0:SW], ps_b[:, 0:SW], old[:, 0:SW], ALU.add).then_inc(vm, 1)

    def scalar(act):
        act.sem_inc(bc, 1)
        if layer == 0:
            with act.Fori(0, TILES) as t:
                act.wait_ge(sm, 4 * t + 4)
                nc.scalar.activation(hm[:, 0:D], tmp[:], ACT.Silu).then_inc(bt, 1)
        with act.Fori(0, NB) as b:
            act.wait_ge(pm, (2 - layer) * TILES + b + 1)
            last = nc.scalar.activation(v["sumT"][:, bass.ds(b * P, P)], ps_a[:, 0:P], ACT.Copy)
            if layer == 0:
                last = nc.scalar.activation(v["deg"][0:1, bass.ds(b * P, P)], ps_a[0:1, P:2 * P], ACT.Copy)
            last.then_inc(bc, 1)

    def tensor(pe):
        T = nc.tensor
        with pe.Fori(0, TILES) as t:
            if layer == 0:
                pe.wait_ge(ld["e"], 16 * (t + 1))
                T.matmul(ps_a[:, 0:D], e_buf[:, 0:P], wc[:], start=True, stop=True).then_inc(pm, 1)
                pe.wait_ge(bt, t + 1)
            else:
                pe.wait_ge(ga["rows"], 16 * (t + 1))
            pe.wait_ge(vm, DVE_STEPS * t + DVE_STEPS - 1)
            T.matmul(ps_b[:, 0:SW], same[:], hm[:, 0:SW], start=True, stop=True).then_inc(pm, 1)
        with pe.Fori(0, NB) as b:
            pe.wait_ge(bk, 16 * (b + 1))
            T.matmul(ps_a[:, 0:P], back[:, 0:D], ident[:], is_transpose=True, start=True, stop=True)
            T.matmul(ps_a[0:1, P:2 * P], back[:, D:SW], ident[:], start=True, stop=True).then_inc(pm, 1)
            pe.wait_ge(bc, b + 2)

    return dict(sync=sync, gpsimd=gpsimd, vector=vector, scalar=scalar, tensor=tensor)


def build_nodes(nc, ctx, sem, sb, v):
    x1 = sb("x1", [P, NB, D])
    x1T = sb("x1T", [P, NP_])
    x1h = sb("x1h", [P, NB, 2, D], F16)
    w1, w2 = sb("l1_w1", [P, 2, D]), sb("l1_w2", [P, D])
    b1, b2bc = sb("l1_b1", [P, 1]), sb("l1_b2", [P, D])
    l1_in, rdeg_in = sem("l1_in"), sem("rdeg_in")
    v = dict(v, x1=x1, x1T=x1T, x1h=x1h, w1=w1, w2=w2, b1_sb=b1, b2bc=b2bc, l1_in=l1_in, rdeg_in=rdeg_in)
    with ExitStack() as c:
        update_0(nc, c, lambda n: c.enter_context(nc.semaphore(n)),
                 lambda n, s, d=F32: c.enter_context(nc.sbuf_tensor("u0_" + n, s, d)), v)
    with ExitStack() as c:
        sums_1(nc, c, lambda n: c.enter_context(nc.semaphore(n)),
               lambda n, s, d=F32: c.enter_context(nc.sbuf_tensor(n, s, d)), v)
    with ExitStack() as c:
        update_1(nc, c, lambda n: c.enter_context(nc.semaphore(n)),
                 lambda n, s, d=F32: c.enter_context(nc.sbuf_tensor(n, s, d)), v)


def blocks(c):
    return slice(c * CH, (c + 1) * CH)


def load_chunk(ap, c):
    return ap[c * CN:(c + 1) * CN, :].rearrange("(j p) n -> p j n", p=P)


def row_stats(V, link, z, st, mv, c):
    for j in range(c * CH, (c + 1) * CH):
        last = V.bn_stats(st[:, j % CH, :], z[:, j, :])
    link(last)
    for j in range(c * CH, (c + 1) * CH):
        last = V.bn_aggr(mv[:, j, :], st[:, j % CH, :])
    return last


def root(nc, sd, mv, eps_col, c):
    return nc.scalar.activation(sd[:, blocks(c)], mv[:, blocks(c), 1], ACT.Sqrt, bias=eps_col[:, 0:1])


def scale_shift(V, link, sd, mv, rs, shift, c):
    link(V.reciprocal(rs[:, blocks(c)], sd[:, blocks(c)]))
    return V.scalar_tensor_tensor(shift[:, blocks(c)], mv[:, blocks(c), 0], -1.0, rs[:, blocks(c)], ALU.mult, ALU.mult)


def update_0(nc, ctx, sem, sb, v):
    sumT, deg, ident = v["sumT"], v["deg"], v["ident"]
    x1, x1T, x1h = v["x1"], v["x1T"], v["x1h"]
    u1a, wagg, bagg, u2, ub1, ub2bc, gbc, bbc = (v[n] for n in ("u1a", "wagg", "bagg", "u2", "ub1_sb", "ub2bc", "gbc", "bbc"))
    R, RB = 3, 4
    xT_c = [sb(f"xT_c{i}", [P, CN]) for i in range(2)]
    x_c = [sb(f"x_c{i}", [P, CH, D]) for i in range(R)]
    xbeta = [sb(f"xbeta{i}", [P, CH, D]) for i in range(RB)]
    hT_c = [sb(f"hT_c{i}", [P, 2, HN]) for i in range(2)]
    z = x1
    st = sb("st", [P, CH, 6])
    mv = [sb(f"mv{i}", [P, NB, 2]) for i in range(2)]
    sd = [sb(f"sd{i}", [P, NB]) for i in range(2)]
    rs = [sb(f"rs{i}", [P, NB]) for i in range(2)]
    shift = sb("shift", [P, NB])
    eps_col = v["eps_col"]
    dg = sb("dg", [P, NB])
    ps_h, ps_y, ps_t = ([ctx.enter_context(nc.psum_tensor(f"u0_{n}{i}", [P, 2, 512], F32)) for i in range(m)]
                        for n, m in (("h", 2), ("y", 1), ("t", 1)))
    ps_y, ps_t = ps_y[0], ps_t[0]
    x_in = [sem(f"u0_x_in{i}") for i in range(R)]
    xT_in = [sem(f"u0_xT_in{i}") for i in range(2)]
    h_mm, h_act, y_mm, z_add, x_ready, norm1, scaled, added = (
        sem(f"u0_{n}") for n in ("h_mm", "h_act", "y_mm", "z_add", "x_ready", "norm1", "scaled", "added"))
    var_ok, sd_ok = ([sem(f"u0_{n}{i}") for i in range(2)] for n in ("var_ok", "sd_ok"))
    stat1, x_norm, x_hi, x_lo, t_mm, t_cp, dv, dg_io, dg_ready = (
        sem(f"u0_{n}") for n in ("stat1", "x_norm", "x_hi", "x_lo", "t_mm", "t_cp", "dv", "dg_io", "dg_ready"))

    with nc.Block() as block:
        @block.sync
        def _(sp):
            for c in range(CHUNKS):
                if c >= 2:
                    sp.wait_ge(h_mm, c - 1)
                sp.dma_start(xT_c[c % 2][:], v["xT"][:, c * CN:(c + 1) * CN]).then_inc(xT_in[c % 2], 16)
                if c >= R:
                    sp.wait_ge(z_add, c - R + 1)
                    sp.wait_ge(x_ready, c - R + 1)
                sp.dma_start(x_c[c % R][:], load_chunk(v["x_nm"], c)).then_inc(x_in[c % R], 16)
                if c == 2:
                    sp.dma_start(v["deg_d"].rearrange("(a n) -> a n", a=1), deg[0:1, 0:NP_]).then_inc(dg_io, 16)
                    sp.wait_ge(dg_io, 16)
                    sp.dma_start(dg[:], v["deg_d"].rearrange("(p j) -> p j", j=NB)).then_inc(dg_io, 16)
                    sp.dma_start(v["w1"][:], v["W1"].rearrange("(c k) n -> k c n", c=2)).then_inc(v["l1_in"], 16)
                    sp.dma_start(v["w2"][:], v["W2"]).then_inc(v["l1_in"], 16)
                    with nc.allow_non_contiguous_dma(reason="one word for each partition"):
                        sp.dma_start(v["b1_sb"][:], v["b1"].rearrange("(n a) -> n a", a=1)).then_inc(v["l1_in"], 16)
                    sp.dma_start(v["b2bc"][:], v["b2"].partition_broadcast(P)).then_inc(v["l1_in"], 16)
            sp.wait_ge(dg_ready, 1)
            sp.dma_start(v["rdeg_d"].rearrange("(p j) -> p j", j=NB), dg[:]).then_inc(dg_io, 16)
            sp.wait_ge(dg_io, 48)
            sp.wait_ge(h_mm, CHUNKS)
            sp.dma_start(deg[:, 0:NP_], v["rdeg_d"].partition_broadcast(P)).then_inc(v["rdeg_in"], 16)

        @block.tensor
        def _(pe):
            T = nc.tensor

            def hidden(c):
                if c >= 2:
                    pe.wait_ge(h_act, c - 1)
                cols = [slice(c * CN + i * HN, c * CN + (i + 1) * HN) for i in range(2)]
                for i in range(2):
                    T.matmul(ps_h[c % 2][:, i, 0:HN], wagg[:], sumT[:, cols[i]], start=True, stop=False)
                    T.matmul(ps_h[c % 2][:, i, 0:HN], bagg[:], deg[0:1, cols[i]], start=False, stop=False)
                pe.wait_ge(xT_in[c % 2], 16 * (c // 2 + 1))
                for i in range(2):
                    last = T.matmul(ps_h[c % 2][:, i, 0:HN], u1a[:], xT_c[c % 2][:, i * HN:(i + 1) * HN], start=False, stop=True)
                last.then_inc(h_mm, 1)

            def output(c):
                pe.wait_ge(h_act, c + 1)
                if c >= 1:
                    pe.wait_ge(z_add, c)
                for j in range(CH):
                    last = T.matmul(ps_y[:, j // 4, (j % 4) * D:(j % 4 + 1) * D],
                                    hT_c[c % 2][:].rearrange("p i n -> p (i n)")[:, j * P:(j + 1) * P], u2[:],
                                    start=True, stop=True)
                last.then_inc(y_mm, 1)

            def transpose(c):
                pe.wait_ge(x_norm, c + 1)
                if c >= 1:
                    pe.wait_ge(t_cp, c)
                for j in range(CH):
                    last = T.matmul(ps_t[:, j // 4, (j % 4) * D:(j % 4 + 1) * D], x1[:, c * CH + j, :], ident[:],
                                    is_transpose=True, start=True, stop=True)
                last.then_inc(t_mm, 1)

            hidden(0)
            for i in range(CHUNKS + 4):
                if i + 1 < CHUNKS:
                    hidden(i + 1)
                if i < CHUNKS:
                    output(i)
                if i >= 4:
                    transpose(i - 4)

        @block.scalar
        def _(act):
            A = nc.scalar
            for i in range(CHUNKS + 4):
                if i < CHUNKS:
                    act.wait_ge(h_mm, i + 1)
                    if i >= 2:
                        act.wait_ge(y_mm, i - 1)
                    A.activation(hT_c[i % 2][:], ps_h[i % 2][:, :, 0:HN], ACT.Silu, bias=ub1[:, 0:1]).then_inc(h_act, 1)
                if 3 <= i < CHUNKS + 3:
                    act.wait_ge(var_ok[1], i - 2)
                    root(nc, sd[1], mv[1], eps_col, i - 3).then_inc(sd_ok[1], 1)
                if 1 <= i <= CHUNKS:
                    c = i - 1
                    act.wait_ge(stat1, c + 1)
                    for j in range(c * CH, (c + 1) * CH):
                        last = A.activation(z[:, j, :], z[:, j, :], ACT.Identity, scale=rs[0][:, j:j + 1], bias=shift[:, j:j + 1])
                    last.then_inc(norm1, 1)
                if i >= 4:
                    c = i - 4
                    act.wait_ge(x_norm, c + 1)
                    A.activation(x1h[:, blocks(c), 0, :], x1[:, blocks(c), :], ACT.Copy).then_inc(x_hi, 1)
                    act.wait_ge(t_mm, c + 1)
                    A.activation(x1T[:, c * CN:c * CN + 4 * P], ps_t[:, 0, :], ACT.Copy)
                    A.activation(x1T[:, c * CN + 4 * P:(c + 1) * CN], ps_t[:, 1, 0:3 * P], ACT.Copy).then_inc(t_cp, 1)
                if i < CHUNKS:
                    act.wait_ge(var_ok[0], i + 1)
                    root(nc, sd[0], mv[0], eps_col, i).then_inc(sd_ok[0], 1)

        @block.gpsimd
        def _(pool):
            G = nc.gpsimd

            def bc(t):
                return t[:].unsqueeze(1).broadcast_to([P, CH, D])

            for i in range(CHUNKS + 4):
                if i < CHUNKS:
                    pool.wait_ge(x_in[i % R], 16 * (i // R + 1))
                    if i >= RB:
                        pool.wait_ge(added, i - RB + 1)
                    G.tensor_tensor(xbeta[i % RB][:], x_c[i % R][:], bc(bbc), ALU.add)
                    G.tensor_tensor(x_c[i % R][:], x_c[i % R][:], bc(ub2bc), ALU.add).then_inc(x_ready, 1)
                if 1 <= i <= CHUNKS:
                    c = i - 1
                    pool.wait_ge(norm1, c + 1)
                    G.tensor_tensor(z[:, blocks(c), :], z[:, blocks(c), :], bc(gbc), ALU.mult).then_inc(scaled, 1)
                if i >= 4:
                    c = i - 4
                    pool.wait_ge(x_hi, c + 1)
                    G.tensor_tensor(x1h[:, blocks(c), 1, :], x1[:, blocks(c), :], x1h[:, blocks(c), 0, :], ALU.subtract).then_inc(x_lo, 1)

        @block.vector
        def _(dve):
            V = nc.vector
            n = [0]

            def link(ins):
                n[0] += 1
                ins.then_inc(dv, 1)
                dve.wait_ge(dv, n[0])

            for i in range(CHUNKS + 3):
                if 1 <= i <= CHUNKS:
                    dve.wait_ge(sd_ok[0], i)
                    scale_shift(V, link, sd[0], mv[0], rs[0], shift, i - 1).then_inc(stat1, 1)
                if i < CHUNKS:
                    dve.wait_ge(x_ready, i + 1)
                    dve.wait_ge(y_mm, i + 1)
                    V.tensor_tensor(z[:, i * CH:i * CH + 4, :], ps_y[:, 0, :].rearrange("p (j n) -> p j n", n=D),
                                    x_c[i % R][:, 0:4, :], ALU.add)
                    V.tensor_tensor(z[:, i * CH + 4:(i + 1) * CH, :], ps_y[:, 1, 0:3 * D].rearrange("p (j n) -> p j n", n=D),
                                    x_c[i % R][:, 4:CH, :], ALU.add).then_inc(z_add, 1)
                    dve.wait_ge(z_add, i + 1)
                    row_stats(V, link, z, st, mv[0], i).then_inc(var_ok[0], 1)
                if 2 <= i < CHUNKS + 2:
                    c = i - 2
                    dve.wait_ge(scaled, c + 1)
                    V.tensor_tensor(z[:, blocks(c), :], z[:, blocks(c), :], xbeta[c % RB][:], ALU.add).then_inc(added, 1)
                    dve.wait_ge(added, c + 1)
                    if i < CHUNKS:
                        dve.wait_ge(var_ok[0], i + 1)
                    row_stats(V, link, z, st, mv[1], c).then_inc(var_ok[1], 1)
                if i == 2:
                    dve.wait_ge(dg_io, 32)
                    link(V.tensor_scalar(dg[:], dg[:], 1.0, None, ALU.max))
                    V.reciprocal(dg[:], dg[:]).then_inc(dg_ready, 1)
                if i >= 3:
                    c = i - 3
                    dve.wait_ge(sd_ok[1], c + 1)
                    link(V.reciprocal(rs[1][:, blocks(c)], sd[1][:, blocks(c)]))
                    for j in range(c * CH, (c + 1) * CH):
                        last = V.tensor_scalar(x1[:, j, :], z[:, j, :], mv[1][:, j, 0:1], rs[1][:, j:j + 1], ALU.subtract, ALU.mult)
                    last.then_inc(x_norm, 1)


def sums_1(nc, ctx, sem, sb, v):
    RING = 4
    A_c = [sb(f"A_c{r}", [P, NB * P], BF16) for r in range(RING)]
    sumT, gbase, x1h = v["sumT"], v["gbase"], v["x1h"]
    ps = [ctx.enter_context(nc.psum_tensor(f"ps_n{i}", [P, 512], F32)) for i in range(RING)]
    a_in = [sem(f"a_in{r}") for r in range(RING)]
    agg_mm, agg_add = sem("s1_mm"), sem("s1_add")
    gen = general_path(nc, ctx, sem, sb, v, 1, None, ps[0], ps[1])
    with nc.Block() as block:
        @block.sync
        def _(sp):
            def fast():
                for r in range(RING):
                    sp.dma_start(A_c[r][:], v["A_d"][r]).then_inc(a_in[r], 16)
                with sp.Fori(0, GROUPS // RING - 1) as i:
                    for r in range(RING):
                        g = RING * i + r
                        sp.wait_ge(agg_mm, g + 1)
                        sp.dma_start(A_c[r][:], v["A_d"][bass.ds(g + RING, 1), :, :].rearrange("a p c -> (a p) c")).then_inc(a_in[r], 16)
            fork(sp, v["flag"], fast, gen["sync"], v["force_general"])

        @block.tensor
        def _(pe):
            def fast():
                with pe.Fori(0, GROUPS // RING) as i:
                    for r in range(RING):
                        pe.wait_ge(a_in[r], 16 * (i + 1))
                        pe.wait_ge(agg_add, RING * i + 1)
                        for a in range(NB):
                            for part in range(2):
                                last = nc.tensor.matmul(ps[r][:, 0:P], x1h[:, a, part, :], A_c[r][:, a * P:(a + 1) * P],
                                                        start=(a == 0 and part == 0), stop=(a == NB - 1 and part == 1))
                        last.then_inc(agg_mm, 1)
            fork(pe, v["flag"], fast, gen["tensor"], v["force_general"])

        @block.vector
        def _(dve):
            def fast():
                nc.vector.memset(sumT[:], 0.0).then_inc(agg_add, 1)
                with dve.Fori(0, GROUPS // RING) as i:
                    for r in range(RING):
                        g = RING * i + r
                        base = dve.value_load(gbase[0:1, bass.ds(g, 1)], min_val=0, max_val=NP_ - 1)
                        dve.wait_ge(agg_mm, g + 1)
                        dve.wait_ge(agg_add, g + 1)
                        nc.vector.tensor_tensor(sumT[:, bass.ds(base, P)], ps[r][:, 0:P], sumT[:, bass.ds(base, P)],
                                                ALU.add).then_inc(agg_add, 1)
            fork(dve, v["flag"], fast, gen["vector"], v["force_general"])

        @block.scalar
        def _(act):
            fork(act, v["flag"], lambda: act.nop(), gen["scalar"], v["force_general"])

        @block.gpsimd
        def _(pool):
            fork(pool, v["flag"], lambda: pool.nop(), gen["gpsimd"], v["force_general"])


def update_1(nc, ctx, sem, sb, v):
    sumT, rdeg = v["sumT"], v["deg"]
    x1, x1T = v["x1"], v["x1T"]
    w1, w2, b1, b2bc = v["w1"], v["w2"], v["b1_sb"], v["b2bc"]
    hT_c = [sb(f"l1_hT{i}", [P, 2, HN]) for i in range(2)]
    z = sb("l1_z", [P, NB, D])
    st = sb("l1_st", [P, CH, 6])
    mv = sb("l1_mv", [P, NB, 2])
    sd, rs, shift = sb("l1_sd", [P, NB]), sb("l1_rs", [P, NB]), sb("l1_shift", [P, NB])
    ps_h, ps_y = ([ctx.enter_context(nc.psum_tensor(f"u1_{n}{i}", [P, 2, 512], F32)) for i in range(2)] for n in "hy")
    dv, scaled, h_mm, h_act, y_mm, z_add, var_ok, sd_ok, stat, normed, stored = (
        sem(f"u1_{n}") for n in ("dv", "scaled", "h_mm", "h_act", "y_mm", "z_add", "var_ok", "sd_ok", "stat", "normed",
                                 "stored"))

    with nc.Block() as block:
        @block.sync
        def _(sp):
            for c in range(CHUNKS):
                sp.wait_ge(normed, c + 1)
                sp.dma_start(load_chunk(v["out"], c), z[:, blocks(c), :]).then_inc(stored, 16)
            sp.wait_ge(stored, 16 * CHUNKS)

        @block.gpsimd
        def _(pool):
            pool.wait_ge(v["rdeg_in"], 16)
            for c in range(CHUNKS):
                cols = slice(c * CN, (c + 1) * CN)
                nc.gpsimd.tensor_tensor(sumT[:, cols], sumT[:, cols], rdeg[:, cols], ALU.mult).then_inc(scaled, 1)

        @block.tensor
        def _(pe):
            T = nc.tensor
            pe.wait_ge(v["l1_in"], 64)

            def hidden(c, half):
                if half == 0 and c >= 2:
                    pe.wait_ge(h_act, c - 1)
                if half == 1:
                    pe.wait_ge(scaled, c + 1)
                for i in range(2):
                    cols = slice(c * CN + i * HN, c * CN + (i + 1) * HN)
                    last = T.matmul(ps_h[c % 2][:, i, 0:HN], w1[:, half, :], (x1T, sumT)[half][:, cols],
                                    start=(half == 0), stop=(half == 1))
                if half == 1:
                    last.then_inc(h_mm, 1)

            hidden(0, 0)
            hidden(1, 0)
            hidden(0, 1)
            for c in range(CHUNKS):
                if c + 1 < CHUNKS:
                    if c >= 1:
                        hidden(c + 1, 0)
                    hidden(c + 1, 1)
                pe.wait_ge(h_act, c + 1)
                if c >= 2:
                    pe.wait_ge(z_add, c - 1)
                for j in range(CH):
                    last = T.matmul(ps_y[c % 2][:, j // 4, (j % 4) * D:(j % 4 + 1) * D],
                                    hT_c[c % 2][:].rearrange("p i n -> p (i n)")[:, j * P:(j + 1) * P], w2[:],
                                    start=True, stop=True)
                last.then_inc(y_mm, 1)

        @block.scalar
        def _(act):
            for i in range(CHUNKS + 2):
                if i < CHUNKS:
                    act.wait_ge(h_mm, i + 1)
                    if i >= 2:
                        act.wait_ge(y_mm, i - 1)
                    nc.scalar.activation(hT_c[i % 2][:], ps_h[i % 2][:, :, 0:HN], ACT.Relu, bias=b1[:, 0:1]).then_inc(h_act, 1)
                if i >= 2:
                    c = i - 2
                    act.wait_ge(stat, c + 1)
                    for j in range(c * CH, (c + 1) * CH):
                        last = nc.scalar.activation(z[:, j, :], z[:, j, :], ACT.Identity, scale=rs[:, j:j + 1], bias=shift[:, j:j + 1])
                    last.then_inc(normed, 1)
                if 1 <= i <= CHUNKS:
                    act.wait_ge(var_ok, i)
                    root(nc, sd, mv, v["eps_col"], i - 1).then_inc(sd_ok, 1)

        @block.vector
        def _(dve):
            V = nc.vector
            n = [0]

            def link(ins):
                n[0] += 1
                ins.then_inc(dv, 1)
                dve.wait_ge(dv, n[0])

            def finish(c):
                dve.wait_ge(sd_ok, c + 1)
                scale_shift(V, link, sd, mv, rs, shift, c).then_inc(stat, 1)

            for c in range(CHUNKS):
                b0 = c * CH
                dve.wait_ge(y_mm, c + 1)
                for i, m in ((0, 4), (1, 3)):
                    last = V.tensor_tensor(z[:, b0 + 4 * i:b0 + 4 * i + m, :],
                                           ps_y[c % 2][:, i, 0:m * D].rearrange("p (j n) -> p j n", n=D),
                                           b2bc[:].unsqueeze(1).broadcast_to([P, m, D]), ALU.add)
                last.then_inc(z_add, 1)
                dve.wait_ge(z_add, c + 1)
                link(V.scalar_tensor_tensor(z[:, blocks(c), :], z[:, blocks(c), :], 0.0, x1[:, blocks(c), :], ALU.max, ALU.add))
                row_stats(V, link, z, st, mv, c).then_inc(var_ok, 1)
                if c >= 1:
                    finish(c - 1)
            finish(CHUNKS - 1)


def kernel(x, src, dst, edge_attr_128, L0_gnn_msg_W1, L0_gnn_msg_b1, L0_gnn_msg_W2, L0_gnn_msg_b2, L0_gnn_upd_W1,
           L0_gnn_upd_b1, L0_gnn_upd_W2, L0_gnn_upd_b2, L0_gnn_ln_gamma, L0_gnn_ln_beta, L1_gnn_W1, L1_gnn_b1,
           L1_gnn_W2, L1_gnn_b2):
    import concourse.bacc as _bacc
    from concourse.bass_utils import run_bass_kernel_spmd as _run

    x, src, dst, e = (np.asarray(a) for a in (x, src, dst, edge_attr_128))
    pad = EP - N_EDGES
    x_nm = np.zeros((NP_, D), x.dtype)
    x_nm[:N_NODES] = x
    eT = np.zeros((D, EP), e.dtype)
    eT[:, :N_EDGES] = e.T
    src_row = np.zeros(EP, src.dtype)
    src_row[:N_EDGES] = src
    dst_row = np.full(EP + 1, NP_, dst.dtype)
    dst_row[:N_EDGES] = dst
    dst_row[N_EDGES:EP] = N_NODES + np.arange(pad) // SPREAD
    arrays = {
        "x_nm": x_nm, "xT": x_nm.T, "eT": eT,
        "src_pt": src_row.reshape(TILES, P).T, "dst_pt": dst_row[:EP].reshape(TILES, P).T,
        "dst_next_pt": dst_row[1:].reshape(TILES, P).T, "src_row": src_row, "dst_row": dst_row[:EP],
        "dst_first": dst_row[::P],
        "mW1": L0_gnn_msg_W1, "mb1": L0_gnn_msg_b1, "mW2": L0_gnn_msg_W2, "mb2": L0_gnn_msg_b2,
        "uW1": L0_gnn_upd_W1, "ub1": L0_gnn_upd_b1, "uW2": L0_gnn_upd_W2, "ub2": L0_gnn_upd_b2,
        "gamma": L0_gnn_ln_gamma, "beta": L0_gnn_ln_beta,
        "W1": L1_gnn_W1, "b1": L1_gnn_b1, "W2": L1_gnn_W2, "b2": L1_gnn_b2,
    }
    arrays = {k: np.ascontiguousarray(np.asarray(a)) for k, a in arrays.items()}
    nc = _bacc.Bacc("TRN2", target_bir_lowering=False, num_devices=1)
    aps = {k: nc.dram_tensor(k, a.shape, mybir.dt.from_np(a.dtype), kind="ExternalInput").ap() for k, a in arrays.items()}
    out = nc.dram_tensor("out", (NP_, D), F32, kind="ExternalOutput").ap()
    bass_gnn_two_layers(nc, out=out, **aps)
    r = _run(nc, [arrays], core_ids=[0])
    return r.results[0]["out"][:N_NODES]
```

```python
import numpy as np
import concourse.bass as bass
from concourse import mybir
from contextlib import ExitStack

F32, BF16, F16, I32 = mybir.dt.float32, mybir.dt.bfloat16, mybir.dt.float16, mybir.dt.int32
ALU = mybir.AluOpType
ACT = mybir.ActivationFunctionType
AX = mybir.AxisListType

N_NODES, N_EDGES, D = 6250, 200000, 128
P = 128
QT, GQ = 4, 7
GT = QT * GQ
GE = GT * P
GROUPS = -(-N_EDGES // GE)
TILES = GROUPS * GT
QUADS = GROUPS * GQ
EP = TILES * P
NB = -(-N_NODES // P)
NP_ = NB * P
NW = NP_ + P
SPREAD = -(-(EP - N_EDGES) // (NP_ - N_NODES))
W0 = 20
WIN = [(0, W0), (2, 10), (5, 12), (8, 12)]
AB = 25
A2 = 2 * AB
ROFF = [A2 * sum(w for _, w in WIN[:j]) for j in range(QT)]
RCOLS = ROFF[-1] + A2 * WIN[-1][1]
GW = 120
LASTQ = P - W0
CLEARED = 96
CH = 7
CHUNKS = NB // CH
CN = CH * P
HN = CN // 2
SW = D + 1
SWP = 132
EPS = 1e-5
SKIP = 8192


def bass_gnn_two_layers(nc, x_nm, xT, eT, src_pt, dst_pt, src_row, dst_row, dst_first, dst_last,
                        mW1, mb1, mW2, mb2, uW1, ub1, uW2, ub2, gamma, beta, W1, b1, W2, b2, out,
                        force_general=False):
    def dram(name, shape, dt):
        return nc.dram_tensor(name, shape, dt).ap()

    P_d = dram("P_d", (NP_, D), F32)
    Q_d = dram("Q_d", (NW, 3 * D), BF16)
    rel_d = dram("rel_d", (EP,), BF16)
    A_d = dram("A_d", (GROUPS, P, NB * P), BF16)
    acc_d = dram("acc_d", (NW, SWP), F32)
    x1_d = dram("x1_d", (NP_, D), F32)
    deg_d = dram("deg_d", (NP_,), F32)
    rdeg_d = dram("rdeg_d", (NP_,), F32)

    with ExitStack() as top:
        def sem(name, ctx=top):
            return ctx.enter_context(nc.semaphore(name))

        def sb(name, shape, dt=F32, ctx=top):
            return ctx.enter_context(nc.sbuf_tensor(name, shape, dt))

        sumT = sb("sumT", [P, NW])
        deg = sb("deg", [P, NW])
        flag = sb("flag", [1, 1], I32)
        offs = sb("offs", [1, QUADS], I32)
        gbase = sb("gbase", [1, GROUPS], I32)
        ident = sb("ident", [P, P])
        identb = sb("identb", [P, P], BF16)
        pid = sb("pid", [P, 1])
        iota = sb("iota", [P, 1000], F16)
        wc = sb("wc", [P, D])
        eps_col = sb("eps_col", [P, 1])
        u1a, wagg, bagg, u2 = sb("u1a", [P, D]), sb("wagg", [P, D]), sb("bagg", [1, D]), sb("u2", [P, D])
        ub1_sb, ub2bc, gbc, bbc = sb("ub1_sb", [P, 1]), sb("ub2bc", [P, D]), sb("gbc", [P, D]), sb("bbc", [P, D])

        with ExitStack() as both:
            gath = sb("gath", [P, GQ, QT * D], F32, both)
            src_i = [sb(f"src_i{k}", [P, GT], I32, both) for k in range(2)]
            eT0 = sb("eT0", [P, GE], F32, both)
            rel_b = sb("rel_b", [P, GE], BF16, both)
            r_in = sem("r_in")
            dst_i0, first_i0 = sb("dst_i0", [P, GT], I32, both), sb("first_i0", [P, GT], I32, both)
            g_in = [sem(f"g_in{q}") for q in range(GQ)]
            e_in = [sem(f"e_in{k}") for k in range(2)]
            i_in = [sem(f"i_in{k}") for k in range(2)]
            names = locals()
            run_parts(nc, (build_prepare, build_edges), ("", ""), lambda n: sem(n, both), names)
        with ExitStack() as ctx:
            build_nodes(nc, ctx, lambda n: sem(n, ctx), lambda n, s, d=F32: sb(n, s, d, ctx), locals())


def run_parts(nc, builders, prefixes, sem, v):
    parts = []
    for build, prefix in zip(builders, prefixes):
        with ExitStack() as ctx:
            parts.append(build(nc, ctx, sem, lambda n, s, d=F32: ctx.enter_context(nc.sbuf_tensor(prefix + n, s, d)), v))
            v = {**v, **parts[-1]}
    with nc.Block() as block:
        @block.sync
        def _(sp):
            for part in parts:
                part["sync"](sp)

        @block.tensor
        def _(pe):
            for part in parts:
                part["tensor"](pe)

        @block.scalar
        def _(act):
            for part in parts:
                part["scalar"](act)

        @block.gpsimd
        def _(pool):
            for part in parts:
                part["gpsimd"](pool)

        @block.vector
        def _(dve):
            for part in parts:
                part["vector"](dve)


def build_prepare(nc, ctx, sem, sb, v):
    P_d, Q_d, rel_d = v["P_d"], v["Q_d"], v["rel_d"]
    pid, ident, identb, iota = v["pid"], v["ident"], v["identb"], v["iota"]
    flag, offs, gbase = v["flag"], v["offs"], v["gbase"]
    wab = sb("wab", [P, 2, D])
    mw2, mw2T, u1b, mb2c = sb("mw2", [P, D]), sb("mw2T", [P, D]), sb("u1b", [P, D]), sb("mb2c", [P, 1])
    xT_sb = sb("xT_sb", [P, NP_])
    b1bc = sb("b1bc", [P, D])
    RP = 2 * GROUPS
    RC = EP // RP
    R_i, RB_i, relR = sb("R_i", [RP, RC + 1], I32), sb("RB_i", [RP, 1], I32), sb("relR", [RP, RC], BF16)
    falls = sb("falls", [RP, RC], BF16)
    F_i, L_i = sb("F_i", [GROUPS, GT + 1], I32), sb("L_i", [GROUPS, GT], I32)
    F1_i = sb("F1_i", [1, TILES], I32)
    dF, dL = sb("dF", [GROUPS, GT]), sb("dL", [GROUPS, GT])
    bad = sb("bad", [GROUPS, 5, GT])
    bad1 = sb("bad1", [P, 2])
    ones_col = sb("ones_col", [P, 1])
    orow = sb("orow", [1, QUADS])
    PR, QR = 4, 4
    Pst = [sb(f"Pst{i}", [P, CH, D]) for i in range(PR)]
    qf = [sb(f"qf{i}", [P, CH, D]) for i in range(2)]
    qr = [sb(f"qr{i}", [P, CH, D]) for i in range(2)]
    Qst = [sb(f"Qst{i}", [P, CH, 3, D], BF16) for i in range(QR)]
    zeros = sb("zeros", [P, 3 * D], BF16)
    ps_p, ps_q = ([ctx.enter_context(nc.psum_tensor(f"ps_{n}{i}", [P, 8, D], F32)) for i in range(2)] for n in "pq")

    w_in, b_in, t_in, r_in, s_in = sem("w_in"), sem("b_in"), sem("t_in"), sem("rows_in"), sem("s_in")
    u_in, wt, flag_ready, weights_ready = sem("u_in"), sem("wt"), sem("flag_ready"), sem("weights_ready")
    x_in = [sem(f"x_in{i}") for i in range(CHUNKS)]
    made, dv, p_mm, q_mm, p_out, q1_out, q2_out, r_out, q3_out, qf_out = (
        sem(n) for n in ("made", "dv", "p_mm", "q_mm", "p_out", "q1_out", "q2_out", "r_out", "q3_out", "qf_out"))
    rel_ready, bad_ready, bad_sum, st_z, st_r = (
        sem(n) for n in ("rel_ready", "bad_ready", "bad_sum", "st_z", "st_r"))
    st_p = [sem(f"st_p{i}") for i in range(PR)]
    st_q = [sem(f"st_q{i}") for i in range(QR)]

    def sync(sp):
        sp.dma_start(wab[:], v["mW1"][0:2 * D, :].rearrange("(c k) n -> k c n", c=2)).then_inc(w_in, 16)
        sp.dma_start(b1bc[:], v["mb1"].partition_broadcast(P)).then_inc(b_in, 16)
        for c in range(CHUNKS):
            sp.dma_start(xT_sb[:, c * CN:(c + 1) * CN], v["xT"][:, c * CN:(c + 1) * CN]).then_inc(x_in[c], 16)
        sp.dma_start(v["wc"][:], v["mW1"][2 * D:3 * D, :]).then_inc(u_in, 16)
        rows = v["dst_row"]
        for h in range(2):
            half = bass.AP(rows.tensor, rows.offset + h * RC, [[2 * RC, GROUPS], [1, RC + 1]])
            sp.dma_start(R_i[h * GROUPS:(h + 1) * GROUPS, :], half).then_inc(r_in, 16)
        for to, a in ((mw2, v["mW2"]), (v["u1a"], v["uW1"][0:D, :]), (u1b, v["uW1"][D:2 * D, :]), (v["u2"], v["uW2"])):
            sp.dma_start(to[:], a).then_inc(u_in, 16)
        with nc.allow_non_contiguous_dma(reason="one word for each partition"):
            sp.dma_start(mb2c[:], v["mb2"].rearrange("(n a) -> n a", a=1)).then_inc(u_in, 16)
            sp.dma_start(v["ub1_sb"][:], v["ub1"].rearrange("(n a) -> n a", a=1)).then_inc(u_in, 16)
        for to, a in ((v["ub2bc"], v["ub2"]), (v["gbc"], v["gamma"]), (v["bbc"], v["beta"])):
            sp.dma_start(to[:], a.partition_broadcast(P)).then_inc(u_in, 16)
        sp.wait_ge(made, 5)
        sp.dma_start(Q_d[NP_:NW, :], zeros[:]).then_inc(st_z, 16)
        for c in range(CHUNKS):
            sp.wait_ge(p_out, c + 1)
            sp.dma_start(P_d[c * CN:(c + 1) * CN, :].rearrange("(p j) n -> p j n", j=CH),
                         Pst[c % PR][:]).then_inc(st_p[c % PR], 16)
        sp.wait_ge(rel_ready, 1)
        sp.dma_start(rel_d.rearrange("(g h c) -> h g c", h=2, c=RC)[0], relR[0:GROUPS, :]).then_inc(st_r, 16)
        sp.dma_start(rel_d.rearrange("(g h c) -> h g c", h=2, c=RC)[1], relR[GROUPS:RP, :]).then_inc(st_r, 16)
        for c in range(CHUNKS):
            sp.wait_ge(q3_out, c + 1)
            sp.dma_start(Q_d[c * CN:(c + 1) * CN, :].rearrange("(p j) n -> p j n", j=CH),
                         Qst[c % QR][:].rearrange("p j t n -> p j (t n)")).then_inc(st_q[c % QR], 16)
            if c == 1:
                sp.wait_ge(st_r, 32)
                sp.dma_start(v["rel_b"][:], rel_d[0:GE].partition_broadcast(P)).then_inc(v["r_in"], 16)
            if c == 3:
                sp.dma_start(v["eT0"][:], v["eT"][:, 0:GE]).then_inc(v["e_in"][0], 16)
                sp.dma_start(v["dst_i0"][:], v["dst_pt"][:, 0:GT]).then_inc(v["i_in"][0], 16)
                sp.dma_start(v["first_i0"][:], v["dst_first"][0:GT].partition_broadcast(P)).then_inc(v["i_in"][0], 16)

    def gpsimd(pool):
        pool.iota(pid[:], [[0, 1]], base=0, channel_multiplier=1, allow_small_or_imprecise_dtypes=True).then_inc(made, 1)
        pool.iota(iota[:], [[1, 1000]], base=0, channel_multiplier=0, allow_small_or_imprecise_dtypes=True).then_inc(made, 1)
        pool.memset(ident[:], 0.0).then_inc(made, 1)
        pool.memset(identb[:], 0.0).then_inc(made, 1)
        pool.memset(zeros[:], 0.0).then_inc(made, 1)
        pool.memset(v["eps_col"][:], EPS)
        pool.memset(ones_col[:], 1.0)
        pool.memset(v["sumT"][:], 0.0)
        pool.memset(v["deg"][0:1, :], 0.0).then_inc(made, 1)
        pool.wait_ge(made, 6)
        for m in (ident, identb):
            pool.affine_select(out=m[:], in_=m[:], compare_op=ALU.not_equal, fill=1.0, base=0,
                               pattern=[[-1, P]], channel_multiplier=1).then_inc(made, 1)
        pool.wait_ge(s_in, 16)
        for i in range(PR):
            pool.wait_ge(st_p[i], 16 * len(range(i, CHUNKS, PR)))
        for c in range(GT):
            q, t = divmod(c, QT)
            pool.indirect_dma_start(v["gath"][:, q, t * D:(t + 1) * D], None, P_d,
                                    bass.IndirectOffsetOnAxis(ap=v["src_i"][0][:, c:c + 1], axis=0)).then_inc(v["g_in"][q], 16)

    def tensor(pe):
        pe.wait_ge(w_in, 16)

        def table(c, half):
            ps, done, free = ((ps_p, p_mm, p_out), (ps_q, q_mm, qf_out))[half]
            pe.wait_ge(x_in[c], 16)
            if c >= 2:
                pe.wait_ge(free, c - 1)
            for j in range(CH):
                nodes = xT_sb[:, c * CN:(c + 1) * CN].rearrange("k (p j) -> k j p", j=CH)[:, j, :]
                last = nc.tensor.matmul(ps[c % 2][:, j, :], nodes, wab[:, half, :], start=True, stop=True)
            last.then_inc(done, 1)

        for c in range(2):
            table(c, 0)
            table(c, 1)
        for half in range(2):
            for c in range(2, CHUNKS):
                table(c, half)
        pe.wait_ge(u_in, 160)
        pe.wait_ge(made, 8)
        nc.tensor.matmul(ps_p[1][:, 0, :], mw2[:], ident[:], is_transpose=True, start=True, stop=True).then_inc(wt, 1)
        pe.wait_ge(wt, 2)
        nc.tensor.matmul(ps_p[1][:, 1, :], mw2T[:], u1b[:], start=True, stop=True)
        nc.tensor.matmul(ps_p[1][0:1, 2, :], mb2c[:], u1b[:], start=True, stop=True).then_inc(wt, 1)
        pe.wait_ge(bad_ready, 1)
        for k in range(2):
            last = nc.tensor.matmul(ps_p[0][0:1, 0, 0:1], bad1[:, k:k + 1], ones_col[:], start=(k == 0), stop=(k == 1))
        last.then_inc(bad_sum, 1)

    def scalar(act):
        firsts, lasts = v["dst_first"], v["dst_last"]
        with nc.allow_non_contiguous_dma(reason="one word for each half of a group"):
            for h in range(2):
                act.dma_start(RB_i[h * GROUPS:(h + 1) * GROUPS, :],
                              firsts[0:TILES].rearrange("(g t) -> g t", t=GT)[:, 0:1]).then_inc(r_in, 16)
        act.dma_start(F_i[:], bass.AP(firsts.tensor, firsts.offset, [[GT, GROUPS], [1, GT + 1]])).then_inc(t_in, 16)
        act.dma_start(L_i[:], lasts.rearrange("(g t) -> g t", t=GT)).then_inc(t_in, 16)
        act.dma_start(F1_i[:], firsts[0:TILES].rearrange("(a t) -> a t", a=1)).then_inc(t_in, 16)
        act.dma_start(v["src_i"][0][:], v["src_pt"][:, 0:GT]).then_inc(s_in, 16)

        def copy_p(c):
            act.wait_ge(p_mm, c + 1)
            if c >= PR:
                act.wait_ge(st_p[c % PR], 16 * (c // PR))
            nc.scalar.activation(Pst[c % PR][:], ps_p[c % 2][:, 0:CH, :], ACT.Copy).then_inc(p_out, 1)

        def first_part(c):
            act.wait_ge(qf_out, c + 1)
            if c >= QR:
                act.wait_ge(st_q[c % QR], 16 * (c // QR))
            nc.scalar.activation(Qst[c % QR][:, :, 0, :], qf[c % 2][:], ACT.Copy).then_inc(q1_out, 1)

        def second_part(c):
            act.wait_ge(r_out, c + 1)
            nc.scalar.activation(Qst[c % QR][:, :, 1, :], qr[c % 2][:], ACT.Copy).then_inc(q2_out, 1)

        copy_p(0)
        first_part(0)
        copy_p(1)
        for c in range(2, CHUNKS):
            copy_p(c)
            if c == 2:
                first_part(1)
                second_part(0)
        for c in range(2, CHUNKS + 1):
            if c < CHUNKS:
                first_part(c)
            second_part(c - 1)
        act.wait_ge(wt, 1)
        nc.scalar.activation(mw2T[:], ps_p[1][:, 0, :], ACT.Copy).then_inc(wt, 1)
        act.wait_ge(wt, 3)
        nc.scalar.activation(v["wagg"][:], ps_p[1][:, 1, :], ACT.Copy)
        nc.scalar.activation(v["bagg"][:], ps_p[1][0:1, 2, :], ACT.Copy).then_inc(weights_ready, 1)

    def vector(dve):
        n = [0]

        def link(ins):
            n[0] += 1
            ins.then_inc(dv, 1)
            dve.wait_ge(dv, n[0])

        V = nc.vector
        def checks():
            link(V.memset(bad1[:], 0.0))
            V.memset(bad[:], 0.0)
            dve.wait_ge(r_in, 64)
            V.tensor_scalar(relR[:], R_i[:, 0:RC], RB_i[:, 0:1], None, ALU.subtract).then_inc(rel_ready, 1)
            link(V.tensor_tensor(falls[:], R_i[:, 0:RC], R_i[:, 1:RC + 1], ALU.is_gt))
            V.reduce_sum(bad1[0:RP, 0:1], falls[:], AX.X)
            dve.wait_ge(t_in, 48)
            F = F_i[:, 0:GT]
            q3 = lambda t: t.rearrange("p (q t) -> p q t", t=QT)
            Fq = q3(F)[:, :, 0:1].broadcast_to([GROUPS, GQ, QT])
            V.tensor_tensor(q3(dF[:]), q3(F), Fq, ALU.subtract)
            link(V.tensor_tensor(q3(dL[:]), q3(L_i[:]), Fq, ALU.subtract))
            for j, (w0, w) in enumerate(WIN):
                V.tensor_scalar(q3(bad[:, 0, :])[:, :, j], q3(dF[:])[:, :, j], float(w0), None, ALU.is_lt)
                V.tensor_scalar(q3(bad[:, 1, :])[:, :, j], q3(dL[:])[:, :, j], float(w0 + w - 1), None, ALU.is_gt)
            last = V.tensor_tensor(bad[:, 2, :], F_i[:, 1:GT + 1], F, ALU.is_le)
            link(last)
            off = q3(F)[:, :, 0]
            V.tensor_tensor(dF[:, 0:GQ], off, F_i[:, 0:1].broadcast_to([GROUPS, GQ]), ALU.subtract)
            V.tensor_tensor(dL[:, 1:GQ], off[:, 1:GQ], off[:, 0:GQ - 1], ALU.subtract)
            link(V.tensor_tensor(dL[:, GQ:GQ + 1], L_i[:, GT - 1:GT], F_i[:, 0:1], ALU.subtract))
            V.tensor_scalar(bad[:, 3, 1:GQ], dL[:, 1:GQ], float(W0 - 1), None, ALU.is_gt)
            V.tensor_scalar(bad[:, 4, 0:1], dL[:, GQ:GQ + 1], float(GW - 1), None, ALU.is_gt)
            V.tensor_scalar(bad[:, 4, 1:2], dF[:, GQ - 1:GQ], float(LASTQ), None, ALU.is_gt)
            link(V.tensor_scalar(bad[:, 4, 2:3], dF[:, GQ - 1:GQ], float(CLEARED - W0), None, ALU.is_lt))
            V.reduce_sum(bad1[0:GROUPS, 1:2], bad[:].rearrange("p a t -> p (a t)"), AX.X).then_inc(bad_ready, 1)
            F1 = F1_i[:].rearrange("p (g q t) -> p g q t", q=GQ, t=QT)[:, :, :, 0]
            link(V.tensor_tensor(orow[:].rearrange("p (g q) -> p g q", q=GQ), F1,
                                 F1[:, :, 0:1].broadcast_to([1, GROUPS, GQ]), ALU.subtract))
            V.tensor_scalar(offs[:], orow[:], 0.0, float(LASTQ), ALU.max, ALU.min)
            V.tensor_scalar(gbase[:], F1[:, :, 0], 0.0, float(NP_ - 1), ALU.max, ALU.min)

        dve.wait_ge(b_in, 16)
        for i in range(CHUNKS + 2):
            if i == 2:
                checks()
            if i < CHUNKS:
                dve.wait_ge(q_mm, i + 1)
                if i >= 2:
                    dve.wait_ge(r_out, i - 1)
                V.tensor_tensor(qf[i % 2][:], ps_q[i % 2][:, 0:CH, :],
                                b1bc[:].unsqueeze(1).broadcast_to([P, CH, D]), ALU.add).then_inc(qf_out, 1)
            if 1 <= i <= CHUNKS:
                c = i - 1
                dve.wait_ge(q1_out, c + 1)
                if c >= 2:
                    dve.wait_ge(q3_out, c - 1)
                V.tensor_tensor(qr[c % 2][:], qf[c % 2][:], Qst[c % QR][:, :, 0, :], ALU.subtract).then_inc(r_out, 1)
            if i >= 2:
                c = i - 2
                dve.wait_ge(q2_out, c + 1)
                V.tensor_tensor(Qst[c % QR][:, :, 2, :], qr[c % 2][:], Qst[c % QR][:, :, 1, :], ALU.subtract).then_inc(q3_out, 1)
        dve.wait_ge(bad_sum, 1)
        V.tensor_scalar(flag[:], ps_p[0][0:1, 0, 0:1], 1.0, None, ALU.min).then_inc(flag_ready, 1)

    def settled(eng):
        eng.wait_ge(made, 8)
        eng.wait_ge(s_in, 16)
        eng.wait_ge(flag_ready, 1)
        eng.wait_ge(weights_ready, 1)
        eng.wait_ge(st_z, 16)
        eng.wait_ge(st_r, 32)
        for stored, ring in ((st_p, PR), (st_q, QR)):
            for i in range(ring):
                eng.wait_ge(stored[i], 16 * len(range(i, CHUNKS, ring)))

    return dict(sync=sync, tensor=tensor, scalar=scalar, gpsimd=gpsimd, vector=vector, settled=settled)


def build_edges(nc, ctx, sem, sb, v):
    flag, offs, gbase, force_general = v["flag"], v["offs"], v["gbase"], v["force_general"]
    pid, ident, identb, iota, wc = v["pid"], v["ident"], v["identb"], v["iota"], v["wc"]
    sumT, deg = v["sumT"], v["deg"]
    gath, src_i, g_in = v["gath"], v["src_i"], v["g_in"]

    eT = [v["eT0"], sb("eT1", [P, GE])]
    dst_i = [v["dst_i0"], sb("dst_i1", [P, GT], I32)]
    first_i = [v["first_i0"], sb("first_i1", [P, GT], I32)]
    nodeE = [sb(f"nodeE{k}", [P, GE], BF16) for k in range(2)]
    Qw = [sb(f"Qw{k}", [P, 3 * D], BF16) for k in range(2)]
    rel_g = [sb(f"rel_g{k}", [P, GT]) for k in range(2)]
    rel_q = sb("rel_q", [P, GT])
    blk_i, low_i = sb("blk_i", [P, GT], I32), sb("low_i", [P, GT], I32)
    key = [sb(f"key{k}", [P, GT]) for k in range(2)]
    low = [sb(f"low{k}", [P, GT]) for k in range(2)]
    edgeN = [sb(f"edgeN{k}", [P, QT, P]) for k in range(2)]
    edgeL = [sb(f"edgeL{k}", [P, QT, P], BF16) for k in range(2)]
    edgeK = [sb(f"edgeK{k}", [P, RCOLS], BF16) for k in range(2)]
    pre = [sb(f"pre{k}", [P, QT * D]) for k in range(2)]
    h = [sb(f"h{k}", [P, QT, D + 2]) for k in range(2)]
    counts = [sb(f"counts{k}", [P, A2, P], BF16) for k in range(2)]
    carry = [sb(f"carry{k}", [P, A2], BF16) for k in range(2)]
    sumS = sb("sumS", [P, SWP])

    ps_pre = [ctx.enter_context(nc.psum_tensor(f"ps_pre{k}", [P, QT * D], F32)) for k in range(2)]
    ps_cnt = [ctx.enter_context(nc.psum_tensor(f"ps_cnt{k}", [P, 2, 512], F32)) for k in range(2)]
    ps_sum = [ctx.enter_context(nc.psum_tensor(f"ps_sum{k}", [P, 512], F32)) for k in range(2)]
    TR = 2 * P

    e_in, i_in, r_in, rel_b = v["e_in"], v["i_in"], v["r_in"], v["rel_b"]
    s_in = [sem(f"s_in{k}") for k in range(2)]
    q_in = [sem(f"q_in{k}") for k in range(2)]
    c_out = [sem(f"c_out{k}") for k in range(2)]
    prepared = sem("prepared")
    onehots = sem("onehots")
    pre_mm, cnt_mm, sum_mm = sem("pre_mm"), sem("cnt_mm"), sem("sum_mm")
    pre_add, silu, cnt_copy = sem("pre_add"), sem("silu"), sem("cnt_copy")
    carried = sem("carried")
    sum_copy, sum_tr, sum_add = sem("sum_copy"), sem("sum_tr"), sem("sum_add")
    dv = sem("key_parts")
    h_ones = sem("h_ones")
    gen = general_path(nc, ctx, sem, sb, v, 0, eT[0], ps_pre[0], ps_sum[0])

    def loop(eng, first, group, last):
        first()
        with eng.Fori(0, (GROUPS - 2) // 2) as i:
            group(i, 1)
            group(i + 1, 0)
        last()

    def sync(sp):
        v["settled"](sp)
        def load_window(g, k):
            base = sp.value_load(gbase[0:1, bass.ds(g, 1)], min_val=0, max_val=NP_ - 1)
            sp.dma_start(Qw[k][:], v["Q_d"][bass.ds(base, P), :]).then_inc(q_in[k], 16)

        def load(g, k):
            sp.dma_start(src_i[k][:], v["src_pt"][:, bass.ds(g * GT, GT)]).then_inc(s_in[k], 16)
            sp.dma_start(dst_i[k][:], v["dst_pt"][:, bass.ds(g * GT, GT)]).then_inc(i_in[k], 16)
            sp.dma_start(first_i[k][:], v["dst_first"][bass.ds(g * GT, GT)].partition_broadcast(P)).then_inc(i_in[k], 16)
            load_window(g, k)
            sp.dma_start(eT[k][:], v["eT"][:, bass.ds(g * GE, GE)]).then_inc(e_in[k], 16)

        def load_rel(g):
            sp.dma_start(rel_b[:], v["rel_d"][bass.ds(g * GE, GE)].partition_broadcast(P)).then_inc(r_in, 16)

        def store(g, k):
            sp.wait_ge(cnt_copy, g * GQ + GQ)
            sp.dma_start(v["A_d"][bass.ds(g, 1), :, :].rearrange("a p c -> (a p) c"),
                         counts[k][:, 0:NB, :].rearrange("p a d -> p (a d)")).then_inc(c_out[k], 16)

        def fast():
            load_window(0, 0)
            load(1, 1)
            sp.wait_ge(prepared, 1)
            load_rel(1)
            with sp.Fori(0, (GROUPS - 2) // 2) as i:
                for k in range(2):
                    g = 2 * i + k
                    sp.wait_ge(prepared, g + 2)
                    load_rel(g + 2)
                    sp.wait_ge(sum_mm, g * GQ + GQ)
                    load(g + 2, k)
                    store(g, k)
            for g in (GROUPS - 2, GROUPS - 1):
                store(g, g % 2)
            for k in range(2):
                sp.wait_ge(c_out[k], 16 * (GROUPS // 2))

        fork(sp, flag, fast, gen["sync"], force_general)

    def gpsimd(pool):
        v["settled"](pool)
        turn = sem("turn")

        def group(half, k):
            g = 2 * half + k
            pool.wait_ge(s_in[k], 16 * (half + k))
            pool.sem_inc(turn, 1)
            for q in range(GQ):
                pool.wait_ge(pre_add, (g - 1) * GQ + q + 1)
                pool.sem_inc(turn, 1)
                for t in range(QT):
                    c = q * QT + t
                    pool.indirect_dma_start(
                        gath[:, q, t * D:(t + 1) * D], None, v["P_d"],
                        bass.IndirectOffsetOnAxis(ap=src_i[k][:, c:c + 1], axis=0)).then_inc(g_in[q], 16)

        def fast():
            loop(pool, lambda: None, group, lambda: group(GROUPS // 2 - 1, 1))

        fork(pool, flag, fast, gen["gpsimd"], force_general)

    def vector(dve):
        v["settled"](dve)
        V = nc.vector
        def make_keys(half, k, first=False):
            g = 2 * half + k
            if not (first and k == 0):
                dve.wait_ge(s_in[k], 16 * (half + k))
            dve.wait_ge(i_in[k], 32 * (half + 1))
            D3 = dst_i[k][:]
            Fg = first_i[k][:, 0:1].broadcast_to([P, GT])
            Fq = first_i[k][:].rearrange("p (q t) -> p q t", t=QT)[:, :, 0:1].broadcast_to([P, GQ, QT])
            V.tensor_tensor(rel_g[k][:], D3, Fg, ALU.subtract)
            V.tensor_tensor(rel_q[:].rearrange("p (q t) -> p q t", t=QT), D3.rearrange("p (q t) -> p q t", t=QT),
                            Fq, ALU.subtract)
            V.tensor_scalar(blk_i[:], src_i[k][:], 7, None, ALU.arith_shift_right)
            V.tensor_scalar(low_i[:], src_i[k][:], P - 1, None, ALU.bitwise_and).then_inc(dv, 1)
            dve.wait_ge(dv, g + 1)
            V.tensor_copy(low[k][:], low_i[:])
            kq, bq, rq = (t[:].rearrange("p (q t) -> p q t", t=QT) for t in (key[k], blk_i, rel_q))
            for j, (w0, w) in enumerate(WIN):
                V.scalar_tensor_tensor(kq[:, :, j], bq[:, :, j], float(w), rq[:, :, j], ALU.mult, ALU.add)

        def expand(k, cols):
            return V.tensor_scalar(nodeE[k][:, cols], rel_b[:, cols], pid[:, 0:1], None, ALU.is_equal)

        def expand_first(half, k, early=False):
            g = 2 * half + k
            if not early:
                dve.wait_ge(pre_mm, (g - 1) * GQ)
            dve.wait_ge(r_in, 16 * (g + 1))
            expand(k, slice(0, GE // 2))

        def expand_rest(half, k, early=False):
            expand(k, slice(GE // 2, GE))
            if not early:
                dve.wait_ge(c_out[k], 16 * half)
            V.memset(counts[k][:, :, CLEARED:P], 0.0).then_inc(prepared, 1)

        def hots(s, q, k, first=False):
            x = (k + q) % 2
            if not first:
                dve.wait_ge(sum_mm, s - 1)
                dve.wait_ge(cnt_mm, s - 1)
            c = slice(q * QT, (q + 1) * QT)
            io = iota[:, 0:P].unsqueeze(1).broadcast_to([P, QT, P])
            V.tensor_tensor(edgeN[x][:], io, rel_g[k][:, c].unsqueeze(2).broadcast_to([P, QT, P]), ALU.is_equal)
            V.tensor_tensor(edgeL[x][:], io, low[k][:, c].unsqueeze(2).broadcast_to([P, QT, P]), ALU.is_equal)
            for j, (w0, w) in enumerate(WIN):
                last = V.tensor_scalar(edgeK[x][:, ROFF[j]:ROFF[j] + A2 * w], iota[:, w0:w0 + A2 * w],
                                       key[k][:, q * QT + j:q * QT + j + 1], None, ALU.is_equal)
            last.then_inc(onehots, 1)

        def add(s, q, k, g, first=False):
            x = (k + q) % 2
            dve.wait_ge(pre_mm, s + 1)
            dve.wait_ge(g_in[q], 16 * QT * (g + 1))
            if not first:
                dve.wait_ge(silu, s - 1)
            V.tensor_tensor(pre[x][:], ps_pre[x][:], gath[:, q, :], ALU.add).then_inc(pre_add, 1)

        def add_sums(g, k):
            dve.wait_ge(sum_tr, g + 2)
            dve.wait_ge(sum_add, g + 1)
            base = dve.value_load(gbase[0:1, bass.ds(g, 1)], min_val=0, max_val=NP_ - 1)
            V.tensor_tensor(sumT[:, bass.ds(base, P)], ps_sum[k][:, TR:TR + P], sumT[:, bass.ds(base, P)], ALU.add)
            V.tensor_tensor(deg[0:1, bass.ds(base, P)], ps_sum[k][0:1, TR + P:TR + 2 * P], deg[0:1, bass.ds(base, P)],
                            ALU.add).then_inc(sum_add, 1)

        def group(half, k, first=False, last=False):
            g = 2 * half + k
            nxt = (half, 1) if k == 0 else (half + 1, 0)
            for q in range(GQ):
                s = g * GQ + q
                add(s, q, k, g, first and q < 2)
                if q < GQ - 1:
                    hots(s + 1, q + 1, k, first and q == 0)
                elif not last:
                    dve.wait_ge(prepared, g + 2)
                    hots(s + 1, 0, 1 - k)
                if not last and q in (2, 3, 4):
                    if q == 2:
                        make_keys(*nxt)
                    else:
                        (expand_first, expand_rest)[q - 3](*nxt, early=first)
                if q == 5 and not first:
                    add_sums(g - 1, 1 - k)

        def fast():
            for k in range(2):
                V.memset(h[k][:, :, D:D + 2], 1.0).then_inc(h_ones, 1)
            dve.sem_inc(sum_add, 1)
            make_keys(0, 0, first=True)
            expand_first(0, 0, early=True)
            expand_rest(0, 0, early=True)
            dve.wait_ge(prepared, 1)
            hots(0, 0, 0, True)
            loop(dve, lambda: group(0, 0, first=True), group, lambda: group(GROUPS // 2 - 1, 1, last=True))
            add_sums(GROUPS - 1, 1)

        fork(dve, flag, fast, gen["vector"], force_general)

    def tensor(pe):
        v["settled"](pe)
        T = nc.tensor

        def products(s, q, k, half, first=False):
            x = (k + q) % 2
            if q == 0:
                pe.wait_ge(e_in[k], 16 * (half + 1))
                pe.wait_ge(q_in[k], 16 * (half + 1))
                pe.wait_ge(prepared, 2 * half + k + 1)
            if not first:
                pe.wait_ge(pre_add, s - 1)
            for t in range(QT):
                e0 = (q * QT + t) * P
                o = ps_pre[x][:, t * D:(t + 1) * D]
                T.matmul(o, eT[k][:, e0:e0 + P], wc[:], start=True, stop=False)
                for part in range(3):
                    last = T.matmul(o, nodeE[k][:, e0:e0 + P], Qw[k][:, part * D:(part + 1) * D],
                                    start=False, stop=(part == 2))
            last.then_inc(pre_mm, 1)

        def count(s, q, k, g, first=False):
            x = (k + q) % 2
            pe.wait_ge(onehots, s + 1)
            if not first:
                pe.wait_ge(cnt_copy, s - 1)
            for b in range(2):
                o = ps_cnt[x][:, b, 0:AB * W0].rearrange("p (a d) -> p a d", d=W0)
                for j, (w0, w) in enumerate(WIN):
                    r = edgeK[x][:, ROFF[j] + b * AB * w:ROFF[j] + (b + 1) * AB * w].rearrange("p (a d) -> p a d", d=w)
                    last = T.matmul(o[:, :, w0:w0 + w], edgeL[x][:, j, :], r, start=(j == 0),
                                    stop=(j == QT - 1 and q == 0))
            if q > 0:
                pe.wait_ge(carried, g * (GQ - 1) + q)
                for b in range(2):
                    o = ps_cnt[x][:, b, 0:AB * W0].rearrange("p (a d) -> p a d", d=W0)
                    last = T.matmul(o[:, :, 0:1], identb[:], carry[x][:, b * AB:(b + 1) * AB].unsqueeze(2),
                                    start=False, stop=True)
            last.then_inc(cnt_mm, 1)

        def sums(s, q, k, g, first=False):
            x = (k + q) % 2
            pe.wait_ge(silu, s + 1)
            if q == 0 and not first:
                pe.wait_ge(sum_add, g)
            for t in range(QT):
                last = T.matmul(ps_sum[k][:, 0:SW], edgeN[x][:, t, :], h[x][:, t, 0:SW],
                                start=(q == 0 and t == 0), stop=(q == GQ - 1 and t == QT - 1))
            last.then_inc(sum_mm, 1)

        def transpose_sums(g, k):
            pe.wait_ge(sum_copy, g + 1)
            T.matmul(ps_sum[k][:, TR:TR + P], sumS[:, 0:D], ident[:], is_transpose=True, start=True, stop=True)
            T.matmul(ps_sum[k][0:1, TR + P:TR + 2 * P], sumS[:, D:SW], ident[:], start=True, stop=True).then_inc(sum_tr, 1)

        def group(half, k, first=False, last=False, second=False):
            g = 2 * half + k
            for q in range(GQ):
                s = g * GQ + q
                if q < GQ - 1:
                    products(s + 1, q + 1, k, half, first and q == 0)
                elif not last:
                    half1, k1 = (half, 1) if k == 0 else (half + 1, 0)
                    products(s + 1, 0, k1, half1)
                sums(s, q, k, g, first)
                if q < GQ - 1:
                    count(s + 1, q + 1, k, g, first and q == 0)
                elif not last:
                    count(s + 1, 0, k1, g + 1)
                if q == 1 and not first:
                    transpose_sums(g - 1, 1 - k)

        def fast():
            pe.sem_inc(sum_tr, 1)
            pe.wait_ge(h_ones, 2)
            products(0, 0, 0, 0, True)
            count(0, 0, 0, 0, True)
            loop(pe, lambda: group(0, 0, first=True), group, lambda: group(GROUPS // 2 - 1, 1, last=True))
            transpose_sums(GROUPS - 1, 1)

        fork(pe, flag, fast, gen["tensor"], force_general)

    def scalar(act):
        v["settled"](act)
        A = nc.scalar

        act_turn = sem("act_turn")

        def copy_counts(s, q, k, g, off, off_next):
            x = (k + q) % 2
            if q == 0:
                act.wait_ge(prepared, g + 1)
            act.wait_ge(cnt_mm, s + 1)
            act.sem_inc(act_turn, 1)
            A.activation(counts[k][:].rearrange("p (b a) d -> p b a d", b=2)[:, :, :, bass.ds(off, W0)],
                         ps_cnt[x][:, :, 0:AB * W0].rearrange("p b (a d) -> p b a d", d=W0),
                         ACT.Copy).then_inc(cnt_copy, 1)
            if q < GQ - 1:
                act.wait_ge(cnt_copy, s + 1)
                act.sem_inc(act_turn, 1)
                A.activation(carry[1 - x][:].unsqueeze(2), counts[k][:, :, bass.ds(off_next, 1)],
                             ACT.Copy).then_inc(carried, 1)

        def activate(s, q, k, first):
            x = (k + q) % 2
            act.wait_ge(pre_add, s + 1)
            if not first:
                act.wait_ge(sum_mm, s - 1)
            A.activation(h[x][:, :, 0:D], pre[x][:].rearrange("p (t n) -> p t n", n=D), ACT.Silu).then_inc(silu, 1)

        def copy_sums(g, k, first):
            act.wait_ge(sum_mm, (g + 1) * GQ)
            if not first:
                act.wait_ge(sum_tr, g + 1)
            A.activation(sumS[:, 0:SW], ps_sum[k][:, 0:SW], ACT.Copy).then_inc(sum_copy, 1)

        def group(half, k, first=False, last=False):
            g = 2 * half + k
            off = [0] + [act.value_load(offs[0:1, bass.ds(g * GQ + q, 1)], min_val=0, max_val=LASTQ)
                         for q in range(1, GQ)]
            for q in range(GQ):
                s = g * GQ + q
                activate(s, q, k, first and q < 2)
                copy_counts(s, q, k, g, off[q], off[q + 1] if q < GQ - 1 else None)
                if q == 1 and not first:
                    copy_sums(g - 1, 1 - k, False)

        def fast():
            act.wait_ge(h_ones, 2)
            loop(act, lambda: group(0, 0, first=True), group, lambda: group(GROUPS // 2 - 1, 1, last=True))
            copy_sums(GROUPS - 1, 1, False)

        fork(act, flag, fast, gen["scalar"], force_general)

    return dict(sync=sync, tensor=tensor, scalar=scalar, gpsimd=gpsimd, vector=vector)


def fork(eng, flag, fast, general, force_general):
    bad = eng.value_load(flag[0:1, 0:1], min_val=0, max_val=1)
    if force_general is None:
        fast()
        return
    with eng.If(bad == (2 if force_general else 0)):
        fast()
    with eng.Else():
        general(eng)


def general_path(nc, ctx, sem, sb, v, layer, e_buf, ps_a, ps_b):
    ident, wc, acc_d = v["ident"], v["wc"], v["acc_d"]
    L = f"{layer}"
    src_c, dst_c = sb("g_src" + L, [P, 1], I32), sb("g_dst" + L, [P, 1], I32)
    dst_r = sb("g_dst_r" + L, [P, P], I32)
    same = sb("g_same" + L, [P, P])
    before = sb("g_before" + L, [P, P])
    tmp = sb("g_tmp" + L, [P, P])
    dup = sb("g_dup" + L, [P, 1])
    row_to = sb("g_row_to" + L, [P, 1], I32)
    dst_f = sb("g_dst_f" + L, [P, 1])
    rows = sb("g_rows" + L, [P, D])
    q_rows = sb("g_q_rows" + L, [P, 3 * D], BF16)
    old = sb("g_old" + L, [P, SWP])
    new = sb("g_new" + L, [P, SWP])
    hm = sb("g_h" + L, [P, SWP])
    back = sb("g_back" + L, [P, SWP])
    ld = {n: sem(f"g_ld_{n}" + L) for n in ("e", "src", "dst", "dsts")}
    ga = {n: sem(f"g_ga_{n}" + L) for n in ("rows", "q", "old")}
    zr, pm, vm, sm, sc, mk, bk, bt, bc = (sem(f"g_{n}" + L) for n in (
        "zr", "pm", "vm", "sm", "sc", "mk", "bk", "bt", "bc"))
    turn, done = sem("g_turn" + L), sem("g_done" + L)
    DVE_STEPS = 7

    def sync(sp):
        sp.wait_ge(mk, 1)
        for b in range(NW // P):
            sp.dma_start(acc_d[b * P:(b + 1) * P, :], new[:]).then_inc(zr, 16)
        if layer == 1:
            sp.dma_start(v["x1_d"].rearrange("(j p) n -> p j n", p=P), v["x1"][:]).then_inc(zr, 16)
        sp.wait_ge(zr, 16 * (NW // P + layer))
        with sp.Fori(0, TILES) as t:
            sp.wait_ge(done, t + 1)
            if layer == 0:
                sp.dma_start(e_buf[:, 0:P], v["eT"][:, bass.ds(t * P, P)]).then_inc(ld["e"], 16)
            with nc.allow_non_contiguous_dma(reason="one index for each partition"):
                sp.dma_start(src_c[:], v["src_row"][bass.ds(t * P, P)].rearrange("(p a) -> p a", a=1)).then_inc(ld["src"], 16)
                sp.dma_start(dst_c[:], v["dst_row"][bass.ds(t * P, P)].rearrange("(p a) -> p a", a=1)).then_inc(ld["dst"], 16)
            sp.dma_start(dst_r[:], v["dst_row"][bass.ds(t * P, P)].partition_broadcast(P)).then_inc(ld["dsts"], 16)
        sp.wait_ge(done, TILES + 1)
        with sp.Fori(0, NB) as b:
            sp.wait_ge(bc, b + 1)
            sp.dma_start(back[:], acc_d[bass.ds(b * P, P), :]).then_inc(bk, 16)

    def gpsimd(pool):
        pool.memset(new[:], 0.0)
        pool.memset(hm[:], 1.0)
        pool.memset(before[:], 0.0).then_inc(mk, 1)
        pool.wait_ge(mk, 1)
        pool.affine_select(out=before[:], in_=before[:], compare_op=ALU.is_ge, fill=1.0, base=0,
                           pattern=[[1, P]], channel_multiplier=-1).then_inc(mk, 1)
        table = v["P_d"] if layer == 0 else v["x1_d"]
        at = lambda c: bass.IndirectOffsetOnAxis(ap=c, axis=0)
        pool.wait_ge(zr, 16 * (NW // P + layer))
        pool.sem_inc(done, 1)
        with pool.Fori(0, TILES) as t:
            pool.wait_ge(ld["src"], 16 * (t + 1))
            pool.wait_ge(ld["dst"], 16 * (t + 1))
            pool.sem_inc(turn, 1)
            if layer == 0:
                pool.indirect_dma_start(rows[:], None, table, at(src_c[:, 0:1])).then_inc(ga["rows"], 16)
                pool.indirect_dma_start(q_rows[:], None, v["Q_d"], at(dst_c[:, 0:1])).then_inc(ga["q"], 16)
            else:
                pool.indirect_dma_start(hm[:, 0:D], None, table, at(src_c[:, 0:1])).then_inc(ga["rows"], 16)
            pool.indirect_dma_start(old[:], None, acc_d, at(dst_c[:, 0:1])).then_inc(ga["old"], 16)
            pool.wait_ge(vm, DVE_STEPS * (t + 1))
            pool.sem_inc(turn, 1)
            pool.indirect_dma_start(acc_d, at(row_to[:, 0:1]), new[:], None,
                                    bounds_check=NW - 1, oob_is_err=False).then_inc(sc, 16)
            pool.wait_ge(sc, 16 * (t + 1))
            pool.sem_inc(done, 1)

    def vector(dve):
        V = nc.vector

        dve.wait_ge(mk, 2)
        with dve.Fori(0, TILES) as t:
            k = [0]

            def link(ins):
                k[0] += 1
                ins.then_inc(vm, 1)
                dve.wait_ge(vm, DVE_STEPS * t + k[0])
            dve.wait_ge(ld["dst"], 16 * (t + 1))
            dve.wait_ge(ld["dsts"], 16 * (t + 1))
            dve.wait_ge(done, t + 1)
            link(V.tensor_copy(dst_f[:], dst_c[:]))
            link(V.tensor_scalar(same[:], dst_r[:], dst_f[:, 0:1], None, ALU.is_equal))
            link(V.tensor_tensor(tmp[:], same[:], before[:], ALU.mult))
            link(V.reduce_sum(dup[:], tmp[:], AX.X))
            link(V.tensor_scalar(dup[:], dup[:], 1.0, float(SKIP), ALU.min, ALU.mult))
            link(V.tensor_tensor(row_to[:], dup[:], dst_f[:], ALU.add))
            dve.wait_ge(ga["old"], 16 * (t + 1))
            if layer == 0:
                dve.wait_ge(ga["rows"], 16 * (t + 1))
                dve.wait_ge(ga["q"], 16 * (t + 1))
                dve.wait_ge(pm, 2 * t + 1)
                V.tensor_tensor(tmp[:], ps_a[:, 0:D], rows[:], ALU.add).then_inc(sm, 1)
                for part in range(3):
                    dve.wait_ge(sm, 4 * t + part + 1)
                    V.tensor_tensor(tmp[:], tmp[:], q_rows[:, part * D:(part + 1) * D], ALU.add).then_inc(sm, 1)
                dve.wait_ge(pm, 2 * t + 2)
            else:
                dve.wait_ge(pm, t + 1)
            V.tensor_tensor(new[:, 0:SW], ps_b[:, 0:SW], old[:, 0:SW], ALU.add).then_inc(vm, 1)

    def scalar(act):
        act.sem_inc(bc, 1)
        if layer == 0:
            with act.Fori(0, TILES) as t:
                act.wait_ge(sm, 4 * t + 4)
                nc.scalar.activation(hm[:, 0:D], tmp[:], ACT.Silu).then_inc(bt, 1)
        with act.Fori(0, NB) as b:
            act.wait_ge(pm, (2 - layer) * TILES + b + 1)
            last = nc.scalar.activation(v["sumT"][:, bass.ds(b * P, P)], ps_a[:, 0:P], ACT.Copy)
            if layer == 0:
                last = nc.scalar.activation(v["deg"][0:1, bass.ds(b * P, P)], ps_a[0:1, P:2 * P], ACT.Copy)
            last.then_inc(bc, 1)

    def tensor(pe):
        T = nc.tensor
        with pe.Fori(0, TILES) as t:
            if layer == 0:
                pe.wait_ge(ld["e"], 16 * (t + 1))
                T.matmul(ps_a[:, 0:D], e_buf[:, 0:P], wc[:], start=True, stop=True).then_inc(pm, 1)
                pe.wait_ge(bt, t + 1)
            else:
                pe.wait_ge(ga["rows"], 16 * (t + 1))
            pe.wait_ge(vm, DVE_STEPS * t + DVE_STEPS - 1)
            T.matmul(ps_b[:, 0:SW], same[:], hm[:, 0:SW], start=True, stop=True).then_inc(pm, 1)
        with pe.Fori(0, NB) as b:
            pe.wait_ge(bk, 16 * (b + 1))
            T.matmul(ps_a[:, 0:P], back[:, 0:D], ident[:], is_transpose=True, start=True, stop=True)
            T.matmul(ps_a[0:1, P:2 * P], back[:, D:SW], ident[:], start=True, stop=True).then_inc(pm, 1)
            pe.wait_ge(bc, b + 2)

    return dict(sync=sync, gpsimd=gpsimd, vector=vector, scalar=scalar, tensor=tensor, bc=bc)


def build_nodes(nc, ctx, sem, sb, v):
    x1 = sb("x1", [P, NB, D])
    x1T = sb("x1T", [P, NP_])
    x1h = sb("x1h", [P, NB, 2, D], F16)
    A_c0, a_in0 = sb("A_c0", [P, NB * P], BF16), sem("a_in0")
    w1, w2 = sb("l1_w1", [P, 2, D]), sb("l1_w2", [P, D])
    b1, b2bc = sb("l1_b1", [P, 1]), sb("l1_b2", [P, D])
    l1_in, rdeg_in = sem("l1_in"), sem("rdeg_in")
    v = dict(v, A_c0=A_c0, a_in0=a_in0, x1=x1, x1T=x1T, x1h=x1h, w1=w1, w2=w2, b1_sb=b1, b2bc=b2bc, l1_in=l1_in, rdeg_in=rdeg_in)
    run_parts(nc, (update_0, sums_1, update_1), ("u0_", "", ""), sem, v)


def blocks(c):
    return slice(c * CH, (c + 1) * CH)


def load_chunk(ap, c):
    return ap[c * CN:(c + 1) * CN, :].rearrange("(j p) n -> p j n", p=P)


def row_stats(V, link, z, st, mv, c):
    for j in range(c * CH, (c + 1) * CH):
        last = V.bn_stats(st[:, j % CH, :], z[:, j, :])
    link(last)
    for j in range(c * CH, (c + 1) * CH):
        last = V.bn_aggr(mv[:, j, :], st[:, j % CH, :])
    return last


def root(nc, sd, mv, eps_col, c):
    return nc.scalar.activation(sd[:, blocks(c)], mv[:, blocks(c), 1], ACT.Sqrt, bias=eps_col[:, 0:1])


def scale_shift(V, link, sd, mv, rs, shift, c):
    link(V.reciprocal(rs[:, blocks(c)], sd[:, blocks(c)]))
    return V.scalar_tensor_tensor(shift[:, blocks(c)], mv[:, blocks(c), 0], -1.0, rs[:, blocks(c)], ALU.mult, ALU.mult)


def update_0(nc, ctx, sem, sb, v):
    sumT, deg, ident = v["sumT"], v["deg"], v["ident"]
    x1, x1T, x1h = v["x1"], v["x1T"], v["x1h"]
    u1a, wagg, bagg, u2, ub1, ub2bc, gbc, bbc = (v[n] for n in ("u1a", "wagg", "bagg", "u2", "ub1_sb", "ub2bc", "gbc", "bbc"))
    R, RB = 3, 4
    xT_c = [sb(f"xT_c{i}", [P, CN]) for i in range(2)]
    x_c = [sb(f"x_c{i}", [P, CH, D]) for i in range(R)]
    hT_c = [sb(f"hT_c{i}", [P, 2, HN]) for i in range(2)]
    xbeta = [sb(f"xbeta{i}", [P, CH, D]) for i in range(RB)]
    z = x1
    st = sb("st", [P, CH, 6])
    mv = [sb(f"mv{i}", [P, NB, 2]) for i in range(2)]
    sd = [sb(f"sd{i}", [P, NB]) for i in range(2)]
    rs = [sb(f"rs{i}", [P, NB]) for i in range(2)]
    shift = sb("shift", [P, NB])
    eps_col = v["eps_col"]
    dg = sb("dg", [P, NB])
    ps_h, ps_y, ps_t = ([ctx.enter_context(nc.psum_tensor(f"u0_{n}{i}", [P, 2, 512], F32)) for i in range(m)]
                        for n, m in (("h", 2), ("y", 1), ("t", 1)))
    ps_y, ps_t = ps_y[0], ps_t[0]
    x_in = [sem(f"u0_x_in{i}") for i in range(R)]
    xT_in = [sem(f"u0_xT_in{i}") for i in range(2)]
    h_mm, h_act, y_mm, z_add, x_ready, norm1, scaled, added = (
        sem(f"u0_{n}") for n in ("h_mm", "h_act", "y_mm", "z_add", "x_ready", "norm1", "scaled", "added"))
    var_ok, sd_ok = ([sem(f"u0_{n}{i}") for i in range(2)] for n in ("var_ok", "sd_ok"))
    stat1, x_norm, x_hi, x_lo, t_mm, t_cp, dv, dg_io, dg_ready = (
        sem(f"u0_{n}") for n in ("stat1", "x_norm", "x_hi", "x_lo", "t_mm", "t_cp", "dv", "dg_io", "dg_ready"))

    def sync(sp):
        for c in range(CHUNKS):
            if c >= 2:
                sp.wait_ge(h_mm, c - 1)
            sp.dma_start(xT_c[c % 2][:], v["xT"][:, c * CN:(c + 1) * CN]).then_inc(xT_in[c % 2], 16)
            if c >= R:
                sp.wait_ge(z_add, c - R + 1)
                sp.wait_ge(x_ready, c - R + 1)
            sp.dma_start(x_c[c % R][:], load_chunk(v["x_nm"], c)).then_inc(x_in[c % R], 16)
            if c == 2:
                sp.dma_start(v["deg_d"].rearrange("(a n) -> a n", a=1), deg[0:1, 0:NP_]).then_inc(dg_io, 16)
                sp.wait_ge(dg_io, 16)
                sp.dma_start(dg[:], v["deg_d"].rearrange("(p j) -> p j", j=NB)).then_inc(dg_io, 16)
                sp.dma_start(v["w1"][:], v["W1"].rearrange("(c k) n -> k c n", c=2)).then_inc(v["l1_in"], 16)
                sp.dma_start(v["w2"][:], v["W2"]).then_inc(v["l1_in"], 16)
                with nc.allow_non_contiguous_dma(reason="one word for each partition"):
                    sp.dma_start(v["b1_sb"][:], v["b1"].rearrange("(n a) -> n a", a=1)).then_inc(v["l1_in"], 16)
                sp.dma_start(v["b2bc"][:], v["b2"].partition_broadcast(P)).then_inc(v["l1_in"], 16)
        if v["force_general"] is not True:
            with sp.If(sp.value_load(v["flag"][0:1, 0:1], min_val=0, max_val=1) == 0):
                sp.dma_start(v["A_c0"][:], v["A_d"][0]).then_inc(v["a_in0"], 16)
        sp.wait_ge(dg_ready, 1)
        sp.dma_start(v["rdeg_d"].rearrange("(p j) -> p j", j=NB), dg[:]).then_inc(dg_io, 16)
        sp.wait_ge(dg_io, 48)

    def transpose(pe, c):
        T = nc.tensor
        pe.wait_ge(x_norm, c + 1)
        if c >= 1:
            pe.wait_ge(t_cp, c)
        for j in range(CH):
            last = T.matmul(ps_t[:, j // 4, (j % 4) * D:(j % 4 + 1) * D], x1[:, c * CH + j, :], ident[:],
                            is_transpose=True, start=True, stop=True)
        last.then_inc(t_mm, 1)

    def tensor(pe):
        T = nc.tensor

        def hidden(c):
            if c >= 2:
                pe.wait_ge(h_act, c - 1)
            cols = [slice(c * CN + i * HN, c * CN + (i + 1) * HN) for i in range(2)]
            for i in range(2):
                T.matmul(ps_h[c % 2][:, i, 0:HN], wagg[:], sumT[:, cols[i]], start=True, stop=False)
                T.matmul(ps_h[c % 2][:, i, 0:HN], bagg[:], deg[0:1, cols[i]], start=False, stop=False)
            pe.wait_ge(xT_in[c % 2], 16 * (c // 2 + 1))
            for i in range(2):
                last = T.matmul(ps_h[c % 2][:, i, 0:HN], u1a[:], xT_c[c % 2][:, i * HN:(i + 1) * HN], start=False, stop=True)
            last.then_inc(h_mm, 1)

        def output(c):
            pe.wait_ge(h_act, c + 1)
            if c >= 1:
                pe.wait_ge(z_add, c)
            for j in range(CH):
                last = T.matmul(ps_y[:, j // 4, (j % 4) * D:(j % 4 + 1) * D],
                                hT_c[c % 2][:].rearrange("p i n -> p (i n)")[:, j * P:(j + 1) * P], u2[:],
                                start=True, stop=True)
            last.then_inc(y_mm, 1)

        hidden(0)
        for i in range(CHUNKS):
            if 1 <= i < CHUNKS - 1:
                hidden(i + 1)
            output(i)
            if i == 0:
                hidden(1)
            if i >= 4:
                transpose(pe, i - 4)

    def scalar(act):
        A = nc.scalar
        for i in range(CHUNKS + 4):
            if i < CHUNKS:
                act.wait_ge(h_mm, i + 1)
                if i >= 2:
                    act.wait_ge(y_mm, i - 1)
                A.activation(hT_c[i % 2][:], ps_h[i % 2][:, :, 0:HN], ACT.Silu, bias=ub1[:, 0:1]).then_inc(h_act, 1)
            if 1 <= i <= CHUNKS:
                act.wait_ge(var_ok[0], i)
                root(nc, sd[0], mv[0], eps_col, i - 1).then_inc(sd_ok[0], 1)
            if 3 <= i < CHUNKS + 3:
                act.wait_ge(var_ok[1], i - 2)
                root(nc, sd[1], mv[1], eps_col, i - 3).then_inc(sd_ok[1], 1)
            if 1 <= i <= CHUNKS:
                c = i - 1
                act.wait_ge(stat1, c + 1)
                for j in range(c * CH, (c + 1) * CH):
                    last = A.activation(z[:, j, :], z[:, j, :], ACT.Identity, scale=rs[0][:, j:j + 1], bias=shift[:, j:j + 1])
                last.then_inc(norm1, 1)
            if i >= 4:
                c = i - 4
                act.wait_ge(x_norm, c + 1)
                A.activation(x1h[:, blocks(c), 0, :], x1[:, blocks(c), :], ACT.Copy).then_inc(x_hi, 1)
                act.wait_ge(t_mm, c + 1)
                A.activation(x1T[:, c * CN:c * CN + 4 * P], ps_t[:, 0, :], ACT.Copy)
                A.activation(x1T[:, c * CN + 4 * P:(c + 1) * CN], ps_t[:, 1, 0:3 * P], ACT.Copy).then_inc(t_cp, 1)

    def gpsimd(pool):
        G = nc.gpsimd

        def bc(t):
            return t[:].unsqueeze(1).broadcast_to([P, CH, D])

        for i in range(CHUNKS + 4):
            if i < CHUNKS:
                pool.wait_ge(x_in[i % R], 16 * (i // R + 1))
                if i >= RB:
                    pool.wait_ge(added, i - RB + 1)
                G.tensor_tensor(xbeta[i % RB][:], x_c[i % R][:], bc(bbc), ALU.add)
                G.tensor_tensor(x_c[i % R][:], x_c[i % R][:], bc(ub2bc), ALU.add).then_inc(x_ready, 1)
            if 1 <= i <= CHUNKS:
                c = i - 1
                pool.wait_ge(norm1, c + 1)
                G.tensor_tensor(z[:, blocks(c), :], z[:, blocks(c), :], bc(gbc), ALU.mult).then_inc(scaled, 1)
            if i >= 4:
                c = i - 4
                pool.wait_ge(x_hi, c + 1)
                G.tensor_tensor(x1h[:, blocks(c), 1, :], x1[:, blocks(c), :], x1h[:, blocks(c), 0, :], ALU.subtract).then_inc(x_lo, 1)

    def vector(dve):
        V = nc.vector
        n = [0]

        def link(ins):
            n[0] += 1
            ins.then_inc(dv, 1)
            dve.wait_ge(dv, n[0])

        for i in range(CHUNKS + 3):
            if 1 <= i <= CHUNKS:
                dve.wait_ge(sd_ok[0], i)
                scale_shift(V, link, sd[0], mv[0], rs[0], shift, i - 1).then_inc(stat1, 1)
            if i < CHUNKS:
                dve.wait_ge(x_ready, i + 1)
                dve.wait_ge(y_mm, i + 1)
                V.tensor_tensor(z[:, i * CH:i * CH + 4, :], ps_y[:, 0, :].rearrange("p (j n) -> p j n", n=D),
                                x_c[i % R][:, 0:4, :], ALU.add)
                V.tensor_tensor(z[:, i * CH + 4:(i + 1) * CH, :], ps_y[:, 1, 0:3 * D].rearrange("p (j n) -> p j n", n=D),
                                x_c[i % R][:, 4:CH, :], ALU.add).then_inc(z_add, 1)
                dve.wait_ge(z_add, i + 1)
                row_stats(V, link, z, st, mv[0], i).then_inc(var_ok[0], 1)
            if 2 <= i < CHUNKS + 2:
                c = i - 2
                dve.wait_ge(scaled, c + 1)
                V.tensor_tensor(z[:, blocks(c), :], z[:, blocks(c), :], xbeta[c % RB][:], ALU.add).then_inc(added, 1)
                dve.wait_ge(added, c + 1)
                if i < CHUNKS:
                    dve.wait_ge(var_ok[0], i + 1)
                row_stats(V, link, z, st, mv[1], c).then_inc(var_ok[1], 1)
            if i == 2:
                dve.wait_ge(dg_io, 32)
                link(V.tensor_scalar(dg[:], dg[:], 1.0, None, ALU.max))
                V.reciprocal(dg[:], dg[:]).then_inc(dg_ready, 1)
            if i >= 3:
                c = i - 3
                dve.wait_ge(sd_ok[1], c + 1)
                link(V.reciprocal(rs[1][:, blocks(c)], sd[1][:, blocks(c)]))
                for j in range(c * CH, (c + 1) * CH):
                    last = V.tensor_scalar(x1[:, j, :], z[:, j, :], mv[1][:, j, 0:1], rs[1][:, j:j + 1], ALU.subtract, ALU.mult)
                last.then_inc(x_norm, 1)

    return dict(sync=sync, tensor=tensor, scalar=scalar, gpsimd=gpsimd, vector=vector,
                transpose=transpose, x_norm=x_norm, x_lo=x_lo, t_cp=t_cp, h_mm=h_mm, z_add=z_add, dg_io=dg_io)


def sums_1(nc, ctx, sem, sb, v):
    RING = 4
    A_c = [v["A_c0"]] + [sb(f"A_c{r}", [P, NB * P], BF16) for r in range(1, RING)]
    sumT, gbase, x1h = v["sumT"], v["gbase"], v["x1h"]
    ps = [ctx.enter_context(nc.psum_tensor(f"ps_n{i}", [P, 512], F32)) for i in range(RING)]
    a_in = [v["a_in0"]] + [sem(f"a_in{r}") for r in range(1, RING)]
    agg_mm, agg_add = sem("s1_mm"), sem("s1_add")
    gen = general_path(nc, ctx, sem, sb, v, 1, None, ps[0], ps[1])

    def settled(eng):
        for done in (v["x_norm"], v["x_lo"], v["t_cp"]):
            eng.wait_ge(done, CHUNKS)
        eng.wait_ge(v["dg_io"], 48)

    def load_rdeg(sp):
        sp.wait_ge(v["h_mm"], CHUNKS)
        sp.dma_start(v["deg"][:, 0:NP_], v["rdeg_d"].partition_broadcast(P)).then_inc(v["rdeg_in"], 16)

    def general(name):
        def program(eng):
            settled(eng)
            if name == "sync":
                load_rdeg(eng)
            gen[name](eng)
        return program

    def sync(sp):
        def fast():
            for r in range(1, RING):
                if r == 1:
                    sp.wait_ge(v["z_add"], CHUNKS)
                if r == 3:
                    sp.wait_ge(v["x_norm"], CHUNKS)
                sp.dma_start(A_c[r][:], v["A_d"][r]).then_inc(a_in[r], 16)
            load_rdeg(sp)
            with sp.Fori(0, GROUPS // RING - 1) as i:
                for r in range(RING):
                    g = RING * i + r
                    sp.wait_ge(agg_mm, g + 1)
                    sp.dma_start(A_c[r][:], v["A_d"][bass.ds(g + RING, 1), :, :].rearrange("a p c -> (a p) c")).then_inc(a_in[r], 16)
        fork(sp, v["flag"], fast, general("sync"), v["force_general"])

    def tensor(pe):
        def group(i, r, first=False):
            pe.wait_ge(a_in[r], 16 * (i + 1))
            if not first:
                pe.wait_ge(agg_add, RING * i + 1)
            for a in range(NB):
                if first and r == 0 and a % CH == 0:
                    if 3 <= a // CH + 1 < CHUNKS:
                        v["transpose"](pe, a // CH + 1)
                    pe.wait_ge(v["x_lo"], a // CH + 1)
                for part in range(2):
                    last = nc.tensor.matmul(ps[r][:, 0:GW], x1h[:, a, part, :], A_c[r][:, a * P:a * P + GW],
                                            start=(a == 0 and part == 0), stop=(a == NB - 1 and part == 1))
            last.then_inc(agg_mm, 1)

        def fast():
            for r in range(RING):
                group(0, r, first=True)
            with pe.Fori(1, GROUPS // RING) as i:
                for r in range(RING):
                    group(i, r)
            pe.wait_ge(agg_add, GROUPS + 1)
        def all_general(pe):
            for c in range(3, CHUNKS):
                v["transpose"](pe, c)
            general("tensor")(pe)

        fork(pe, v["flag"], fast, all_general, v["force_general"])

    def vector(dve):
        def fast():
            dve.wait_ge(v["h_mm"], CHUNKS)
            nc.vector.memset(sumT[:], 0.0).then_inc(agg_add, 1)
            with dve.Fori(0, GROUPS // RING) as i:
                for r in range(RING):
                    g = RING * i + r
                    base = dve.value_load(gbase[0:1, bass.ds(g, 1)], min_val=0, max_val=NP_ - 1)
                    dve.wait_ge(agg_mm, g + 1)
                    dve.wait_ge(agg_add, g + 1)
                    nc.vector.tensor_tensor(sumT[:, bass.ds(base, GW)], ps[r][:, 0:GW], sumT[:, bass.ds(base, GW)],
                                            ALU.add).then_inc(agg_add, 1)
        fork(dve, v["flag"], fast, general("vector"), v["force_general"])

    def scalar(act):
        fork(act, v["flag"], lambda: act.nop(), general("scalar"), v["force_general"])

    def gpsimd(pool):
        def all_sums(eng):
            general("gpsimd")(eng)
            eng.wait_ge(gen["bc"], NB + 1)
        fork(pool, v["flag"], lambda: pool.wait_ge(agg_add, GROUPS + 1), all_sums, v["force_general"])

    return dict(sync=sync, tensor=tensor, scalar=scalar, gpsimd=gpsimd, vector=vector)


def update_1(nc, ctx, sem, sb, v):
    sumT, rdeg = v["sumT"], v["deg"]
    x1, x1T = v["x1"], v["x1T"]
    w1, w2, b1, b2bc = v["w1"], v["w2"], v["b1_sb"], v["b2bc"]
    hT_c = [sb(f"l1_hT{i}", [P, 2, HN]) for i in range(2)]
    z = sb("l1_z", [P, NB, D])
    st = sb("l1_st", [P, CH, 6])
    mv = sb("l1_mv", [P, NB, 2])
    sd, rs, shift = sb("l1_sd", [P, NB]), sb("l1_rs", [P, NB]), sb("l1_shift", [P, NB])
    ps_h, ps_y = ([ctx.enter_context(nc.psum_tensor(f"u1_{n}{i}", [P, 2, 512], F32)) for i in range(2)] for n in "hy")
    dv, scaled, h_mm, h_act, y_mm, z_add, var_ok, sd_ok, stat, normed, stored = (
        sem(f"u1_{n}") for n in ("dv", "scaled", "h_mm", "h_act", "y_mm", "z_add", "var_ok", "sd_ok", "stat", "normed",
                                 "stored"))

    def sync(sp):
        for c in range(CHUNKS):
            sp.wait_ge(normed, c + 1)
            sp.dma_start(load_chunk(v["out"], c), z[:, blocks(c), :]).then_inc(stored, 16)
        sp.wait_ge(stored, 16 * CHUNKS)

    def gpsimd(pool):
        pool.wait_ge(v["rdeg_in"], 16)
        for c in range(CHUNKS):
            cols = slice(c * CN, (c + 1) * CN)
            nc.gpsimd.tensor_tensor(sumT[:, cols], sumT[:, cols], rdeg[:, cols], ALU.mult).then_inc(scaled, 1)

    def tensor(pe):
        T = nc.tensor
        pe.wait_ge(v["l1_in"], 64)

        def hidden(c, half):
            if half == 0 and c >= 2:
                pe.wait_ge(h_act, c - 1)
            if half == 1:
                pe.wait_ge(scaled, c + 1)
            for i in range(2):
                cols = slice(c * CN + i * HN, c * CN + (i + 1) * HN)
                last = T.matmul(ps_h[c % 2][:, i, 0:HN], w1[:, half, :], (x1T, sumT)[half][:, cols],
                                start=(half == 0), stop=(half == 1))
            if half == 1:
                last.then_inc(h_mm, 1)

        hidden(0, 0)
        hidden(0, 1)
        hidden(1, 0)
        for c in range(CHUNKS):
            if 1 <= c < CHUNKS - 1:
                hidden(c + 1, 0)
                hidden(c + 1, 1)
            pe.wait_ge(h_act, c + 1)
            if c >= 2:
                pe.wait_ge(z_add, c - 1)
            for j in range(CH):
                last = T.matmul(ps_y[c % 2][:, j // 4, (j % 4) * D:(j % 4 + 1) * D],
                                hT_c[c % 2][:].rearrange("p i n -> p (i n)")[:, j * P:(j + 1) * P], w2[:],
                                start=True, stop=True)
            last.then_inc(y_mm, 1)
            if c == 0:
                hidden(1, 1)

    def scalar(act):
        for i in range(CHUNKS + 2):
            if i < CHUNKS:
                act.wait_ge(h_mm, i + 1)
                if i >= 2:
                    act.wait_ge(y_mm, i - 1)
                nc.scalar.activation(hT_c[i % 2][:], ps_h[i % 2][:, :, 0:HN], ACT.Relu, bias=b1[:, 0:1]).then_inc(h_act, 1)
            if i >= 2:
                c = i - 2
                act.wait_ge(stat, c + 1)
                for j in range(c * CH, (c + 1) * CH):
                    last = nc.scalar.activation(z[:, j, :], z[:, j, :], ACT.Identity, scale=rs[:, j:j + 1], bias=shift[:, j:j + 1])
                last.then_inc(normed, 1)
            if 1 <= i <= CHUNKS:
                act.wait_ge(var_ok, i)
                root(nc, sd, mv, v["eps_col"], i - 1).then_inc(sd_ok, 1)

    def vector(dve):
        V = nc.vector
        n = [0]

        def link(ins):
            n[0] += 1
            ins.then_inc(dv, 1)
            dve.wait_ge(dv, n[0])

        def finish(c):
            dve.wait_ge(sd_ok, c + 1)
            scale_shift(V, link, sd, mv, rs, shift, c).then_inc(stat, 1)

        for c in range(CHUNKS):
            b0 = c * CH
            dve.wait_ge(y_mm, c + 1)
            for i, m in ((0, 4), (1, 3)):
                last = V.tensor_tensor(z[:, b0 + 4 * i:b0 + 4 * i + m, :],
                                       ps_y[c % 2][:, i, 0:m * D].rearrange("p (j n) -> p j n", n=D),
                                       b2bc[:].unsqueeze(1).broadcast_to([P, m, D]), ALU.add)
            last.then_inc(z_add, 1)
            dve.wait_ge(z_add, c + 1)
            link(V.scalar_tensor_tensor(z[:, blocks(c), :], z[:, blocks(c), :], 0.0, x1[:, blocks(c), :], ALU.max, ALU.add))
            row_stats(V, link, z, st, mv, c).then_inc(var_ok, 1)
            if c >= 1:
                finish(c - 1)
        finish(CHUNKS - 1)

    return dict(sync=sync, tensor=tensor, scalar=scalar, gpsimd=gpsimd, vector=vector)


def kernel(x, src, dst, edge_attr_128, L0_gnn_msg_W1, L0_gnn_msg_b1, L0_gnn_msg_W2, L0_gnn_msg_b2, L0_gnn_upd_W1,
           L0_gnn_upd_b1, L0_gnn_upd_W2, L0_gnn_upd_b2, L0_gnn_ln_gamma, L0_gnn_ln_beta, L1_gnn_W1, L1_gnn_b1,
           L1_gnn_W2, L1_gnn_b2):
    import concourse.bacc as _bacc
    from concourse.bass_utils import run_bass_kernel_spmd as _run

    x, src, dst, e = (np.asarray(a) for a in (x, src, dst, edge_attr_128))
    pad = EP - N_EDGES
    x_nm = np.zeros((NP_, D), x.dtype)
    x_nm[:N_NODES] = x
    eT = np.zeros((D, EP), e.dtype)
    eT[:, :N_EDGES] = e.T
    src_row = np.zeros(EP, src.dtype)
    src_row[:N_EDGES] = src
    dst_row = np.full(EP + 1, NP_, dst.dtype)
    dst_row[:N_EDGES] = dst
    dst_row[N_EDGES:EP] = N_NODES + np.arange(pad) // SPREAD
    arrays = {
        "x_nm": x_nm, "xT": x_nm.T, "eT": eT,
        "src_pt": src_row.reshape(TILES, P).T, "dst_pt": dst_row[:EP].reshape(TILES, P).T,
        "src_row": src_row, "dst_row": dst_row, "dst_first": dst_row[::P], "dst_last": dst_row[P - 1:EP:P],
        "mW1": L0_gnn_msg_W1, "mb1": L0_gnn_msg_b1, "mW2": L0_gnn_msg_W2, "mb2": L0_gnn_msg_b2,
        "uW1": L0_gnn_upd_W1, "ub1": L0_gnn_upd_b1, "uW2": L0_gnn_upd_W2, "ub2": L0_gnn_upd_b2,
        "gamma": L0_gnn_ln_gamma, "beta": L0_gnn_ln_beta,
        "W1": L1_gnn_W1, "b1": L1_gnn_b1, "W2": L1_gnn_W2, "b2": L1_gnn_b2,
    }
    arrays = {k: np.ascontiguousarray(np.asarray(a)) for k, a in arrays.items()}
    nc = _bacc.Bacc("TRN2", target_bir_lowering=False, num_devices=1)
    aps = {k: nc.dram_tensor(k, a.shape, mybir.dt.from_np(a.dtype), kind="ExternalInput").ap() for k, a in arrays.items()}
    out = nc.dram_tensor("out", (NP_, D), F32, kind="ExternalOutput").ap()
    bass_gnn_two_layers(nc, out=out, **aps)
    r = _run(nc, [arrays], core_ids=[0])
    return r.results[0]["out"][:N_NODES]
```
